# Optimizing a Trainium2 kernel written in Bass

```python
import numpy as np
import jax
import jax.numpy as jnp

def _softmax(x, axis=-1):
    return jax.nn.softmax(x, axis=axis)

def _gelu(x):
    return jax.nn.gelu(x, approximate=True)

def _silu(x):
    return jax.nn.silu(x)

def _sigmoid(x):
    return jax.nn.sigmoid(x)

def _layernorm(x, axis=-1, eps=1e-05):
    m = jnp.mean(x, axis=axis, keepdims=True)
    v = jnp.var(x, axis=axis, keepdims=True)
    return (x - m) / jnp.sqrt(v + eps)

def _scatter_add(tgt, idx, src, axis=0):
    return tgt.at[idx].add(src)

def _segment_sum(src, seg, n):
    return jax.ops.segment_sum(src, seg, n)
kernel_name = 'mk_adaln_ffn_d2_seqx_r4_f7fab0'

def setup_inputs(seed: int=0):
    np.random.seed(seed)
    _w = jnp.asarray

    def _rec_inputs():
        import jax
        import jax.numpy as jnp
        _rk = jax.random.key(seed)
        x = -0.0003929 + 0.9999 * jax.random.normal(jax.random.fold_in(_rk, 1), (8, 256, 256), jnp.float32)
        _lenS = 256 - jax.random.randint(jax.random.fold_in(_rk, 7), (8,), 0, max(1, 256 // 4) + 1, jnp.int32)
        _lenS2 = 256 - jax.random.randint(jax.random.fold_in(_rk, 8), (8,), 0, max(1, 256 // 4) + 1, jnp.int32)
        itok_B_0_2 = jax.random.randint(jax.random.fold_in(_rk, 11), (8,), 0, 3, jnp.int32)
        itok_B_0_8 = jax.random.randint(jax.random.fold_in(_rk, 12), (8,), 0, 9, jnp.int32)
        return (x, itok_B_0_2, itok_B_0_8)
    x, itok_B_0_2, itok_B_0_8 = _rec_inputs()

    def _L0_cond_setup():
        import jax, jax.numpy as jnp
        import numpy as np
        D_MODEL = 256
        D_FF = 1024
        N_EXPERTS = 5
        BATCH = 8
        SEQ = 512

        def _gated_ffn(x, wi0, wi1, wo):
            g = jax.nn.gelu(x @ wi0, approximate=True)
            l = x @ wi1
            return g * l @ wo
        key = jax.random.key(seed)
        ks = jax.random.split(key, 12)
        s = 0.02
        inp = {'hidden_states': jax.random.normal(ks[0], (BATCH, SEQ, D_MODEL), jnp.float32), 'type_label': jax.random.randint(ks[1], (BATCH,), 0, N_EXPERTS, jnp.int32), 'Wi0': jax.random.normal(ks[2], (N_EXPERTS, D_MODEL, D_FF), jnp.float32) * s, 'Wi1': jax.random.normal(ks[3], (N_EXPERTS, D_MODEL, D_FF), jnp.float32) * s, 'Wo': jax.random.normal(ks[4], (N_EXPERTS, D_FF, D_MODEL), jnp.float32) * s, 'sWi0': jax.random.normal(ks[5], (D_MODEL, D_FF), jnp.float32) * s, 'sWi1': jax.random.normal(ks[6], (D_MODEL, D_FF), jnp.float32) * s, 'sWo': jax.random.normal(ks[7], (D_FF, D_MODEL), jnp.float32) * s, 'g0': jax.random.normal(ks[8], (2 * D_MODEL, D_MODEL), jnp.float32) * s, 'g1': jax.random.normal(ks[9], (D_MODEL, 2), jnp.float32) * s}
        return inp
    _L0_cond_all = _L0_cond_setup()
    _L0_cond_in = {k: v for k, v in _L0_cond_all.items() if k in ('Wi0', 'Wi1', 'Wo', 'sWi0', 'sWi1', 'sWo', 'g0', 'g1')}
    del _L0_cond_all

    def _L0_ffn_setup():
        import jax, jax.numpy as jnp
        import numpy as np
        D_MODEL = 256
        D_FF = 512
        N_EXPERTS = 8
        TOP_K = 2
        CLAMP = 10000.0
        ROUTER_EPS = 1e-08
        LN_EPS = 1e-05

        def _layernorm(x, g, b):
            mu = jnp.mean(x, axis=-1, keepdims=True)
            var = jnp.mean(jnp.square(x - mu), axis=-1, keepdims=True)
            return (x - mu) * jax.lax.rsqrt(var + LN_EPS) * g + b
        key = jax.random.key(seed)
        k1, k2, k3, k4 = jax.random.split(key, 4)
        B, S = (8, 256)
        x = jax.random.normal(k1, (B, S, D_MODEL), dtype=jnp.float32)
        ln_gamma = jnp.ones((D_MODEL,), jnp.float32)
        ln_beta = jnp.zeros((D_MODEL,), jnp.float32)
        bound = 0.02 * float(np.sqrt(3.0))
        router_w = jax.random.uniform(k2, (N_EXPERTS, D_MODEL), jnp.float32, -bound, bound)
        gate_up_w = jax.random.normal(k3, (N_EXPERTS, 2 * D_FF, D_MODEL), jnp.float32) * (1.0 / np.sqrt(D_MODEL))
        down_w = jax.random.normal(k4, (N_EXPERTS, D_MODEL, D_FF), jnp.float32) * (1.0 / np.sqrt(D_FF))
        return {'x': x, 'ln_gamma': ln_gamma, 'ln_beta': ln_beta, 'router_w': router_w, 'gate_up_w': gate_up_w, 'down_w': down_w}
    _L0_ffn_all = _L0_ffn_setup()
    _L0_ffn_in = {k: v for k, v in _L0_ffn_all.items() if k in ('ln_gamma', 'ln_beta', 'router_w', 'gate_up_w', 'down_w')}
    del _L0_ffn_all

    def _L1_cond_setup():
        import jax, jax.numpy as jnp
        import numpy as np
        LN_EPS = 1e-05
        key = jax.random.key(seed)
        ks = jax.random.split(key, 8)
        B, S, H, A, L = (32, 512, 256, 64, 10)
        return {'hidden_states': jax.random.normal(ks[0], (B, S, H), dtype=jnp.float32), 'language_ids': jax.random.randint(ks[1], (B,), 0, L, dtype=jnp.int64), 'W1': jax.random.normal(ks[2], (L, H, A), dtype=jnp.float32) * (1.0 / np.sqrt(H)), 'b1': jnp.zeros((L, A), dtype=jnp.float32), 'W2': jax.random.normal(ks[3], (L, A, H), dtype=jnp.float32) * (1.0 / np.sqrt(A)), 'b2': jnp.zeros((L, H), dtype=jnp.float32), 'gamma': jnp.ones((L, H), dtype=jnp.float32), 'beta': jnp.zeros((L, H), dtype=jnp.float32)}
    _L1_cond_all = _L1_cond_setup()
    _L1_cond_in = {k: v for k, v in _L1_cond_all.items() if k in ('W1', 'b1', 'W2', 'b2', 'gamma', 'beta')}
    del _L1_cond_all

    def _L1_ffn_setup():
        import jax, jax.numpy as jnp
        import numpy as np
        QP = 127.0
        MIN_RANGE = 1e-06

        def _ste_round(x):
            return x + jax.lax.stop_gradient(jnp.round(x) - x)

        def _quant_per_tensor(x):
            scale = jnp.maximum(jnp.max(jnp.abs(x)), MIN_RANGE) / QP
            return (_ste_round(x / scale), scale)

        def _qlinear(x2d, w, b):
            xq, sx = _quant_per_tensor(x2d)
            wq, sw = _quant_per_tensor(w)
            out = jnp.matmul(xq, wq.T) + b[None, :]
            return out * (sw * sx)
        key = jax.random.key(seed)
        k = jax.random.split(key, 5)
        B, N, D, H = (8, 256, 256, 1024)
        return {'x': jax.random.normal(k[0], (B, N, D), dtype=jnp.float32), 'w1': jax.random.normal(k[1], (H, D), dtype=jnp.float32) * 0.02, 'b1': jax.random.normal(k[2], (H,), dtype=jnp.float32) * 0.02, 'w2': jax.random.normal(k[3], (D, H), dtype=jnp.float32) * 0.02, 'b2': jax.random.normal(k[4], (D,), dtype=jnp.float32) * 0.02}
    _L1_ffn_all = _L1_ffn_setup()
    _L1_ffn_in = {k: v for k, v in _L1_ffn_all.items() if k in ('w1', 'b1', 'w2', 'b2')}
    del _L1_ffn_all
    return {'x': x, 'itok_B_0_2': itok_B_0_2, 'itok_B_0_8': itok_B_0_8, 'L0_cond_Wi0': _L0_cond_in['Wi0'], 'L0_cond_Wi1': _L0_cond_in['Wi1'], 'L0_cond_Wo': _L0_cond_in['Wo'], 'L0_cond_sWi0': _L0_cond_in['sWi0'], 'L0_cond_sWi1': _L0_cond_in['sWi1'], 'L0_cond_sWo': _L0_cond_in['sWo'], 'L0_cond_g0': _L0_cond_in['g0'], 'L0_cond_g1': _L0_cond_in['g1'], 'L0_ffn_ln_gamma': _L0_ffn_in['ln_gamma'], 'L0_ffn_ln_beta': _L0_ffn_in['ln_beta'], 'L0_ffn_router_w': _L0_ffn_in['router_w'], 'L0_ffn_gate_up_w': _L0_ffn_in['gate_up_w'], 'L0_ffn_down_w': _L0_ffn_in['down_w'], 'L1_cond_W1': _L1_cond_in['W1'], 'L1_cond_b1': _L1_cond_in['b1'], 'L1_cond_W2': _L1_cond_in['W2'], 'L1_cond_b2': _L1_cond_in['b2'], 'L1_cond_gamma': _L1_cond_in['gamma'], 'L1_cond_beta': _L1_cond_in['beta'], 'L1_ffn_w1': _L1_ffn_in['w1'], 'L1_ffn_b1': _L1_ffn_in['b1'], 'L1_ffn_w2': _L1_ffn_in['w2'], 'L1_ffn_b2': _L1_ffn_in['b2']}

def reference(x, itok_B_0_2, itok_B_0_8, L0_cond_Wi0, L0_cond_Wi1, L0_cond_Wo, L0_cond_sWi0, L0_cond_sWi1, L0_cond_sWo, L0_cond_g0, L0_cond_g1, L0_ffn_ln_gamma, L0_ffn_ln_beta, L0_ffn_router_w, L0_ffn_gate_up_w, L0_ffn_down_w, L1_cond_W1, L1_cond_b1, L1_cond_W2, L1_cond_b2, L1_cond_gamma, L1_cond_beta, L1_ffn_w1, L1_ffn_b1, L1_ffn_w2, L1_ffn_b2):
    import jax
    import jax.numpy as jnp

    def _L0_cond_ref(hidden_states, type_label, Wi0, Wi1, Wo, sWi0, sWi1, sWo, g0, g1):
        import jax, jax.numpy as jnp
        import numpy as np
        D_MODEL = 256
        D_FF = 1024
        N_EXPERTS = 5
        BATCH = 8
        SEQ = 512

        def _gated_ffn(x, wi0, wi1, wo):
            g = jax.nn.gelu(x @ wi0, approximate=True)
            l = x @ wi1
            return g * l @ wo
        share_out = _gated_ffn(hidden_states, sWi0, sWi1, sWo)
        wi0 = Wi0[type_label]
        wi1 = Wi1[type_label]
        wo = Wo[type_label]
        hg = jax.nn.gelu(jnp.einsum('bsd,bdf->bsf', hidden_states, wi0), approximate=True)
        hl = jnp.einsum('bsd,bdf->bsf', hidden_states, wi1)
        expert_out = jnp.einsum('bsf,bfd->bsd', hg * hl, wo)
        gate_in = jnp.concatenate([expert_out[:, 0], share_out[:, 0]], axis=-1)
        weights = jax.nn.softmax(jax.nn.relu(gate_in @ g0) @ g1, axis=-1)
        w0 = weights[:, 0][:, None, None]
        w1 = weights[:, 1][:, None, None]
        return expert_out * w0 + share_out * w1

    def _L0_ffn_ref(x, ln_gamma, ln_beta, router_w, gate_up_w, down_w):
        import jax, jax.numpy as jnp
        import numpy as np
        D_MODEL = 256
        D_FF = 512
        N_EXPERTS = 8
        TOP_K = 2
        CLAMP = 10000.0
        ROUTER_EPS = 1e-08
        LN_EPS = 1e-05

        def _layernorm(x, g, b):
            mu = jnp.mean(x, axis=-1, keepdims=True)
            var = jnp.mean(jnp.square(x - mu), axis=-1, keepdims=True)
            return (x - mu) * jax.lax.rsqrt(var + LN_EPS) * g + b
        B, S, D = x.shape
        xn = _layernorm(x, ln_gamma, ln_beta)
        xf = xn.reshape(-1, D)
        N = xf.shape[0]
        logits = jnp.clip(xf @ router_w.T, -CLAMP, CLAMP)
        m = jnp.max(logits, axis=-1, keepdims=True)
        e = jnp.exp(logits - m)
        probs = e / (jnp.sum(e, axis=-1, keepdims=True) + ROUTER_EPS)
        probs = jnp.clip(probs, ROUTER_EPS, 1.0)
        topk_p, topk_i = jax.lax.top_k(probs, TOP_K)
        dense_gate = jnp.zeros((N, N_EXPERTS), probs.dtype).at[jnp.arange(N)[:, None], topk_i].add(topk_p)
        out = jnp.zeros_like(xf)
        for eid in range(N_EXPERTS):
            xe = xf * dense_gate[:, eid:eid + 1]
            gu = xe @ gate_up_w[eid].T
            gate, up = jnp.split(gu, 2, axis=-1)
            hidden = jax.nn.silu(gate) * up
            out = out + hidden @ down_w[eid].T
        return x + out.reshape(B, S, D)

    def _L1_cond_ref(hidden_states, language_ids, W1, b1, W2, b2, gamma, beta):
        import jax, jax.numpy as jnp
        import numpy as np
        LN_EPS = 1e-05
        w1 = W1[language_ids]
        w2 = W2[language_ids]
        h = jnp.einsum('bsh,bha->bsa', hidden_states, w1) + b1[language_ids][:, None, :]
        h = jax.nn.relu(h)
        adapted = jnp.einsum('bsa,bah->bsh', h, w2) + b2[language_ids][:, None, :]
        x = hidden_states + adapted
        mean = jnp.mean(x, axis=-1, keepdims=True)
        var = jnp.mean(jnp.square(x - mean), axis=-1, keepdims=True)
        normed = (x - mean) * jax.lax.rsqrt(var + LN_EPS)
        return normed * gamma[language_ids][:, None, :] + beta[language_ids][:, None, :]

    def _L1_ffn_ref(x, w1, b1, w2, b2):
        import jax, jax.numpy as jnp
        import numpy as np
        QP = 127.0
        MIN_RANGE = 1e-06

        def _ste_round(x):
            return x + jax.lax.stop_gradient(jnp.round(x) - x)

        def _quant_per_tensor(x):
            scale = jnp.maximum(jnp.max(jnp.abs(x)), MIN_RANGE) / QP
            return (_ste_round(x / scale), scale)

        def _qlinear(x2d, w, b):
            xq, sx = _quant_per_tensor(x2d)
            wq, sw = _quant_per_tensor(w)
            out = jnp.matmul(xq, wq.T) + b[None, :]
            return out * (sw * sx)
        B, N, D = x.shape
        h = _qlinear(x.reshape(-1, D), w1, b1)
        h = jax.nn.gelu(h, approximate=False)
        o = _qlinear(h, w2, b2)
        return o.reshape(B, N, -1)
    x = x + _L0_ffn_ref(_L0_cond_ref(x, itok_B_0_2, L0_cond_Wi0, L0_cond_Wi1, L0_cond_Wo, L0_cond_sWi0, L0_cond_sWi1, L0_cond_sWo, L0_cond_g0, L0_cond_g1), L0_ffn_ln_gamma, L0_ffn_ln_beta, L0_ffn_router_w, L0_ffn_gate_up_w, L0_ffn_down_w)
    x = x + _L1_ffn_ref(_L1_cond_ref(x, itok_B_0_8, L1_cond_W1, L1_cond_b1, L1_cond_W2, L1_cond_b2, L1_cond_gamma, L1_cond_beta), L1_ffn_w1, L1_ffn_b1, L1_ffn_w2, L1_ffn_b2)
    return x

_drawn_inputs = setup_inputs


def setup_inputs(seed=0):
    import zlib

    import numpy as np

    out = dict(_drawn_inputs(seed))
    spreads = {'L0_ffn_ln_gamma': (1.0, 0.6),
     'L0_ffn_ln_beta': (0.0, 0.8),
     'L1_cond_b1': (0.0, 0.693),
     'L1_cond_b2': (0.0, 0.567),
     'L1_cond_gamma': (1.0, 0.6),
     'L1_cond_beta': (0.0, 0.513)}
    factors = {'L0_cond_g0': 8.0, 'L0_cond_g1': 8.0, 'L1_ffn_b1': 8.0, 'L1_ffn_b2': 8.0}
    for name, (base, spread) in spreads.items():
        noise = np.random.default_rng([zlib.crc32(name.encode()), seed]).standard_normal(out[name].shape)
        drawn = base * np.exp(spread * noise) if base else spread * noise
        out[name] = jnp.asarray(drawn.astype(out[name].dtype))
    for name, factor in factors.items():
        out[name] = (out[name] * factor).astype(out[name].dtype)
    return out
```

```python
from contextlib import ExitStack

import numpy as np

import concourse.bass as bass
from concourse import mybir

P = 128
F32, F16, BF16, I32 = mybir.dt.float32, mybir.dt.float16, mybir.dt.bfloat16, mybir.dt.int32
ALU = mybir.AluOpType
ACT = mybir.ActivationFunctionType
AX = mybir.AxisListType.X

SX, SW = 16.0, 1024.0
SH = 256.0
SN, SE, SHE = 8.0, 256.0, 64.0
MAGIC = 1.5 * 2.0 ** 23


def hold(eng, reg, sem, value, met):
    if isinstance(value, int):
        eng.wait_ge(sem, value)
        return
    eng.reg_mov(reg, value)
    eng.wait_ge(*met)
    eng.wait_ge(sem, reg)


def linker(eng, sem, base=0):
    n = [0]

    def link(ins, reg=None, met=None):
        n[0] += 1
        ins.then_inc(sem, 1)
        if reg is None:
            eng.wait_ge(sem, base + n[0])
        else:
            hold(eng, reg, sem, base + n[0], met)
    link.n = n
    return link


def build(nc, x, xT, itokA, itokC, Wi0, Wi1, Wo, sWi0, sWi1, sWo, g0, g1T, gamma0, beta0, routerT, guT, dnT,
          cW1, cb1T, cW2, cb2, cgamma, cbeta, w1T, b1T, w2T, b2, out, stop=None):
    NB, S, D = x.shape
    TOK = NB * S
    NT = TOK // P
    TB = S // P
    KD = D // P
    NEA, _, F = Wi0.shape
    FC = F // P
    PAIRS = FC // 2
    NP = 2 * PAIRS
    E, _, F2 = guT.shape
    FE = F2 // 2
    KE = FE // P
    NL, _, A = cW1.shape
    TOPK = 2
    NBLK = (TOPK * TOK + E * (P - 1)) // P
    UNR = 3
    assert (D, F, S, FE, NBLK % UNR) == (256, 1024, 256, 512, 0)

    xn_dram = nc.dram_tensor("xn_rows", [TOK, D], F32).ap()
    res_dram = nc.dram_tensor("residual_rows", [TOK, D], F32).ap()
    moe_dram = nc.dram_tensor("moe_rows", [TOPK * TOK + NBLK * P, D], F32).ap()

    with ExitStack() as ctx:
        def sb(name, shape, dt=F32):
            return ctx.enter_context(nc.sbuf_tensor(name, shape, dt))

        def pb(name, shape):
            return ctx.enter_context(nc.psum_tensor(name, shape, F32))

        def sem(name):
            return ctx.enter_context(nc.semaphore(name))

        xb_sb = sb("xb_sb", [P, TB, D])
        xt_area = sb("xt_area", [P, 2 * KD * TOK], F16)
        moe_area = sb("moe_area", [P, 2 * (KD * E * F2 + KE * E * D)], F16)
        ffn_area = sb("ffn_area", [P, 4 * (KD * F * 2 + FC * D) // 1], F16)
        stage = sb("stage", [P, 2, KD * F])
        gelu_g = sb("gelu_g", [P, 2, S])
        hid = sb("hid", [P, 2, S])
        hid_hl = sb("hid_hl", [P, 2, 2, 2, S], F16)
        S_out = sb("S_out", [P, TB, D])
        E_out = sb("E_out", [P, TB, D])
        XN = sb("XN", [P, TB, D])
        xnT = sb("xnT", [P, KD, S])
        gam = sb("gam", [P, D])
        bet = sb("bet", [P, D])
        g0_sb = sb("g0_sb", [P, 2 * KD, D])
        rw_sb = sb("rw_sb", [P, KD, E])
        LG = sb("LG", [P, NT, E])
        ident = sb("ident", [P, P])
        upper = sb("upper", [P, P])
        ones = sb("ones", [P, P])
        iota_row = sb("iota_row", [P, P])
        iota_p = sb("iota_p", [P, 1])
        rev_e = sb("rev_e", [P, E])
        itA = sb("itA", [1, NB], I32)
        itC = sb("itC", [1, NB], I32)
        row = sb("row", [1, 3 * D])
        g1_row, junk_row = row[0:1, 0:2 * D].rearrange("p (j d) -> p j d", j=2), row[0:1, 2 * D:3 * D]
        tiny = sb("tiny", [P, 64])
        gT = tiny[:, 0:4]
        logit2, mx1, dl2, ex2 = tiny[0:1, 4:6], tiny[0:1, 6:7], tiny[0:1, 8:10], tiny[0:1, 10:12]
        sm1, rs1, w2row, ebase = tiny[0:1, 12:13], tiny[0:1, 13:14], tiny[0:1, 14:16], tiny[0:1, 16:18]
        wbc, rstd, vpe = tiny[:, 18:20], tiny[:, 20:22], tiny[:, 22:24]
        mhalf, eps2 = tiny[:, 24:26], tiny[:, 42:44]
        mv = tiny[:, 26:30].rearrange("p (t s) -> p t s", t=2)
        bst = tiny[:, 30:42].rearrange("p (t s) -> p t s", t=2)

        XTh = xt_area[:, 0:KD * TOK].rearrange("p (k n) -> p k n", k=KD)
        XTl = xt_area[:, KD * TOK:].rearrange("p (k n) -> p k n", k=KD)
        ng, nd = KD * E * F2, KE * E * D
        GUh = moe_area[:, 0:ng].rearrange("p (k e f) -> p k e f", k=KD, e=E)
        GUl = moe_area[:, ng:2 * ng].rearrange("p (k e f) -> p k e f", k=KD, e=E)
        DNh = moe_area[:, 2 * ng:2 * ng + nd].rearrange("p (k e d) -> p k e d", k=KE, e=E)
        DNl = moe_area[:, 2 * ng + nd:].rearrange("p (k e d) -> p k e d", k=KE, e=E)
        nw = KD * F

        def ffn_w(s, j):
            v = ffn_area[:, (6 * s + j) * nw:(6 * s + j + 1) * nw]
            return v.rearrange("p (k f) -> p k f", k=KD) if j < 4 else v.rearrange("p (c d) -> p c d", c=FC)

        early = moe_area[:, ng:].bitcast(F32)
        xT_in = early[:, 0:KD * TOK].rearrange("p (u k n) -> p u k n", u=4, k=KD)
        sW_in = early[:, KD * TOK:KD * TOK + 3 * nw].rearrange("p (j v) -> p j v", j=3)

        halves = [pb(f"psum_half{i}", [P, 4, 512]) for i in range(2)]
        pG = [halves[0][:, i, :] for i in range(2)]
        pL = [halves[0][:, 2 + i, :] for i in range(2)]
        pD = halves[1][:, 0:2, :]
        pM, pR = halves[1][:, 2, :], halves[1][:, 3, :]

        x_in = [sem(f"x_in{u}") for u in range(4)]
        w_in = [sem(f"w_in{u}") for u in range(6)]
        small_in, ids_in = sem("small_in"), sem("ids_in")
        xb_in, gate_in, res_stored = sem("xb_in"), sem("gate_in"), sem("res_stored")
        buf_in = [sem("buf0_in"), sem("buf1_in")]
        conv_hi, conv_lo = sem("conv_hi"), sem("conv_lo")
        up_done, dn_done = sem("up_done"), sem("dn_done")
        gelu_done, h_done, hh_done, hl_done = sem("gelu_done"), sem("h_done"), sem("hh_done"), sem("hl_done")
        ev_done = sem("ev_done")
        gt_done, hg_done, wb_done, xnt_done, log_done = (sem(n) for n in (
            "gt_done", "hg_done", "wb_done", "xnt_done", "log_done"))
        gTc_done, dlt_done, w_done, y_done, bn_done, nrm_done, xnTc_done, lg_done = (sem(n) for n in (
            "gTc_done", "dlt_done", "w_done", "y_done", "bn_done", "nrm_done", "xnTc_done", "lg_done"))
        ex_done, res_done, rstd_done, xn_ready, xn_stored = (sem(n) for n in (
            "ex_done", "res_done", "rstd_done", "xn_ready", "xn_stored"))
        consts, dve_link, pool_link = sem("consts"), sem("dve_link"), sem("pool_link")

        NCONV = 9
        PRO = 10
        SLOT_OF = [0, 0, 1, 2, 3, 4, 5, 6, 7]
        DVE_LINKS, POOL_LINKS = 8 + 2, 2

        def conv_piece(u, i):
            half = FC // 2
            if u < 4:
                j, h = u // 2, u % 2
                src = stage[:, j, :].rearrange("p (k f) -> p k f", k=KD)[:, :, h * 512:h * 512 + 512]
                hi, lo = (ffn_w(1, 2 * j + q)[:, :, h * 512:h * 512 + 512] for q in range(2))
                return src, hi, lo, SW, j, (3 + 3 * i - 2 if j == 0 else 1 + 2 * i)
            if u < 6:
                h = u - 4
                src = stage[:, 0, :].rearrange("p (c d) -> p c d", c=FC)[:, h * half:(h + 1) * half, :]
                hi, lo = (ffn_w(1, 4 + q)[:, h * half:(h + 1) * half, :] for q in range(2))
                return src, hi, lo, SW, 0, 3 * i + 2
            if u < 8:
                h = u - 6
                src = stage[:, 1, :].rearrange("p (k f) -> p k f", k=KD)[:, :, h * 512:h * 512 + 512]
                hi, lo = (w[:, :, bass.ds(i, 1), h * 512:h * 512 + 512] for w in (GUh, GUl))
                return src, hi, lo, SE, 1, 2 * i + 2
            src = stage[:, 0, 0:KE * D].rearrange("p (k d) -> p k d", k=KE)
            hi, lo = (w[:, :, bass.ds(i, 1), :] for w in (DNh, DNl))
            return src, hi, lo, SE, 0, 3 * i + 3

        def early_piece(n):
            order = ["x0", "w0", "w2", "w4", "w1", "w3", "w5", "x1", "x2", "x3"]
            kind, u = order[n][0], int(order[n][1])
            if kind == "x":
                tok = slice(u * 512, u * 512 + 512)
                return xT_in[:, u], XTh[:, :, tok], XTl[:, :, tok], SX, x_in[u]
            j, h = u // 2, u % 2
            if j < 2:
                src = sW_in[:, j, :].rearrange("p (k f) -> p k f", k=KD)[:, :, h * 512:h * 512 + 512]
                hi, lo = (ffn_w(0, 2 * j + q)[:, :, h * 512:h * 512 + 512] for q in range(2))
            else:
                src = sW_in[:, j, :].rearrange("p (c d) -> p c d", c=FC)[:, h * 4:h * 4 + 4, :]
                hi, lo = (ffn_w(0, 4 + q)[:, h * 4:h * 4 + 4, :] for q in range(2))
            return src, hi, lo, SW, w_in[u]

        def flat3(ap):
            return ap.rearrange("p k e f -> p k (e f)") if len(ap.shape) == 4 else ap

        with nc.Block() as blk:
            @blk.sync
            def _(sp):
                sp.dma_start(itA[0:1, :], itokA.rearrange("(a n) -> a n", a=1)).then_inc(ids_in, 16)
                sp.dma_start(itC[0:1, :], itokC.rearrange("(a n) -> a n", a=1)).then_inc(ids_in, 16)
                xT_v = xT.rearrange("(u v) (k p) s -> u p k v s", u=4, p=P)
                for n in range(PRO):
                    kind, u = ["x0", "w0", "w2", "w4", "w1", "w3", "w5", "x1", "x2", "x3"][n]
                    u = int(u)
                    if kind == "x":
                        for k in range(KD):
                            sp.dma_start(xT_in[:, u, k].rearrange("p (v s) -> p v s", v=2),
                                         xT_v[u, :, k]).then_inc(x_in[u], 16)
                    else:
                        j, h = u // 2, u % 2
                        if j < 2:
                            w = (sWi0, sWi1)[j].rearrange("(k p) f -> p k f", p=P)[:, :, h * 512:h * 512 + 512]
                            dst = sW_in[:, j, :].rearrange("p (k f) -> p k f", k=KD)[:, :, h * 512:h * 512 + 512]
                        else:
                            w = sWo.rearrange("(c p) d -> p c d", p=P)[:, h * 4:h * 4 + 4, :]
                            dst = sW_in[:, j, :].rearrange("p (c d) -> p c d", c=FC)[:, h * 4:h * 4 + 4, :]
                        sp.dma_start(dst, w).then_inc(w_in[u], 16)
                sp.dma_start(g0_sb[:, :, :], g0.rearrange("(c p) d -> p c d", p=P)).then_inc(gate_in, 16)
                sp.dma_start(g1_row, g1T.rearrange("(a j) d -> a j d", a=1)).then_inc(gate_in, 16)
                sp.dma_start(rw_sb[:, :, :], routerT.rearrange("(k p) e -> p k e", p=P)).then_inc(gate_in, 16)
                sp.dma_start(gam[:, :], gamma0.partition_broadcast(P)).then_inc(small_in, 16)
                sp.dma_start(bet[:, :], beta0.partition_broadcast(P)).then_inc(small_in, 16)
                sp.wait_ge(ids_in, 32)

                def loads(i):
                    e = sp.value_load(itA[0:1, bass.ds(i, 1)], min_val=0, max_val=NEA - 1)

                    def w_of(w):
                        return w[bass.ds(e, 1), :, :]
                    first = isinstance(i, int)
                    if not first:
                        sp.wait_ge(conv_lo, i * NCONV + PRO - 1)
                    sp.dma_start(stage[:, 1, :].rearrange("p (k f) -> p k f", k=KD),
                                 w_of(Wi1).rearrange("e (k p) f -> p (e k) f", p=P)).then_inc(buf_in[1], 16)
                    if not first:
                        sp.wait_ge(conv_lo, i * NCONV + PRO)
                    sp.dma_start(stage[:, 0, :].rearrange("p (k f) -> p k f", k=KD),
                                 w_of(Wi0).rearrange("e (k p) f -> p (e k) f", p=P)).then_inc(buf_in[0], 16)
                    sp.wait_ge(conv_lo, i * NCONV + PRO + 2)
                    sp.dma_start(stage[:, 0, :].rearrange("p (c d) -> p c d", c=FC),
                                 w_of(Wo).rearrange("e (c p) d -> p (e c) d", p=P)).then_inc(buf_in[0], 16)
                    sp.wait_ge(conv_lo, i * NCONV + PRO + 4)
                    sp.dma_start(stage[:, 1, :].rearrange("p (k f) -> p k f", k=KD),
                                 guT[bass.ds(i, 1), :, :].rearrange("e (k p) f -> p (e k) f", p=P)).then_inc(buf_in[1], 16)
                    sp.wait_ge(conv_lo, i * NCONV + PRO + 6)
                    sp.dma_start(stage[:, 0, 0:KE * D].rearrange("p (k d) -> p k d", k=KE),
                                 dnT[bass.ds(i, 1), :, :].rearrange("e (k p) d -> p (e k) d", p=P)).then_inc(buf_in[0], 16)

                def load_residual(g, first=False):
                    if not first:
                        sp.wait_ge(res_stored, g * 16)
                        sp.wait_ge(xn_stored, g * 16)
                    sp.dma_start(xb_sb[:, :, :], x.rearrange("b (t p) d -> p b t d", p=P)[:, bass.ds(g, 1)]
                                 ).then_inc(xb_in, 16)

                def store_xn(g):
                    sp.wait_ge(res_done, g + 1)
                    sp.dma_start(res_dram.rearrange("(b t p) d -> p b t d", t=TB, p=P)[:, bass.ds(g, 1)],
                                 xb_sb[:, :, :]).then_inc(res_stored, 16)
                    sp.wait_ge(xn_ready, g + 1)
                    sp.dma_start(xn_dram.rearrange("(b t p) d -> p b t d", t=TB, p=P)[:, bass.ds(g, 1)],
                                 XN[:, :, :]).then_inc(xn_stored, 16)
                loads(0)
                load_residual(0, first=True)
                with sp.Fori(1, NB) as i:
                    loads(i)
                    store_xn(i - 1)
                    load_residual(i)
                store_xn(NB - 1)
                sp.wait_ge(xn_stored, 16 * NB)
                sp.wait_ge(res_stored, 16 * NB)

            @blk.gpsimd
            def _(pool):
                link = linker(pool, consts)
                link(nc.gpsimd.memset(ident[:, :], 0.0))
                link(nc.gpsimd.memset(ones[:, :], 1.0))
                link(nc.gpsimd.memset(tiny[:, 16:26], -0.5))
                link(nc.gpsimd.memset(ebase, float(np.e)))
                link(nc.gpsimd.memset(eps2, 1e-5))
                link(nc.gpsimd.affine_select(out=ident[:, :], in_=ident[:, :], compare_op=ALU.not_equal, fill=1.0,
                                             base=0, pattern=[[-1, P]], channel_multiplier=1))
                link(nc.gpsimd.affine_select(out=upper[:, :], in_=ones[:, :], compare_op=ALU.is_gt, fill=0.0,
                                             base=0, pattern=[[1, P]], channel_multiplier=-1))
                link(nc.gpsimd.iota(iota_row[:, :], pattern=[[1, P]], base=0, channel_multiplier=0,
                                    allow_small_or_imprecise_dtypes=True))
                link(nc.gpsimd.iota(iota_p[:, :], pattern=[[1, 1]], base=0, channel_multiplier=1,
                                    allow_small_or_imprecise_dtypes=True))
                link(nc.gpsimd.iota(rev_e[:, :], pattern=[[-1, E]], base=E, channel_multiplier=0,
                                    allow_small_or_imprecise_dtypes=True))
                assert link.n[0] == 10
                pool.wait_ge(small_in, 32)

                def gate(g):
                    lk = linker(pool, pool_link, g * POOL_LINKS)
                    pool.wait_ge(dlt_done, g + 1)
                    nc.gpsimd.tensor_tensor(ex2, ebase, dl2, ALU.pow).then_inc(ex_done, 1)
                    pool.wait_ge(y_done, g + 1)
                    pool.wait_ge(xb_in, g * 16 + 16)
                    xb = xb_sb[:, :, :]
                    nc.gpsimd.tensor_tensor(xb, xb, XN[:, :, :], ALU.add).then_inc(res_done, 1)
                    pool.wait_ge(bn_done, g + 1)
                    lk(nc.gpsimd.tensor_tensor(vpe, mv[:, :, 1], eps2, ALU.add))
                    nc.gpsimd.tensor_tensor(rstd, vpe, mhalf, ALU.pow).then_inc(rstd_done, 1)
                    pool.wait_ge(nrm_done, g + 1)
                    gb = gam[:, :].unsqueeze(1).to_broadcast([P, TB, D])
                    bb = bet[:, :].unsqueeze(1).to_broadcast([P, TB, D])
                    lk(nc.gpsimd.tensor_tensor(XN[:, :, :], XN[:, :, :], gb, ALU.mult))
                    nc.gpsimd.tensor_tensor(XN[:, :, :], XN[:, :, :], bb, ALU.add).then_inc(xn_ready, 1)
                    assert lk.n[0] == POOL_LINKS
                gate(0)
                with pool.Fori(1, NB) as g:
                    gate(g)

            @blk.scalar
            def _(act):
                for n in range(PRO):
                    src, hi, lo, scale, arrived = early_piece(n)
                    act.wait_ge(arrived, 32 if arrived in x_in else 16)
                    nc.scalar.activation(hi, src, ACT.Copy, scale=scale).then_inc(conv_hi, 1)

                def iteration(i):
                    for p in range(NP):
                        n = i * NP + p
                        q = p % 2
                        act.wait_ge(up_done, n + 1)
                        if not (isinstance(i, int) and p == 0):
                            act.wait_ge(h_done, n)
                        nc.scalar.activation(gelu_g[:, :, :], pG[q][:, :].rearrange("p (c s) -> p c s", c=2),
                                             ACT.Gelu_apprx_tanh, scale=1.0 / (SX * SW)).then_inc(gelu_done, 1)
                        for u in range(NCONV):
                            if SLOT_OF[u] != p:
                                continue
                            src, hi, lo, scale, b, loads = conv_piece(u, i)
                            act.wait_ge(buf_in[b], loads * 16)
                            if u == 0:
                                act.wait_ge(up_done, i * NP)
                                act.wait_ge(dn_done, i * NP)
                            if u == 6 and isinstance(i, int):
                                act.wait_ge(conv_lo, PRO)
                            nc.scalar.activation(hi, src if u < 6 or True else src, ACT.Copy, scale=scale).then_inc(conv_hi, 1)
                        act.wait_ge(h_done, n + 1)
                        if not (isinstance(i, int) and p < 2):
                            act.wait_ge(dn_done, n - 1)
                        nc.scalar.activation(hid_hl[:, q, 0], hid[:, :, :], ACT.Copy).then_inc(hh_done, 1)
                iteration(0)
                with act.Fori(1, NB) as i:
                    iteration(i)

            @blk.vector
            def _(dve):
                held = dve.alloc_register("held_dve")
                for n in range(PRO):
                    src, hi, lo, scale, arrived = early_piece(n)
                    dve.wait_ge(conv_hi, n + 1)
                    nc.vector.scalar_tensor_tensor(lo, src, scale, hi, ALU.mult, ALU.subtract).then_inc(conv_lo, 1)
                dve.wait_ge(gate_in, 48)
                dve.wait_ge(consts, 10)

                def evac(dst, count):
                    dve.wait_ge(dn_done, count)
                    nc.vector.tensor_scalar(dst[:, :, :], pD[:, :, 0:D], 1.0 / (SH * SW), None,
                                            ALU.mult).then_inc(ev_done, 1)

                def gate(slot, g, lk):
                    if slot == 1:
                        dve.wait_ge(gt_done, g + 1)
                        nc.vector.tensor_copy(gT, pR[:, 0:4]).then_inc(gTc_done, 1)
                    if slot == 2:
                        dve.wait_ge(hg_done, g + 1)
                        for j in range(2):
                            lk(nc.vector.scalar_tensor_tensor(junk_row, pR[0:1, 0:D], 0.0, g1_row[:, j, :],
                                                              ALU.max, ALU.mult, accum_out=logit2[:, j:j + 1]))
                        lk(nc.vector.tensor_reduce(mx1, logit2, AX, ALU.max))
                        nc.vector.tensor_scalar(dl2, logit2, mx1, None, ALU.subtract).then_inc(dlt_done, 1)
                    if slot == 3:
                        dve.wait_ge(ex_done, g + 1)
                        lk(nc.vector.tensor_reduce(sm1, ex2, AX, ALU.add))
                        lk(nc.vector.reciprocal(rs1, sm1))
                        nc.vector.tensor_scalar(w2row, ex2, rs1, None, ALU.mult).then_inc(w_done, 1)
                    if slot == 4:
                        dve.wait_ge(wb_done, g + 1)
                        lk(nc.vector.tensor_copy(wbc, pR[:, 0:2]))
                        lk(nc.vector.tensor_scalar(S_out[:, :, :], S_out[:, :, :], wbc[:, 1:2], None, ALU.mult))
                        dve.wait_ge(xb_in, g * 16 + 16)
                        nc.vector.scalar_tensor_tensor(XN[:, :, :], E_out[:, :, :], wbc[:, 0:1], S_out[:, :, :],
                                                       ALU.mult, ALU.add).then_inc(y_done, 1)
                    if slot == 5:
                        dve.wait_ge(y_done, g + 1)
                        lk(nc.vector.bn_stats(bst[:, 0, :], XN[:, 0, :]))
                        lk(nc.vector.bn_stats(bst[:, 1, :], XN[:, 1, :]), held, (consts, 10))
                        lk(nc.vector.bn_aggr(mv[:, 0, :], bst[:, 0, :]), held, (consts, 10))
                        nc.vector.bn_aggr(mv[:, 1, :], bst[:, 1, :]).then_inc(bn_done, 1)
                    if slot == 6:
                        dve.wait_ge(rstd_done, g + 1)
                        dve.wait_ge(res_done, g + 1)
                        dve.wait_ge(bn_done, g + 1)
                        for t in range(TB):
                            r = nc.vector.tensor_scalar(XN[:, t, :], XN[:, t, :], mv[:, t, 0:1], rstd[:, t:t + 1],
                                                        ALU.subtract, ALU.mult)
                        r.then_inc(nrm_done, 1)
                    if slot == 7:
                        dve.wait_ge(xnt_done, g + 1)
                        nc.vector.tensor_copy(xnT[:, :, :], pR[:, :].rearrange("p (k s) -> p k s", k=KD)).then_inc(xnTc_done, 1)
                    if slot == 8:
                        dve.wait_ge(log_done, g + 1)
                        nc.vector.tensor_scalar(LG[:, bass.ds(g * TB, TB), :],
                                                pR[:, 0:TB * E].rearrange("p (t e) -> p t e", t=TB),
                                                1e4, -1e4, ALU.min, ALU.max).then_inc(lg_done, 1)

                def iteration(i):
                    first = isinstance(i, int)
                    lk = linker(dve, dve_link, (i - 1) * DVE_LINKS)
                    for p in range(NP):
                        n = i * NP + p
                        q = p % 2
                        if p == 7 and not first:
                            gate(7, i - 1, lk)
                        dve.wait_ge(gelu_done, n + 1)
                        if not (first and p == 0):
                            dve.wait_ge(hl_done, n)
                        nc.vector.scalar_tensor_tensor(hid[:, :, :], pL[q][:, :].rearrange("p (c s) -> p c s", c=2),
                                                       SH / (SX * SW), gelu_g[:, :, :],
                                                       ALU.mult, ALU.mult).then_inc(h_done, 1)
                        for u in range(NCONV):
                            if SLOT_OF[u] != p:
                                continue
                            src, hi, lo, scale, b, loads = conv_piece(u, i)
                            dve.wait_ge(conv_hi, i * NCONV + PRO + u + 1)
                            nc.vector.scalar_tensor_tensor(flat3(lo), src, scale, flat3(hi),
                                                           ALU.mult, ALU.subtract).then_inc(conv_lo, 1)
                        if p == 4 and not first:
                            gate(4, i - 1, lk)
                        dve.wait_ge(hh_done, n + 1)
                        nc.vector.tensor_tensor(hid_hl[:, q, 1], hid[:, :, :], hid_hl[:, q, 0],
                                                ALU.subtract).then_inc(hl_done, 1)
                        if p == 0 and not first:
                            evac(E_out, i * NP)
                        if p == 4:
                            if not first:
                                dve.wait_ge(y_done, i)
                            evac(S_out, i * NP + PAIRS)
                        if not first and p in (1, 2, 3, 5, 6):
                            gate(p, i - 1, lk)
                    if not first:
                        gate(8, i - 1, lk)
                        assert lk.n[0] == DVE_LINKS, lk.n
                iteration(0)
                with dve.Fori(1, NB) as i:
                    iteration(i)
                evac(E_out, NB * NP)
                lk = linker(dve, dve_link, (NB - 1) * DVE_LINKS)
                for slot in range(1, 9):
                    gate(slot, NB - 1, lk)

            @blk.tensor
            def _(pe):
                def up(i, p):
                    q, s = p % 2, p // PAIRS
                    n = i * NP + p
                    if not (isinstance(i, int) and p < 2):
                        pe.wait_ge(h_done, n - 1)
                    if p == PAIRS:
                        pe.wait_ge(conv_lo, i * NCONV + PRO + 4)
                    tok = bass.ds(i * S, S)
                    for c in range(2):
                        f = slice((2 * (p % PAIRS) + c) * P, (2 * (p % PAIRS) + c + 1) * P)
                        for bank, j in ((pG[q], 0), (pL[q], 2)):
                            o = bank[:, c * S:(c + 1) * S]
                            wh, wl = ffn_w(s, j), ffn_w(s, j + 1)
                            for k in range(KD):
                                nc.tensor.matmul(o, wh[:, k, f], XTh[:, k, tok], start=(k == 0), stop=False)
                                nc.tensor.matmul(o, wh[:, k, f], XTl[:, k, tok], start=False, stop=False)
                                last = nc.tensor.matmul(o, wl[:, k, f], XTh[:, k, tok], start=False,
                                                        stop=(k == KD - 1))
                    last.then_inc(up_done, 1)

                def down(i, p):
                    q, s = p % 2, p // PAIRS
                    n = i * NP + p
                    pe.wait_ge(hl_done, n + 1)
                    if p == 0 and not (isinstance(i, int) and i == 0):
                        pe.wait_ge(ev_done, i * 2)
                    if p == PAIRS:
                        pe.wait_ge(ev_done, i * 2 + 1)
                        pe.wait_ge(conv_lo, i * NCONV + PRO + 6)
                    woh, wol = ffn_w(s, 4), ffn_w(s, 5)
                    for t in range(TB):
                        ts = slice(t * P, (t + 1) * P)
                        for c in range(2):
                            f = 2 * (p % PAIRS) + c
                            hh, hl = hid_hl[:, q, 0, c, ts], hid_hl[:, q, 1, c, ts]
                            nc.tensor.matmul(pD[:, t, 0:D], hh, woh[:, f, :],
                                             start=(p % PAIRS == 0 and c == 0), stop=False)
                            nc.tensor.matmul(pD[:, t, 0:D], hh, wol[:, f, :], start=False, stop=False)
                            last = nc.tensor.matmul(pD[:, t, 0:D], hl, woh[:, f, :], start=False,
                                                    stop=(p % PAIRS == PAIRS - 1 and c == 1))
                    last.then_inc(dn_done, 1)

                def gate(step, g):
                    if step == "columns":
                        pe.wait_ge(ev_done, g * 2 + 2)
                        for c in range(2 * KD):
                            src = (E_out if c < KD else S_out)[0:1, 0, (c % KD) * P:(c % KD + 1) * P]
                            last = nc.tensor.matmul(pR[:, c:c + 1], src, ones[0:1, 0:1], start=True, stop=True)
                        last.then_inc(gt_done, 1)
                    if step == "hidden":
                        pe.wait_ge(gTc_done, g + 1)
                        for c in range(2 * KD):
                            last = nc.tensor.matmul(pR[0:1, 0:D], gT[:, c:c + 1], g0_sb[:, c, :],
                                                    start=(c == 0), stop=(c == 2 * KD - 1))
                        last.then_inc(hg_done, 1)
                    if step == "weights":
                        pe.wait_ge(w_done, g + 1)
                        nc.tensor.matmul(pR[:, 0:2], ones[0:1, :], w2row, start=True, stop=True).then_inc(wb_done, 1)
                    if step == "transpose":
                        pe.wait_ge(xn_ready, g + 1)
                        for t in range(TB):
                            for k in range(KD):
                                last = nc.tensor.transpose(pR[:, k * S + t * P:k * S + (t + 1) * P],
                                                           XN[:, t, k * P:(k + 1) * P], ident[:, :])
                        last.then_inc(xnt_done, 1)
                    if step == "logits":
                        pe.wait_ge(xnTc_done, g + 1)
                        for t in range(TB):
                            for k in range(KD):
                                last = nc.tensor.matmul(pR[:, t * E:(t + 1) * E], xnT[:, k, t * P:(t + 1) * P],
                                                        rw_sb[:, k, :], start=(k == 0), stop=(k == KD - 1))
                        last.then_inc(log_done, 1)

                pe.wait_ge(conv_lo, PRO)
                pe.wait_ge(gate_in, 48)
                pe.wait_ge(consts, 10)
                STEP = {1: "columns", 2: "hidden", 4: "weights", 7: "transpose"}
                for p in range(NP):
                    up(0, p)
                    if p:
                        down(0, p - 1)
                with pe.Fori(1, NB) as i:
                    for p in range(NP):
                        if p in (4, 7):
                            gate(STEP[p], i - 1)
                        up(i, p)
                        if p in (1, 2):
                            gate(STEP[p], i - 1)
                        if p == 7:
                            gate("logits", i - 1)
                        if p:
                            down(i, p - 1)
                        else:
                            down(i - 1, NP - 1)
                down(NB - 1, NP - 1)
                for step in ("columns", "hidden", "weights", "transpose", "logits"):
                    gate(step, NB - 1)
        NA = TOPK * NT
        onehot_slot = xt_area[:, :].bitcast(F32).rearrange("p (a m) -> p a m", a=NA)
        blk_vals = ffn_area[:, 12 * nw // 2:12 * nw // 2 + 2 * NA * 3 * NBLK].bitcast(F32).rearrange(
            "p (a v j) -> p a v j", a=NA, v=3)
        work = stage[:, :, :].rearrange("p a b -> p (a b)")
        NTE = NT * E

        def tile_of(n, dt=F32):
            v = work[:, n * NTE:(n + 1) * NTE]
            return v if dt == F32 else v.bitcast(dt)

        def te(ap):
            return ap.rearrange("p (t e) -> p t e", e=E)

        d_t, ex_t, p_t, eq_t, oh = te(tile_of(0)), te(tile_of(1)), te(tile_of(2)), te(tile_of(3)), [
            te(tile_of(4)), te(tile_of(5))]
        M_t, cum, pos_t = te(tile_of(6)), [te(tile_of(7)), te(tile_of(8))], te(tile_of(9))
        tot_t = te(tile_of(10))
        sm = tile_of(11)
        m16, s16, r16 = sm[:, 0:NT], sm[:, NT:2 * NT], sm[:, 2 * NT:3 * NT]
        gate2 = sm[:, 64:64 + NA].rearrange("p (r t) -> p r t", r=TOPK)
        k16 = sm[:, 3 * NT:4 * NT]
        sn = tile_of(12)
        nb_f, nb_raw, start_f = sn[:, 0:E], sn[:, E:2 * E], sn[:, 2 * E:3 * E]
        bend = [sn[:, 3 * E:4 * E], sn[:, 4 * E:5 * E]]
        nb_i = tile_of(13, I32)[:, 0:E]
        POS = tile_of(14)[:, 0:NA]
        pos_i, blk_i, row_i = (tile_of(15, I32)[:, n * NA:(n + 1) * NA] for n in range(3))
        blk_f, row_f, dest_f = (tile_of(16)[:, n * NA:(n + 1) * NA] for n in range(3))
        tab = work[:, 17 * NTE:17 * NTE + 3 * NBLK].rearrange("p (v j) -> p v j", v=3)
        un_t = tile_of(18)[:, 0:NBLK]
        pad_row = tile_of(18)[:, 64:64 + NBLK]
        be_cmp = work[0:1, 19 * NTE:19 * NTE + NBLK * E].rearrange("p (j e) -> p j e", e=E)
        be_f = work[0:1, 22 * NTE:22 * NTE + NBLK]
        dest_i = xb_sb[:, 0, 0:NBLK].bitcast(I32)
        tok_i = xb_sb[:, 0, 64:64 + NBLK].bitcast(I32)
        gate_silu = xb_sb[:, 0, 128:128 + NBLK]
        gate_up_s = xb_sb[:, 0, 192:192 + NBLK]
        be_i = xb_sb[0:1, 1, 0:NBLK].bitcast(I32)
        tok_col = xb_sb[:, 1, 64:64 + UNR].bitcast(I32)
        dest_col = xb_sb[:, 1, 80:80 + UNR].bitcast(I32)

        shift_done, exp_done, mask_done, prefix_done, slots_done, vals_done, table_done, dest_ready = (
            sem(n) for n in ("shift_done", "exp_done", "mask_done", "prefix_done", "slots_done",
                             "vals_done", "table_done", "dest_ready"))
        route_link = sem("route_link")

        def over_e(ap):
            return ap.unsqueeze(2).to_broadcast([P, NT, E])

        def over_t(ap):
            return ap.unsqueeze(1).to_broadcast([P, NT, E])

        with nc.Block() as blk:
            @blk.gpsimd
            def _(pool):
                nc.gpsimd.iota(pad_row, pattern=[[P, NBLK]], base=TOPK * TOK, channel_multiplier=1,
                               allow_small_or_imprecise_dtypes=True).then_inc(dest_ready, 1)
                nc.gpsimd.iota(dest_f, pattern=[[TOK, TOPK], [P, NT]], base=0, channel_multiplier=1,
                               allow_small_or_imprecise_dtypes=True).then_inc(dest_ready, 1)

            @blk.scalar
            def _(act):
                act.wait_ge(shift_done, 1)
                nc.scalar.activation(ex_t, d_t, ACT.Exp).then_inc(exp_done, 1)

            @blk.vector
            def _(dve):
                lk = linker(dve, route_link)
                v = nc.vector
                lk(v.tensor_reduce(m16, LG[:, :, :], AX, ALU.max))
                v.tensor_tensor(d_t, LG[:, :, :], over_e(m16), ALU.subtract).then_inc(shift_done, 1)
                dve.wait_ge(exp_done, 1)
                lk(v.tensor_reduce(s16, ex_t, AX, ALU.add))
                lk(v.tensor_scalar(s16, s16, 1e-8, None, ALU.add))
                lk(v.reciprocal(r16, s16))
                lk(v.tensor_tensor(p_t, ex_t, over_e(r16), ALU.mult))
                lk(v.tensor_scalar(p_t, p_t, 1e-8, 1.0, ALU.max, ALU.min))
                for r in range(TOPK):
                    lk(v.tensor_reduce(gate2[:, r, :], p_t, AX, ALU.max))
                    lk(v.tensor_tensor(eq_t, p_t, over_e(gate2[:, r, :]), ALU.is_equal))
                    lk(v.tensor_tensor(eq_t, eq_t, over_t(rev_e[:, :]), ALU.mult))
                    lk(v.tensor_reduce(k16, eq_t, AX, ALU.max))
                    lk(v.tensor_tensor(oh[r], over_t(rev_e[:, :]), over_e(k16), ALU.is_equal))
                    if r == 0:
                        lk(v.scalar_tensor_tensor(p_t, oh[0], -4.0, p_t, ALU.mult, ALU.add))
                v.tensor_tensor(M_t, oh[0], oh[1], ALU.add).then_inc(mask_done, 1)
                dve.wait_ge(prefix_done, 1)
                lk(v.tensor_copy(tot_t, te(pL[0][:, 0:NTE])))
                lk(v.tensor_copy(cum[0], tot_t))
                b, sh = 0, 1
                while sh < NT:
                    lk(v.tensor_tensor(cum[1 - b][:, sh:, :], cum[b][:, sh:, :], cum[b][:, :NT - sh, :], ALU.add))
                    lk(v.tensor_copy(cum[1 - b][:, :sh, :], cum[b][:, :sh, :]))
                    b, sh = 1 - b, 2 * sh
                incl = cum[b]
                lk(v.tensor_scalar(nb_i, incl[:, NT - 1, :], float(P - 1), None, ALU.add))
                lk(v.tensor_scalar(nb_i, nb_i, 7, None, ALU.logical_shift_right))
                lk(v.tensor_copy(nb_f, nb_i))
                lk(v.tensor_copy(bend[0], nb_f))
                c, sh = 0, 1
                while sh < E:
                    lk(v.tensor_tensor(bend[1 - c][:, sh:], bend[c][:, sh:], bend[c][:, :E - sh], ALU.add))
                    lk(v.tensor_copy(bend[1 - c][:, :sh], bend[c][:, :sh]))
                    c, sh = 1 - c, 2 * sh
                lk(v.tensor_tensor(start_f, bend[c], nb_f, ALU.subtract))
                lk(v.tensor_scalar(start_f, start_f, float(P), None, ALU.mult))
                lk(v.tensor_tensor(pos_t, incl, tot_t, ALU.subtract))
                lk(v.tensor_tensor(pos_t, pos_t, te(pG[0][:, 0:NTE]), ALU.add))
                lk(v.tensor_tensor(pos_t, pos_t, over_t(start_f), ALU.add))
                for r in range(TOPK):
                    lk(v.tensor_tensor(eq_t, pos_t, oh[r], ALU.mult))
                    lk(v.tensor_reduce(POS[:, r * NT:(r + 1) * NT], eq_t, AX, ALU.add))
                lk(v.tensor_copy(pos_i, POS))
                lk(v.tensor_scalar(blk_i, pos_i, 7, None, ALU.logical_shift_right))
                lk(v.tensor_scalar(row_i, pos_i, P - 1, None, ALU.bitwise_and))
                lk(v.tensor_copy(blk_f, blk_i))
                lk(v.tensor_copy(row_f, row_i))
                dve.wait_ge(dest_ready, 2)
                shape = [P, NA, NBLK]
                lk(v.tensor_tensor(blk_vals[:, :, 2, :], iota_row[:, 0:NBLK].unsqueeze(1).to_broadcast(shape),
                                   blk_f.unsqueeze(2).to_broadcast(shape), ALU.is_equal))
                lk(v.tensor_tensor(blk_vals[:, :, 0, :], blk_vals[:, :, 2, :],
                                   dest_f.unsqueeze(2).to_broadcast(shape), ALU.mult))
                v.tensor_tensor(blk_vals[:, :, 1, :], blk_vals[:, :, 2, :],
                                sm[:, 64:64 + NA].unsqueeze(2).to_broadcast(shape), ALU.mult).then_inc(vals_done, 1)
                for a in range(0, NA, 8):
                    shape = [P, 8, P]
                    v.tensor_tensor(onehot_slot[:, a:a + 8, :], iota_row[:, :].unsqueeze(1).to_broadcast(shape),
                                    row_f[:, a:a + 8].unsqueeze(2).to_broadcast(shape),
                                    ALU.is_equal).then_inc(slots_done, 1)
                shape = [1, NBLK, E]
                lk(v.tensor_tensor(be_cmp, bend[c][0:1, :].unsqueeze(1).to_broadcast(shape),
                                   iota_row[0:1, 0:NBLK].unsqueeze(2).to_broadcast(shape), ALU.is_le))
                lk(v.tensor_reduce(be_f, be_cmp, AX, ALU.add))
                lk(v.tensor_scalar(be_i, be_f, float(E - 1), None, ALU.min))
                dve.wait_ge(table_done, 1)
                lk(v.tensor_copy(tab, pR[:, 0:3 * NBLK].rearrange("p (v j) -> p v j", v=3)))
                lk(v.tensor_scalar(un_t, tab[:, 2, :], -1.0, 1.0, ALU.mult, ALU.add))
                lk(v.tensor_tensor(un_t, un_t, pad_row, ALU.mult))
                lk(v.tensor_tensor(dest_i, tab[:, 0, :], un_t, ALU.add))
                lk(v.tensor_scalar(tok_i, dest_i, TOK - 1, None, ALU.bitwise_and))
                lk(v.tensor_scalar(gate_silu, tab[:, 1, :], 1.0 / (SN * SE), None, ALU.mult))
                lk(v.tensor_scalar(gate_up_s, tab[:, 1, :], SHE / (SN * SE), None, ALU.mult))

            @blk.tensor
            def _(pe):
                pe.wait_ge(mask_done, 1)
                m = M_t.rearrange("p t e -> p (t e)")
                nc.tensor.matmul(pG[0][:, 0:NTE], upper[:, :], m, start=True, stop=True)
                nc.tensor.matmul(pL[0][:, 0:NTE], ones[:, :], m, start=True, stop=True).then_inc(prefix_done, 1)
                pe.wait_ge(vals_done, 1)
                for a in range(NA):
                    if a % 8 == 0:
                        pe.wait_ge(slots_done, a // 8 + 1)
                    last = nc.tensor.matmul(pR[:, 0:3 * NBLK], onehot_slot[:, a, :],
                                            blk_vals[:, a].rearrange("p v j -> p (v j)"),
                                            start=(a == 0), stop=(a == NA - 1))
                last.then_inc(table_done, 1)

        mix = ffn_area[:, 0:12 * nw // 2].bitcast(F32)
        xg = [mix[:, u * D:(u + 1) * D] for u in range(UNR)]
        orow = [mix[:, (UNR + u) * D:(UNR + u + 1) * D] for u in range(UNR)]
        sg = gelu_g[:, :, :].rearrange("p c s -> p (c s)")
        hm = hid[:, :, :].rearrange("p c s -> p (c s)")
        xgT = S_out[:, :, :].rearrange("p t d -> p (t d)").bitcast(F16).rearrange(
            "p (h k s) -> p h k s", h=4, k=KD)
        hT = hid_hl[:, 0].rearrange("p h c s -> p h (c s)").rearrange("p h (k s) -> p h k s", k=KE)
        pX, pH = pG[1], pL[1]
        xg_in, moe_stored = [sem(f"xg_in{u}") for u in range(UNR)], [sem(f"moe_stored{u}") for u in range(UNR)]
        xt_done, xh_done, xl_done, gu_done, silu_done, hm_done, ht_done, hth_done, htl_done, dnb_done, out_ready = (
            sem(n) for n in ("xt_done", "xh_done", "xl_done", "gu_done", "silu_done", "hm_done", "ht_done",
                             "hth_done", "htl_done", "dnb_done", "out_ready"))
        mix_link = sem("mix_link")
        NI = NBLK // UNR

        adapt = ffn_area[:, :].bitcast(F32)
        base = 2 * UNR * D
        per = KD * A + 3 * D
        aW1 = [adapt[:, base + b * per:base + b * per + KD * A].rearrange("p (k a) -> p k a", k=KD) for b in range(NB)]
        aRows = adapt[:, base:base + NB * per].rearrange("p (b v) -> p b v", b=NB)
        aW1 = aRows[:, :, 0:KD * A].rearrange("p b (k a) -> p b k a", k=KD)
        aW2 = aRows[0:A + 1, :, KD * A:KD * A + D]
        aGam = aRows[:, :, KD * A + D:KD * A + 2 * D]
        aBet = aRows[:, :, KD * A + 2 * D:KD * A + 3 * D]
        base += NB * per
        aB1 = adapt[0:A, base:base + NB]
        base += NB
        rr = adapt[:, base:base + 2 * TOPK * TB * D].rearrange("p (q r t d) -> p q r t d", q=2, r=TOPK, t=TB)
        base += 2 * TOPK * TB * D
        x2T = adapt[:, base:base + KD * S].rearrange("p (k s) -> p k s", k=KD)
        base += KD * S
        aH = adapt[0:A + 1, base:base + S]
        w1_in = xt_area[:, 0:2 * KD * F].bitcast(F32).rearrange("p (k f) -> p k f", k=KD)
        w2_in = xt_area[:, 2 * KD * F:].bitcast(F32).rearrange("p (c d) -> p c d", c=FC)
        b1_sb = tiny[:, 44:44 + FC]
        b2_sb = gam[:, :]
        adapt_in, ffn1_in = sem("adapt_in"), sem("ffn1_in")

        with nc.Block() as blk:
            @blk.gpsimd
            def _(pool):
                held = pool.alloc_register("held_pool")
                def gather(i, u, links, wait=True):
                    j = i * UNR + u
                    if wait:
                        pool.wait_ge(xt_done, j - UNR + 1)
                    nc.gpsimd.tensor_copy(tok_col[:, u:u + 1], tok_i[:, bass.ds(j, 1)]).then_inc(mix_link, 1)
                    hold(pool, held, mix_link, links, (consts, 10))
                    nc.gpsimd.indirect_dma_start(xg[u], None, xn_dram, bass.IndirectOffsetOnAxis(
                        ap=tok_col[:, u:u + 1], axis=0)).then_inc(xg_in[u], 16)

                def scatter(i, u, links):
                    j = i * UNR + u
                    if not (isinstance(i, int) and i == 0):
                        pool.wait_ge(moe_stored[u], i * 16)
                    nc.gpsimd.tensor_copy(dest_col[:, u:u + 1], dest_i[:, bass.ds(j, 1)]).then_inc(mix_link, 1)
                    pool.wait_ge(mix_link, links)
                    hold(pool, held, out_ready, j + 1, (consts, 10))
                    nc.gpsimd.indirect_dma_start(moe_dram, bass.IndirectOffsetOnAxis(
                        ap=dest_col[:, u:u + 1], axis=0), orow[u], None).then_inc(moe_stored[u], 16)
                for u in range(UNR):
                    gather(0, u, u + 1, wait=False)
                for u in range(UNR):
                    gather(1, u, UNR + 2 * u + 1)
                    scatter(0, u, UNR + 2 * u + 2)
                with pool.Fori(1, NI - 1) as i:
                    for u in range(UNR):
                        gather(i + 1, u, UNR + i * 2 * UNR + 2 * u + 1)
                        scatter(i, u, UNR + i * 2 * UNR + 2 * u + 2)
                for u in range(UNR):
                    scatter(NI - 1, u, UNR + (NI - 1) * 2 * UNR + u + 1)
                for u in range(UNR):
                    pool.wait_ge(moe_stored[u], NI * 16)

            @blk.scalar
            def _(act):
                def split_x(j):
                    act.wait_ge(xt_done, j + 1)
                    nc.scalar.activation(xgT[:, 0], pX[:, 0:D].rearrange("p (k s) -> p k s", k=KD), ACT.Copy,
                                         scale=SN).then_inc(xh_done, 1)

                def block(j, last=False):
                    act.wait_ge(gu_done, j + 1)
                    nc.scalar.activation(sg, pG[0][:, :], ACT.Silu,
                                         scale=gate_silu[:, bass.ds(j, 1)]).then_inc(silu_done, 1)
                    if not last:
                        split_x(j + 1)
                    act.wait_ge(ht_done, j + 1)
                    nc.scalar.activation(hT[:, 0], pH[:, :].rearrange("p (k s) -> p k s", k=KE),
                                         ACT.Copy).then_inc(hth_done, 1)
                split_x(0)
                with act.Fori(0, NI - 1) as i:
                    for u in range(UNR):
                        block(i * UNR + u)
                for u in range(UNR):
                    block((NI - 1) * UNR + u, last=(u == UNR - 1))

            @blk.sync
            def _(sp):
                with sp.Fori(0, NB) as b:
                    n = sp.value_load(itC[0:1, bass.ds(b, 1)], min_val=0, max_val=NL - 1)
                    one = bass.ds(n, 1)
                    at = bass.ds(b, 1)
                    sp.dma_start(aW1[:, at], cW1[one, :, :].rearrange("l (k p) a -> p l k a", p=P)).then_inc(adapt_in, 16)
                    sp.dma_start(aW2[0:A, at, :], cW2[one, :, :].rearrange("l a d -> a l d")).then_inc(adapt_in, 16)
                    sp.dma_start(aW2[A:A + 1, at, :], cb2[one, :].unsqueeze(0)).then_inc(adapt_in, 16)
                    sp.dma_start(aB1[:, at], cb1T[one, :, :].rearrange("l a o -> (l a) o")).then_inc(adapt_in, 16)
                    sp.dma_start(aGam[:, at, :], cgamma[one, :].partition_broadcast(P)).then_inc(adapt_in, 16)
                    sp.dma_start(aBet[:, at, :], cbeta[one, :].partition_broadcast(P)).then_inc(adapt_in, 16)
                sp.dma_start(w1_in, w1T.rearrange("(k p) f -> p k f", p=P)).then_inc(ffn1_in, 16)
                sp.dma_start(w2_in, w2T.rearrange("(c p) d -> p c d", p=P)).then_inc(ffn1_in, 16)
                sp.dma_start(b1_sb, b1T).then_inc(ffn1_in, 16)
                sp.dma_start(b2_sb, b2.partition_broadcast(P)).then_inc(ffn1_in, 16)
                sp.wait_ge(adapt_in, 6 * 16 * NB)
                sp.wait_ge(ffn1_in, 64)

            @blk.vector
            def _(dve):
                def split_x(j):
                    dve.wait_ge(xh_done, j + 1)
                    nc.vector.scalar_tensor_tensor(xgT[:, 1], pX[:, 0:D].rearrange("p (k s) -> p k s", k=KD), SN,
                                                   xgT[:, 0], ALU.mult, ALU.subtract).then_inc(xl_done, 1)

                def emit(i, u):
                    dve.wait_ge(dnb_done, i * UNR + u + 1)
                    if not (isinstance(i, int) and i == 0):
                        dve.wait_ge(moe_stored[u], i * 16)
                    nc.vector.tensor_scalar(orow[u], pD[:, 0, 0:D], 1.0 / (SHE * SE), None,
                                            ALU.mult).then_inc(out_ready, 1)

                def block(i, u, first=False, last=False):
                    j = i * UNR + u
                    dve.wait_ge(silu_done, j + 1)
                    nc.vector.scalar_tensor_tensor(hm, pL[0][:, :], gate_up_s[:, bass.ds(j, 1)], sg,
                                                   ALU.mult, ALU.mult).then_inc(hm_done, 1)
                    if not last:
                        split_x(j + 1)
                    if not first:
                        emit(i if u else i - 1, (u - 1) % UNR)
                    dve.wait_ge(hth_done, j + 1)
                    nc.vector.tensor_tensor(hT[:, 1], pH[:, :].rearrange("p (k s) -> p k s", k=KE), hT[:, 0],
                                            ALU.subtract).then_inc(htl_done, 1)
                split_x(0)
                for u in range(UNR):
                    block(0, u, first=(u == 0))
                with dve.Fori(1, NI - 1) as i:
                    for u in range(UNR):
                        block(i, u)
                for u in range(UNR):
                    block(NI - 1, u, last=(u == UNR - 1))
                emit(NI - 1, UNR - 1)

            @blk.tensor
            def _(pe):
                def transpose_x(i, u):
                    pe.wait_ge(xg_in[u], i * 16 + 16)
                    if not (isinstance(i, int) and i * UNR + u == 0):
                        pe.wait_ge(xl_done, i * UNR + u)
                    for k in range(KD):
                        last = nc.tensor.transpose(pX[:, k * P:(k + 1) * P], xg[u][:, k * P:(k + 1) * P], ident[:, :])
                    last.then_inc(xt_done, 1)

                def gate_up(i, u):
                    j = i * UNR + u
                    e = pe.value_load(be_i[0:1, bass.ds(j, 1)], min_val=0, max_val=E - 1)
                    pe.wait_ge(xl_done, j + 1)
                    if not (isinstance(j, int) and j == 0):
                        pe.wait_ge(hm_done, j)
                    for h, bank in enumerate((pG[0], pL[0])):
                        for k in range(KD):
                            wh = GUh[:, k, bass.ds(e, 1), h * FE:(h + 1) * FE].rearrange("p e f -> p (e f)")
                            wl = GUl[:, k, bass.ds(e, 1), h * FE:(h + 1) * FE].rearrange("p e f -> p (e f)")
                            nc.tensor.matmul(bank[:, :], xgT[:, 0, k, :], wh, start=(k == 0), stop=False)
                            nc.tensor.matmul(bank[:, :], xgT[:, 1, k, :], wh, start=False, stop=False)
                            last = nc.tensor.matmul(bank[:, :], xgT[:, 0, k, :], wl, start=False, stop=(k == KD - 1))
                    last.then_inc(gu_done, 1)
                    return e

                def transpose_h(j):
                    pe.wait_ge(hm_done, j + 1)
                    if not (isinstance(j, int) and j == 0):
                        pe.wait_ge(htl_done, j)
                    for k in range(KE):
                        last = nc.tensor.transpose(pH[:, k * P:(k + 1) * P], hm[:, k * P:(k + 1) * P], ident[:, :])
                    last.then_inc(ht_done, 1)

                def down(j):
                    e = pe.value_load(be_i[0:1, bass.ds(j, 1)], min_val=0, max_val=E - 1)
                    pe.wait_ge(htl_done, j + 1)
                    if not (isinstance(j, int) and j == 0):
                        pe.wait_ge(out_ready, j)
                    for k in range(KE):
                        wh = DNh[:, k, bass.ds(e, 1), :].rearrange("p e d -> p (e d)")
                        wl = DNl[:, k, bass.ds(e, 1), :].rearrange("p e d -> p (e d)")
                        o = pD[:, 0, 0:D]
                        nc.tensor.matmul(o, hT[:, 0, k, :], wh, start=(k == 0), stop=False)
                        nc.tensor.matmul(o, hT[:, 1, k, :], wh, start=False, stop=False)
                        last = nc.tensor.matmul(o, hT[:, 0, k, :], wl, start=False, stop=(k == KE - 1))
                    last.then_inc(dnb_done, 1)

                def block(i, u, first=False, last=False):
                    j = i * UNR + u
                    gate_up(i, u)
                    if not last:
                        transpose_x(i + 1 if u == UNR - 1 else i, (u + 1) % UNR)
                    if not first:
                        down(j - 1)
                    transpose_h(j)
                transpose_x(0, 0)
                for u in range(UNR):
                    block(0, u, first=(u == 0))
                with pe.Fori(1, NI - 1) as i:
                    for u in range(UNR):
                        block(i, u)
                for u in range(UNR):
                    block(NI - 1, u, last=(u == UNR - 1))
                down(NBLK - 1)
        if stop == "M":
            return
        X = stage[:, :, :].rearrange("p a b -> p (a b)").rearrange("p (n d) -> p n d", n=NT)
        big = moe_area[:, :].bitcast(F32)
        h_all = big[:, 0:FC * TOK].rearrange("p (f n) -> p f n", f=FC)
        o = FC * TOK
        X3 = big[:, o:o + NT * D].rearrange("p (n d) -> p n d", n=NT)
        o += NT * D
        x3q = big[:, o:o + KD * TOK // 2].bitcast(BF16).rearrange("p (k n) -> p k n", k=KD)
        x3T = xt_area[:, :].bitcast(F32).rearrange("p (k n) -> p k n", k=KD)
        hq = ffn_area[:, 0:FC * TOK].bitcast(BF16).rearrange("p (f n) -> p f n", f=FC)
        w1q = g0_sb[:, :, :].rearrange("p c d -> p (c d)").bitcast(BF16).rearrange("p (k f) -> p k f", k=KD)
        w2q = [t[:, :, :].rearrange("p t d -> p (t d)").bitcast(BF16).rearrange("p (c d) -> p c d", d=D)
               for t in (E_out, XN)]
        stats = sb("stats", [P, 6 * NT])
        mv_all = sb("mv_all", [P, 2 * NT])
        mvv = mv_all[:, :].rearrange("p (n s) -> p n s", s=2)
        rstd_all = sb("rstd_all", [P, 2 * NT])
        mh_all = rstd_all[:, NT:]
        amax = sb("amax", [P, 2 * NB])
        spread = sb("spread", [P, 64])
        wmax, wtop, wdiag, wall = spread[:, 0:2], spread[0:2, 2:3], spread[0:2, 4:6], spread[:, 6:8]
        wstep, winv = spread[:, 8:10], spread[:, 10:12]
        xmax, xtop, xdiag, xall, xstep, xinv = (spread[:, 12 + n:13 + n] for n in range(6))
        hmax, htop, hdiag, hall, hstep, hinv = (spread[:, 18 + n:19 + n] for n in range(6))
        s1, s2, b1s = spread[:, 24:25], spread[:, 25:26], spread[:, 32:32 + FC]
        b2s = bet[:, :]

        rows_in = [sem(f"rows_in{q}") for q in range(2)]
        rows_used, t2_done, t2c_done, m1_done, relu_done, m2_done, pre_done, pre_link = (sem(n) for n in (
            "rows_used", "t2_done", "t2c_done", "m1_done", "relu_done", "m2_done", "pre_done", "pre_link"))
        var_done, rstd2_done, nrm2_done, x3_done, t3_done, t3c_done, max_done, c_link, cp_link = (sem(n) for n in (
            "var_done", "rstd2_done", "nrm2_done", "x3_done", "t3_done", "t3c_done", "max_done", "c_link", "cp_link"))
        wq_link, wt_ready, wt_done, wd_ready, wd_done, wq_done = (sem(n) for n in (
            "wq_link", "wt_ready", "wt_done", "wd_ready", "wd_done", "wq_done"))
        one_row = sem("one_row")
        pT2, pA, pT3, pW = pR, pM, pG[0], pG[1]

        def scale_chain(lk, v, dve, part, top, diag, full, step, inv, bank, n, t_ready, t_done, d_ready, d_done, base):
            t_ready_ins = lk
            dve.wait_ge(t_done, base)
            lk(v.tensor_reduce(top, bank[0:n, 0:P], AX, ALU.max))
            v.tensor_scalar(diag, ident[0:n, 0:n], top, None, ALU.mult).then_inc(d_ready, 1)
            dve.wait_ge(d_done, base)
            lk(v.tensor_copy(full, bank[:, P:P + n]))
            lk(v.tensor_scalar(step, full, 1e-6, 1.0 / 127.0, ALU.max, ALU.mult))
            lk(v.reciprocal(inv, step))

        def spread_max(pe, part, diag, bank, n, t_ready, t_done, d_ready, d_done, base):
            pe.wait_ge(t_ready, base)
            nc.tensor.transpose(bank[0:n, 0:P], part, ident[:, :]).then_inc(t_done, 1)
            pe.wait_ge(d_ready, base)
            nc.tensor.matmul(bank[:, P:P + n], ones[0:n, :], diag, start=True, stop=True).then_inc(d_done, 1)

        with nc.Block() as blk:
            @blk.sync
            def _(sp):
                rank_rows = moe_dram[0:TOPK * TOK, :].rearrange("(r b t p) d -> p b r t d", r=TOPK, t=TB, p=P)
                res_rows = res_dram.rearrange("(b t p) d -> p b t d", t=TB, p=P)
                for b in range(NB):
                    q = b % 2
                    if b >= 2:
                        sp.wait_ge(rows_used, b - 1)
                    sp.dma_start(X[:, b * TB:(b + 1) * TB, :], res_rows[:, b]).then_inc(rows_in[q], 16)
                    for r in range(TOPK):
                        sp.dma_start(rr[:, q, r], rank_rows[:, b, r]).then_inc(rows_in[q], 16)

            @blk.gpsimd
            def _(pool):
                lk = linker(pool, cp_link)
                lk(nc.gpsimd.memset(mh_all, -0.5))
                nc.gpsimd.memset(aH[A:A + 1, :], 1.0).then_inc(one_row, 1)
                pool.wait_ge(one_row, 1)
                for b in range(NB):
                    q = b % 2
                    xb = X[:, b * TB:(b + 1) * TB, :]
                    pool.wait_ge(rows_in[q], 48 * (b // 2 + 1))
                    lk(nc.gpsimd.tensor_tensor(xb, xb, rr[:, q, 0], ALU.add))
                    nc.gpsimd.tensor_tensor(xb, xb, rr[:, q, 1], ALU.add).then_inc(rows_used, 1)
                pool.wait_ge(var_done, 1)
                nc.gpsimd.tensor_tensor(rstd_all[:, 0:NT], stats[:, 0:NT], mh_all, ALU.pow).then_inc(rstd2_done, 1)
                for b in range(NB):
                    x3 = X3[:, b * TB:(b + 1) * TB, :]
                    pool.wait_ge(nrm2_done, b + 1)
                    lk(nc.gpsimd.tensor_tensor(x3, x3, aGam[:, b, :].unsqueeze(1).to_broadcast([P, TB, D]), ALU.mult))
                    nc.gpsimd.tensor_tensor(x3, x3, aBet[:, b, :].unsqueeze(1).to_broadcast([P, TB, D]),
                                            ALU.add).then_inc(x3_done, 1)

            @blk.scalar
            def _(act):
                for b in range(NB):
                    act.wait_ge(t2_done, b + 1)
                    if b:
                        act.wait_ge(m1_done, b)
                    nc.scalar.activation(x2T, pT2.rearrange("p (k s) -> p k s", k=KD), ACT.Copy).then_inc(t2c_done, 1)
                    act.wait_ge(m1_done, b + 1)
                    if b:
                        act.wait_ge(m2_done, b)
                    nc.scalar.activation(aH[0:A, :], pA[0:A, 0:S], ACT.Relu, bias=aB1[:, b:b + 1]).then_inc(relu_done, 1)
                for b in range(NB):
                    act.wait_ge(t3_done, b + 1)
                    nc.scalar.activation(x3T[:, :, b * S:(b + 1) * S], pT3.rearrange("p (k s) -> p k s", k=KD),
                                         ACT.Copy).then_inc(t3c_done, 1)

            @blk.vector
            def _(dve):
                v = nc.vector
                lk = linker(dve, wq_link)
                lk(v.tensor_reduce(wmax[:, 0:1], w1_in.rearrange("p k f -> p (k f)"), AX, ALU.max, apply_absolute_value=True))
                v.tensor_reduce(wmax[:, 1:2], w2_in.rearrange("p c d -> p (c d)"), AX, ALU.max,
                                apply_absolute_value=True).then_inc(wt_ready, 1)
                scale_chain(lk, v, dve, wmax, wtop, wdiag, wall, wstep, winv, pW, 2, wt_ready, wt_done, wd_ready, wd_done, 1)
                for j, (w, q) in enumerate(((w1_in, [w1q]), (w2_in, w2q))):
                    lk(v.tensor_scalar(w, w, winv[:, j:j + 1], MAGIC, ALU.mult, ALU.add))
                    for n, part in enumerate(q):
                        c = w.shape[1] // len(q)
                        lk(v.tensor_scalar(part, w[:, n * c:(n + 1) * c, :], MAGIC, None, ALU.subtract))
                st = stats[:, :].rearrange("p (n s) -> p n s", s=6)
                for b in range(NB):
                    t = slice(b * TB, (b + 1) * TB)
                    dve.wait_ge(m2_done, b + 1)
                    v.tensor_tensor(X3[:, t, :], pD[:, :, 0:D], X[:, t, :], ALU.add).then_inc(pre_done, 1)
                    dve.wait_ge(pre_done, b + 1)
                    for n in range(b * TB, (b + 1) * TB):
                        lk(v.bn_stats(st[:, n, :], X3[:, n, :]))
                        lk(v.bn_aggr(mvv[:, n, :], st[:, n, :]))
                v.tensor_scalar(stats[:, 0:NT], mvv[:, :, 1], 1e-5, None, ALU.add).then_inc(var_done, 1)
                dve.wait_ge(rstd2_done, 1)
                for b in range(NB):
                    for n in range(b * TB, (b + 1) * TB):
                        last = v.tensor_scalar(X3[:, n, :], X3[:, n, :], mvv[:, n, 0:1], rstd_all[:, n:n + 1],
                                               ALU.subtract, ALU.mult)
                    last.then_inc(nrm2_done, 1)
                for b in range(NB):
                    dve.wait_ge(t3c_done, b + 1)
                    v.tensor_reduce(amax[:, b:b + 1], x3T[:, :, b * S:(b + 1) * S], mybir.AxisListType.XY, ALU.max,
                                    apply_absolute_value=True).then_inc(max_done, 1)

            @blk.tensor
            def _(pe):
                def t2(b):
                    pe.wait_ge(rows_used, b + 1)
                    if b:
                        pe.wait_ge(t2c_done, b)
                    for t in range(TB):
                        for k in range(KD):
                            last = nc.tensor.transpose(pT2[:, k * S + t * P:k * S + (t + 1) * P],
                                                       X[:, b * TB + t, k * P:(k + 1) * P], ident[:, :])
                    last.then_inc(t2_done, 1)

                def m1(b):
                    pe.wait_ge(t2c_done, b + 1)
                    if b:
                        pe.wait_ge(relu_done, b)
                    for k in range(KD):
                        last = nc.tensor.matmul(pA[0:A, 0:S], aW1[:, b, k, :], x2T[:, k, :], start=(k == 0), stop=(k == KD - 1))
                    last.then_inc(m1_done, 1)

                def m2(b):
                    pe.wait_ge(relu_done, b + 1)
                    if b:
                        pe.wait_ge(pre_done, b)
                    for t in range(TB):
                        last = nc.tensor.matmul(pD[:, t, 0:D], aH[:, t * P:(t + 1) * P], aW2[:, b, :], start=True, stop=True)
                    last.then_inc(m2_done, 1)
                pe.wait_ge(one_row, 1)
                spread_max(pe, wmax, wdiag, pW, 2, wt_ready, wt_done, wd_ready, wd_done, 1)
                t2(0)
                for b in range(NB):
                    if b + 1 < NB:
                        t2(b + 1)
                    if b:
                        m2(b - 1)
                    m1(b)
                m2(NB - 1)
                for b in range(NB):
                    pe.wait_ge(x3_done, b + 1)
                    if b:
                        pe.wait_ge(t3c_done, b)
                    for t in range(TB):
                        for k in range(KD):
                            last = nc.tensor.transpose(pT3[:, k * S + t * P:k * S + (t + 1) * P],
                                                       X3[:, b * TB + t, k * P:(k + 1) * P], ident[:, :])
                    last.then_inc(t3_done, 1)

        if stop == "C":
            return
        NCH = 4
        CH = TOK // NCH
        d_link, xt_rdy, xt_dn, xd_rdy, xd_dn = (sem(n) for n in ("d_link", "xt_rdy", "xt_dn", "xd_rdy", "xd_dn"))
        s1_done, r1_done, q1_done, mm1_done, g_done, gmax_done = (sem(n) for n in (
            "s1_done", "r1_done", "q1_done", "mm1_done", "g_done", "gmax_done"))
        ht_rdy, ht_dn, hd_rdy, hd_dn, s2_done, b2_done, z_done, rh_done, qh_act, qh_dve, acc_done, o_done, out_stored = (
            sem(n) for n in ("ht_rdy", "ht_dn", "hd_rdy", "hd_dn", "s2_done", "b2_done", "z_done", "rh_done",
                             "qh_act", "qh_dve", "acc_done", "o_done", "out_stored"))
        act_chunks = [1, 3, 5]
        acc = [halves[t // 8][:, (t % 8) // 2, (t % 2) * D:(t % 2 + 1) * D] for t in range(NT)]
        ob = [gelu_g[:, :, :], hid[:, :, :]]

        with nc.Block() as blk:
            @blk.sync
            def _(sp):
                o_rows = out.rearrange("b (t p) d -> p b t d", p=P)
                for b in range(NB):
                    sp.wait_ge(o_done, b + 1)
                    sp.dma_start(o_rows[:, b], X3[:, b * TB:(b + 1) * TB, :]).then_inc(out_stored, 16)
                sp.wait_ge(out_stored, 16 * NB)

            @blk.gpsimd
            def _(pool):
                pool.wait_ge(b2_done, 1)
                for b in range(NB):
                    xb = X[:, b * TB:(b + 1) * TB, :]
                    nc.gpsimd.tensor_tensor(xb, xb, b2s.unsqueeze(1).to_broadcast([P, TB, D]), ALU.add).then_inc(z_done, 1)

            @blk.scalar
            def _(act):
                for c in range(NCH):
                    act.wait_ge(r1_done, c + 1)
                    nc.scalar.activation(x3q[:, :, c * CH:(c + 1) * CH], x3T[:, :, c * CH:(c + 1) * CH], ACT.Copy,
                                         bias=-MAGIC).then_inc(q1_done, 1)
                act.wait_ge(s1_done, 1)
                for f in range(FC):
                    act.wait_ge(mm1_done, f + 1)
                    nc.scalar.activation(h_all[:, f, :], halves[f % 2][:, :, :].rearrange("p b n -> p (b n)"), ACT.Gelu,
                                         bias=b1s[:, f:f + 1], scale=s1).then_inc(g_done, 1)
                for n, f in enumerate(act_chunks):
                    act.wait_ge(rh_done, f + 1)
                    nc.scalar.activation(hq[:, f, :], h_all[:, f, :], ACT.Copy, bias=-MAGIC).then_inc(qh_act, 1)

            @blk.vector
            def _(dve):
                v = nc.vector
                lk = linker(dve, d_link)
                v.tensor_reduce(xmax, amax[:, 0:NB], AX, ALU.max).then_inc(xt_rdy, 1)
                scale_chain(lk, v, dve, xmax, xtop[0:1], xdiag[0:1], xall, xstep, xinv, pR, 1, xt_rdy, xt_dn, xd_rdy, xd_dn, 1)
                for c in range(NCH):
                    xc = x3T[:, :, c * CH:(c + 1) * CH]
                    v.tensor_scalar(xc, xc, xinv, MAGIC, ALU.mult, ALU.add).then_inc(r1_done, 1)
                lk(v.tensor_tensor(s1, xstep, wstep[:, 0:1], ALU.mult))
                v.tensor_scalar(b1s, b1_sb, s1, None, ALU.mult).then_inc(s1_done, 1)
                for f in range(FC):
                    dve.wait_ge(g_done, f + 1)
                    lk(v.tensor_reduce(amax[:, NB + f:NB + f + 1], h_all[:, f, :], AX, ALU.max, apply_absolute_value=True))
                v.tensor_reduce(hmax, amax[:, NB:NB + FC], AX, ALU.max).then_inc(ht_rdy, 1)
                scale_chain(lk, v, dve, hmax, htop[0:1], hdiag[0:1], hall, hstep, hinv, pR, 1, ht_rdy, ht_dn, hd_rdy, hd_dn, 1)

                def to_grid(f):
                    v.tensor_scalar(h_all[:, f, :], h_all[:, f, :], hinv, MAGIC, ALU.mult, ALU.add).then_inc(rh_done, 1)
                to_grid(0)
                lk(v.tensor_tensor(s2, hstep, wstep[:, 1:2], ALU.mult))
                v.tensor_scalar(b2s, b2_sb, s2, None, ALU.mult).then_inc(b2_done, 1)
                for f in range(FC):
                    if f + 1 < FC:
                        to_grid(f + 1)
                    if f not in act_chunks:
                        dve.wait_ge(rh_done, f + 1)
                        v.tensor_scalar(hq[:, f, :], h_all[:, f, :], MAGIC, None, ALU.subtract).then_inc(qh_dve, 1)
                for b in range(NB):
                    dve.wait_ge(acc_done, b + 1)
                    dve.wait_ge(z_done, b + 1)
                    bank = halves[b // 4][:, b % 4, :].rearrange("p (t d) -> p t d", t=TB)
                    v.scalar_tensor_tensor(X3[:, b * TB:(b + 1) * TB, :], bank, s2, X[:, b * TB:(b + 1) * TB, :],
                                           ALU.mult, ALU.add).then_inc(o_done, 1)

            @blk.tensor
            def _(pe):
                spread_max(pe, xmax, xdiag[0:1], pR, 1, xt_rdy, xt_dn, xd_rdy, xd_dn, 1)
                for f in range(FC):
                    if f >= 2:
                        pe.wait_ge(g_done, f - 1)
                    for c in range(NCH):
                        if f == 0:
                            pe.wait_ge(q1_done, c + 1)
                        if f == 1 and c == 0:
                            pe.wait_ge(d_link, 3)
                        for k in range(KD):
                            last = nc.tensor.matmul(halves[f % 2][:, c, :], w1q[:, k, f * P:(f + 1) * P],
                                                    x3q[:, k, c * CH:(c + 1) * CH], start=(k == 0), stop=(k == KD - 1))
                    last.then_inc(mm1_done, 1)
                pe.wait_ge(g_done, FC)
                spread_max(pe, hmax, hdiag[0:1], pR, 1, ht_rdy, ht_dn, hd_rdy, hd_dn, 1)
                for f in range(FC):
                    if f in act_chunks:
                        pe.wait_ge(qh_act, act_chunks.index(f) + 1)
                    else:
                        pe.wait_ge(qh_dve, f + 1 - sum(a < f for a in act_chunks))
                    for t in range(NT):
                        last = nc.tensor.matmul(acc[t], hq[:, f, t * P:(t + 1) * P], w2q[f // 4][:, f % 4, :],
                                                start=(f == 0 and t % 2 == 0), stop=(f == FC - 1 and t % 2 == 1),
                                                skip_group_check=True)
                        if f == FC - 1 and t % 2 == 1:
                            last.then_inc(acc_done, 1)


def kernel(**inputs):
    import concourse.bacc as bacc
    from concourse.bass_utils import run_bass_kernel_spmd

    def host(name):
        return np.asarray(inputs[name])

    def swap(name):
        return np.ascontiguousarray(np.swapaxes(host(name), -1, -2))

    arrays = {
        "x": host("x"), "xT": swap("x"), "itokA": host("itok_B_0_2"), "itokC": host("itok_B_0_8"),
        "Wi0": host("L0_cond_Wi0"), "Wi1": host("L0_cond_Wi1"), "Wo": host("L0_cond_Wo"),
        "sWi0": host("L0_cond_sWi0"), "sWi1": host("L0_cond_sWi1"), "sWo": host("L0_cond_sWo"),
        "g0": host("L0_cond_g0"), "g1T": swap("L0_cond_g1"),
        "gamma0": host("L0_ffn_ln_gamma"), "beta0": host("L0_ffn_ln_beta"), "routerT": swap("L0_ffn_router_w"),
        "guT": swap("L0_ffn_gate_up_w"), "dnT": swap("L0_ffn_down_w"),
        "cW1": host("L1_cond_W1"), "cb1T": host("L1_cond_b1")[:, :, None],
        "cW2": host("L1_cond_W2"), "cb2": host("L1_cond_b2"),
        "cgamma": host("L1_cond_gamma"), "cbeta": host("L1_cond_beta"),
        "w1T": swap("L1_ffn_w1"), "b1T": np.ascontiguousarray(host("L1_ffn_b1").reshape(-1, P).T),
        "w2T": swap("L1_ffn_w2"), "b2": host("L1_ffn_b2"),
    }
    arrays = {"in_" + k: np.ascontiguousarray(v) for k, v in arrays.items()}
    nc = bacc.Bacc("TRN2", target_bir_lowering=False, num_devices=1)
    args = [nc.dram_tensor(k, v.shape, mybir.dt.from_np(v.dtype), kind="ExternalInput").ap()
            for k, v in arrays.items()]
    out = nc.dram_tensor("out_0", host("x").shape, F32, kind="ExternalOutput").ap()
    build(nc, *args, out)
    return run_bass_kernel_spmd(nc, [arrays], core_ids=[0]).results[0]["out_0"]
```

```python
from contextlib import ExitStack

import numpy as np

import concourse.bass as bass
from concourse import mybir

P = 128
F32, F16, BF16, I32 = mybir.dt.float32, mybir.dt.float16, mybir.dt.bfloat16, mybir.dt.int32
ALU = mybir.AluOpType
ACT = mybir.ActivationFunctionType
AX = mybir.AxisListType.X

SX, SW = 16.0, 1024.0
SH = 256.0
SN, SE, SHE = 8.0, 256.0, 64.0
MAGIC = 1.5 * 2.0 ** 23


def hold(eng, reg, sem, value, met):
    if isinstance(value, int):
        eng.wait_ge(sem, value)
        return
    eng.reg_mov(reg, value)
    eng.wait_ge(*met)
    eng.wait_ge(sem, reg)


def linker(eng, sem, base=0):
    n = [0]

    def link(ins, reg=None, met=None):
        n[0] += 1
        ins.then_inc(sem, 1)
        if reg is None:
            eng.wait_ge(sem, base + n[0])
        else:
            hold(eng, reg, sem, base + n[0], met)
    link.n = n
    return link


def build(nc, x, xT, itokA, itokC, Wi0, Wi1, Wo, sWi0, sWi1, sWo, g0, g1T, gamma0, beta0, routerT, guT, dnT,
          cW1, cb1T, cW2, cb2, cgammaT, cbetaT, w1T, b1T, w2T, b2, out):
    NB, S, D = x.shape
    TOK = NB * S
    NT = TOK // P
    TB = S // P
    KD = D // P
    NEA, _, F = Wi0.shape
    FC = F // P
    PAIRS = FC // 2
    NP = 2 * PAIRS
    E, _, F2 = guT.shape
    FE = F2 // 2
    KE = FE // P
    NL, _, A = cW1.shape
    TOPK = 2
    NBLK = (TOPK * TOK + E * (P - 1)) // P
    UNR = 3
    assert (D, F, S, FE, NBLK % UNR) == (256, 1024, 256, 512, 0)

    xn_dram = nc.dram_tensor("xn_rows", [TOK, D], F32).ap()
    res_dram = nc.dram_tensor("residual_rows", [TOK, D], F32).ap()
    moe_dram = nc.dram_tensor("moe_rows", [TOPK * TOK + NBLK * P, D], F32).ap()

    with ExitStack() as ctx:
        def sb(name, shape, dt=F32):
            return ctx.enter_context(nc.sbuf_tensor(name, shape, dt))

        def pb(name, shape):
            return ctx.enter_context(nc.psum_tensor(name, shape, F32))

        def sem(name):
            return ctx.enter_context(nc.semaphore(name))

        xb_sb = sb("xb_sb", [P, TB, D])
        xt_area = sb("xt_area", [P, 2 * KD * TOK], F16)
        moe_area = sb("moe_area", [P, 2 * (KD * E * F2 + KE * E * D)], F16)
        ffn_area = sb("ffn_area", [P, 4 * (KD * F * 2 + FC * D) // 1], F16)
        stage = sb("stage", [P, 2, KD * F])
        gelu_g = sb("gelu_g", [P, 2, S])
        hid = sb("hid", [P, 2, S])
        hid_hl = sb("hid_hl", [P, 2, 2, 2, S], F16)
        S_out = sb("S_out", [P, TB, D])
        E_out = sb("E_out", [P, TB, D])
        XN = sb("XN", [P, TB, D])
        xnT = sb("xnT", [P, KD, S])
        gam = sb("gam", [P, D])
        bet = sb("bet", [P, D])
        g0_sb = sb("g0_sb", [P, 2 * KD, D])
        rw_sb = sb("rw_sb", [P, KD, E])
        LG = sb("LG", [P, NT, E])
        ident = sb("ident", [P, P])
        upper = sb("upper", [P, P])
        ones = sb("ones", [P, P])
        iota_row = sb("iota_row", [P, P])
        iota_p = sb("iota_p", [P, 1])
        rev_e = sb("rev_e", [P, E])
        itA = sb("itA", [1, NB], I32)
        itC = sb("itC", [1, NB], I32)
        row = sb("row", [1, 3 * D])
        g1_row, junk_row = row[0:1, 0:2 * D].rearrange("p (j d) -> p j d", j=2), row[0:1, 2 * D:3 * D]
        tiny = sb("tiny", [P, 64])
        gT = tiny[:, 0:4]
        logit2, mx1, dl2, ex2 = tiny[0:1, 4:6], tiny[0:1, 6:7], tiny[0:1, 8:10], tiny[0:1, 10:12]
        sm1, rs1, w2row, ebase = tiny[0:1, 12:13], tiny[0:1, 13:14], tiny[0:1, 14:16], tiny[0:1, 16:18]
        wbc, rstd, vpe = tiny[:, 18:20], tiny[:, 20:22], tiny[:, 22:24]
        mhalf, eps2 = tiny[:, 24:26], tiny[:, 42:44]
        mv = tiny[:, 26:30].rearrange("p (t s) -> p t s", t=2)
        bst = tiny[:, 30:42].rearrange("p (t s) -> p t s", t=2)

        XTh = xt_area[:, 0:KD * TOK].rearrange("p (k n) -> p k n", k=KD)
        XTl = xt_area[:, KD * TOK:].rearrange("p (k n) -> p k n", k=KD)
        ng, nd = KD * E * F2, KE * E * D
        GUh = moe_area[:, 0:ng].rearrange("p (k e f) -> p k e f", k=KD, e=E)
        GUl = moe_area[:, ng:2 * ng].rearrange("p (k e f) -> p k e f", k=KD, e=E)
        DNh = moe_area[:, 2 * ng:2 * ng + nd].rearrange("p (k e d) -> p k e d", k=KE, e=E)
        DNl = moe_area[:, 2 * ng + nd:].rearrange("p (k e d) -> p k e d", k=KE, e=E)
        nw = KD * F

        def ffn_w(s, j):
            v = ffn_area[:, (6 * s + j) * nw:(6 * s + j + 1) * nw]
            return v.rearrange("p (k f) -> p k f", k=KD) if j < 4 else v.rearrange("p (c d) -> p c d", c=FC)

        early = moe_area[:, ng:].bitcast(F32)
        xT_in = early[:, 0:KD * TOK].rearrange("p (u k n) -> p u k n", u=4, k=KD)
        sW_in = early[:, KD * TOK:KD * TOK + 3 * nw].rearrange("p (j v) -> p j v", j=3)

        halves = [pb(f"psum_half{i}", [P, 4, 512]) for i in range(2)]
        pG = [halves[0][:, i, :] for i in range(2)]
        pL = [halves[0][:, 2 + i, :] for i in range(2)]
        pD = halves[1][:, 0:2, :]
        pM, pR = halves[1][:, 2, :], halves[1][:, 3, :]

        x_in = [sem(f"x_in{u}") for u in range(4)]
        w_in = [sem(f"w_in{u}") for u in range(6)]
        small_in, ids_in = sem("small_in"), sem("ids_in")
        xb_in, gate_in, res_stored = sem("xb_in"), sem("gate_in"), sem("res_stored")
        buf_in = [sem("buf0_in"), sem("buf1_in")]
        conv_hi, conv_lo, early_hi, early_lo = (sem(n) for n in ("conv_hi", "conv_lo", "early_hi", "early_lo"))
        up_done, dn_done = sem("up_done"), sem("dn_done")
        gelu_done, h_done, hh_done, hl_done = sem("gelu_done"), sem("h_done"), sem("hh_done"), sem("hl_done")
        ev_done = sem("ev_done")
        gt_done, hg_done, wb_done, xnt_done, log_done = (sem(n) for n in (
            "gt_done", "hg_done", "wb_done", "xnt_done", "log_done"))
        gTc_done, dlt_done, w_done, y_done, bn_done, nrm_done, xnTc_done, lg_done = (sem(n) for n in (
            "gTc_done", "dlt_done", "w_done", "y_done", "bn_done", "nrm_done", "xnTc_done", "lg_done"))
        ex_done, res_done, rstd_done, xn_ready, xn_stored = (sem(n) for n in (
            "ex_done", "res_done", "rstd_done", "xn_ready", "xn_stored"))
        consts, dve_link, pool_link = sem("consts"), sem("dve_link"), sem("pool_link")

        LAG = 2
        NCONV = 9
        PIECES = [[0, 1], [2], [3], [4], [5], [6], [7], [8]]
        PIECES_0 = [[], [0, 1], [2, 3], [4], [5], [], [6, 7], [8]]
        EARLY = ["x0", "w0", "w2", "w1", "w3", "w4", "w5", "x1", "x2", "x3"]
        PRO = 3
        EARLY_OF = [[3, 4], [5], [6], [7], [8], [9], [], []]
        DVE_LINKS, POOL_LINKS = 8 + 2, 2

        def conv_piece(u, i):
            half = FC // 2
            if u < 4:
                j, h = 1 - u // 2, u % 2
                src = stage[:, j, :].rearrange("p (k f) -> p k f", k=KD)[:, :, h * 512:h * 512 + 512]
                hi, lo = (ffn_w(1, 2 * j + q)[:, :, h * 512:h * 512 + 512] for q in range(2))
                return src, hi, lo, SW, j, (3 * i + 1 if j == 0 else 2 * i + 1)
            if u < 6:
                h = u - 4
                src = stage[:, 0, :].rearrange("p (c d) -> p c d", c=FC)[:, h * half:(h + 1) * half, :]
                hi, lo = (ffn_w(1, 4 + q)[:, h * half:(h + 1) * half, :] for q in range(2))
                return src, hi, lo, SW, 0, 3 * i + 2
            if u < 8:
                h = u - 6
                src = stage[:, 1, :].rearrange("p (k f) -> p k f", k=KD)[:, :, h * 512:h * 512 + 512]
                hi, lo = (w[:, :, bass.ds(i, 1), h * 512:h * 512 + 512] for w in (GUh, GUl))
                return src, hi, lo, SE, 1, 2 * i + 2
            src = stage[:, 0, 0:KE * D].rearrange("p (k d) -> p k d", k=KE)
            hi, lo = (w[:, :, bass.ds(i, 1), :] for w in (DNh, DNl))
            return src, hi, lo, SE, 0, 3 * i + 3

        def early_piece(n):
            kind, u = EARLY[n][0], int(EARLY[n][1])
            if kind == "x":
                tok = slice(u * 512, u * 512 + 512)
                return xT_in[:, u], XTh[:, :, tok], XTl[:, :, tok], SX, x_in[u]
            j, h = u // 2, u % 2
            if j < 2:
                src = sW_in[:, j, :].rearrange("p (k f) -> p k f", k=KD)[:, :, h * 512:h * 512 + 512]
                hi, lo = (ffn_w(0, 2 * j + q)[:, :, h * 512:h * 512 + 512] for q in range(2))
            else:
                src = sW_in[:, j, :].rearrange("p (c d) -> p c d", c=FC)[:, h * 4:h * 4 + 4, :]
                hi, lo = (ffn_w(0, 4 + q)[:, h * 4:h * 4 + 4, :] for q in range(2))
            return src, hi, lo, SW, w_in[u]

        def flat3(ap):
            return ap.rearrange("p k e f -> p k (e f)") if len(ap.shape) == 4 else ap

        with nc.Block() as blk:
            @blk.sync
            def _(sp):
                sp.dma_start(itA[0:1, :], itokA.rearrange("(a n) -> a n", a=1)).then_inc(ids_in, 16)
                sp.dma_start(itC[0:1, :], itokC.rearrange("(a n) -> a n", a=1)).then_inc(ids_in, 16)
                def w_of(w, e):
                    return w[bass.ds(e, 1), :, :]

                def in_k(buf):
                    return stage[:, buf, :].rearrange("p (k f) -> p k f", k=KD)

                def expert_of(i):
                    return sp.value_load(itA[0:1, bass.ds(i, 1)], min_val=0, max_val=NEA - 1)

                def wi_in(i):
                    e = expert_of(i)
                    if not (isinstance(i, int) and i == 0):
                        sp.wait_ge(conv_lo, i * NCONV - 1)
                    sp.dma_start(in_k(1), w_of(Wi1, e).rearrange("e (k p) f -> p (e k) f", p=P)).then_inc(buf_in[1], 16)
                    if not (isinstance(i, int) and i == 0):
                        sp.wait_ge(conv_lo, i * NCONV)
                    sp.dma_start(in_k(0), w_of(Wi0, e).rearrange("e (k p) f -> p (e k) f", p=P)).then_inc(buf_in[0], 16)

                def more_in(i):
                    e = expert_of(i)
                    sp.wait_ge(conv_lo, i * NCONV + 2)
                    sp.dma_start(in_k(1), guT[bass.ds(i, 1), :, :].rearrange("e (k p) f -> p (e k) f", p=P)
                                 ).then_inc(buf_in[1], 16)
                    sp.wait_ge(conv_lo, i * NCONV + 4)
                    sp.dma_start(stage[:, 0, :].rearrange("p (c d) -> p c d", c=FC),
                                 w_of(Wo, e).rearrange("e (c p) d -> p (e c) d", p=P)).then_inc(buf_in[0], 16)

                xT_v = xT.rearrange("(u v) (k p) s -> u p k v s", u=4, p=P)
                for n in range(len(EARLY)):
                    if n == 7:
                        sp.wait_ge(ids_in, 32)
                        wi_in(0)
                    kind, u = EARLY[n][0], int(EARLY[n][1])
                    if kind == "x":
                        for k in range(KD):
                            sp.dma_start(xT_in[:, u, k].rearrange("p (v s) -> p v s", v=2),
                                         xT_v[u, :, k]).then_inc(x_in[u], 16)
                    else:
                        j, h = u // 2, u % 2
                        if j < 2:
                            w = (sWi0, sWi1)[j].rearrange("(k p) f -> p k f", p=P)[:, :, h * 512:h * 512 + 512]
                            dst = sW_in[:, j, :].rearrange("p (k f) -> p k f", k=KD)[:, :, h * 512:h * 512 + 512]
                        else:
                            w = sWo.rearrange("(c p) d -> p c d", p=P)[:, h * 4:h * 4 + 4, :]
                            dst = sW_in[:, j, :].rearrange("p (c d) -> p c d", c=FC)[:, h * 4:h * 4 + 4, :]
                        sp.dma_start(dst, w).then_inc(w_in[u], 16)
                sp.dma_start(g0_sb[:, :, :], g0.rearrange("(c p) d -> p c d", p=P)).then_inc(gate_in, 16)
                sp.dma_start(g1_row, g1T.rearrange("(a j) d -> a j d", a=1)).then_inc(gate_in, 16)
                sp.dma_start(rw_sb[:, :, :], routerT.rearrange("(k p) e -> p k e", p=P)).then_inc(gate_in, 16)
                sp.dma_start(gam[:, :], gamma0.partition_broadcast(P)).then_inc(small_in, 16)
                sp.dma_start(bet[:, :], beta0.partition_broadcast(P)).then_inc(small_in, 16)

                def load_down(i):
                    sp.wait_ge(conv_lo, i * NCONV + 6)
                    sp.dma_start(stage[:, 0, 0:KE * D].rearrange("p (k d) -> p k d", k=KE),
                                 dnT[bass.ds(i, 1), :, :].rearrange("e (k p) d -> p (e k) d", p=P)).then_inc(buf_in[0], 16)

                def load_residual(g, first=False):
                    if not first:
                        sp.wait_ge(res_stored, g * 16)
                        sp.wait_ge(xn_stored, g * 16)
                    sp.dma_start(xb_sb[:, :, :], x.rearrange("b (t p) d -> p b t d", p=P)[:, bass.ds(g, 1)]
                                 ).then_inc(xb_in, 16)

                def store_xn(g):
                    sp.wait_ge(res_done, g + 1)
                    sp.dma_start(res_dram.rearrange("(b t p) d -> p b t d", t=TB, p=P)[:, bass.ds(g, 1)],
                                 xb_sb[:, :, :]).then_inc(res_stored, 16)
                    sp.wait_ge(xn_ready, g + 1)
                    sp.dma_start(xn_dram.rearrange("(b t p) d -> p b t d", t=TB, p=P)[:, bass.ds(g, 1)],
                                 XN[:, :, :]).then_inc(xn_stored, 16)
                load_residual(0, first=True)
                more_in(0)
                load_down(0)
                wi_in(1)
                more_in(1)
                load_down(1)
                with sp.Fori(2, NB) as i:
                    wi_in(i)
                    more_in(i)
                    store_xn(i - 2)
                    load_residual(i - 1)
                    load_down(i)
                store_xn(NB - 2)
                load_residual(NB - 1)
                store_xn(NB - 1)
                sp.wait_ge(xn_stored, 16 * NB)
                sp.wait_ge(res_stored, 16 * NB)

            @blk.gpsimd
            def _(pool):
                link = linker(pool, consts)
                link(nc.gpsimd.memset(ident[:, :], 0.0))
                link(nc.gpsimd.memset(ones[:, :], 1.0))
                link(nc.gpsimd.memset(tiny[:, 16:26], -0.5))
                link(nc.gpsimd.memset(ebase, float(np.e)))
                link(nc.gpsimd.memset(eps2, 1e-5))
                link(nc.gpsimd.affine_select(out=ident[:, :], in_=ident[:, :], compare_op=ALU.not_equal, fill=1.0,
                                             base=0, pattern=[[-1, P]], channel_multiplier=1))
                link(nc.gpsimd.affine_select(out=upper[:, :], in_=ones[:, :], compare_op=ALU.is_gt, fill=0.0,
                                             base=0, pattern=[[1, P]], channel_multiplier=-1))
                link(nc.gpsimd.iota(iota_row[:, :], pattern=[[1, P]], base=0, channel_multiplier=0,
                                    allow_small_or_imprecise_dtypes=True))
                link(nc.gpsimd.iota(iota_p[:, :], pattern=[[1, 1]], base=0, channel_multiplier=1,
                                    allow_small_or_imprecise_dtypes=True))
                link(nc.gpsimd.iota(rev_e[:, :], pattern=[[-1, E]], base=E, channel_multiplier=0,
                                    allow_small_or_imprecise_dtypes=True))
                assert link.n[0] == 10
                pool.wait_ge(small_in, 32)

                def gate(g):
                    lk = linker(pool, pool_link, g * POOL_LINKS)
                    pool.wait_ge(dlt_done, g + 1)
                    nc.gpsimd.tensor_tensor(ex2, ebase, dl2, ALU.pow).then_inc(ex_done, 1)
                    pool.wait_ge(y_done, g + 1)
                    pool.wait_ge(xb_in, g * 16 + 16)
                    xb = xb_sb[:, :, :]
                    nc.gpsimd.tensor_tensor(xb, xb, XN[:, :, :], ALU.add).then_inc(res_done, 1)
                    pool.wait_ge(bn_done, g + 1)
                    lk(nc.gpsimd.tensor_tensor(vpe, mv[:, :, 1], eps2, ALU.add))
                    nc.gpsimd.tensor_tensor(rstd, vpe, mhalf, ALU.pow).then_inc(rstd_done, 1)
                    pool.wait_ge(nrm_done, g + 1)
                    gb = gam[:, :].unsqueeze(1).to_broadcast([P, TB, D])
                    bb = bet[:, :].unsqueeze(1).to_broadcast([P, TB, D])
                    lk(nc.gpsimd.tensor_tensor(XN[:, :, :], XN[:, :, :], gb, ALU.mult))
                    nc.gpsimd.tensor_tensor(XN[:, :, :], XN[:, :, :], bb, ALU.add).then_inc(xn_ready, 1)
                    assert lk.n[0] == POOL_LINKS
                gate(0)
                with pool.Fori(1, NB) as g:
                    gate(g)

            @blk.scalar
            def _(act):
                def early(n):
                    src, hi, lo, scale, arrived = early_piece(n)
                    act.wait_ge(arrived, 32 if arrived in x_in else 16)
                    nc.scalar.activation(hi, src, ACT.Copy, scale=scale).then_inc(early_hi, 1)

                def iteration(i):
                    first = isinstance(i, int) and i == 0
                    for p in range(NP):
                        n = i * NP + p
                        q = p % 2
                        act.wait_ge(up_done, n + 1)
                        if not (first and p == 0):
                            act.wait_ge(h_done, n)
                        nc.scalar.activation(gelu_g[:, :, :], pG[q][:, :].rearrange("p (c s) -> p c s", c=2),
                                             ACT.Gelu_apprx_tanh, scale=1.0 / (SX * SW)).then_inc(gelu_done, 1)
                        for m in EARLY_OF[p] if first else []:
                            early(m)
                        for u in (PIECES_0 if first else PIECES)[p]:
                            src, hi, lo, scale, b, loads = conv_piece(u, i)
                            act.wait_ge(buf_in[b], loads * 16)
                            if u == 0 and not first:
                                act.wait_ge(up_done, i * NP)
                            if u == 4 and not first:
                                act.wait_ge(dn_done, i * NP)
                            if u == 6 and first:
                                act.wait_ge(early_lo, len(EARLY))
                            nc.scalar.activation(hi, src, ACT.Copy, scale=scale).then_inc(conv_hi, 1)
                        act.wait_ge(h_done, n + 1)
                        if not (first and p < 2):
                            act.wait_ge(dn_done, n - 1)
                        nc.scalar.activation(hid_hl[:, q, 0], hid[:, :, :], ACT.Copy).then_inc(hh_done, 1)
                act.wait_ge(consts, 2)
                nc.scalar.activation(tiny[:, 52:53], ones[:, 0:1], ACT.Gelu_apprx_tanh)
                for n in range(PRO):
                    early(n)
                iteration(0)
                with act.Fori(1, NB) as i:
                    iteration(i)

            @blk.vector
            def _(dve):
                held = dve.alloc_register("held_dve")
                def early(n):
                    src, hi, lo, scale, arrived = early_piece(n)
                    dve.wait_ge(early_hi, n + 1)
                    nc.vector.scalar_tensor_tensor(lo, src, scale, hi, ALU.mult, ALU.subtract).then_inc(early_lo, 1)
                for n in range(PRO):
                    early(n)

                def evac(dst, count):
                    dve.wait_ge(dn_done, count)
                    nc.vector.tensor_scalar(dst[:, :, :], pD[:, :, 0:D], 1.0 / (SH * SW), None,
                                            ALU.mult).then_inc(ev_done, 1)

                def gate(slot, g, lk):
                    if slot == 1:
                        dve.wait_ge(gt_done, g + 1)
                        nc.vector.tensor_copy(gT, pR[:, 0:4]).then_inc(gTc_done, 1)
                    if slot == 2:
                        dve.wait_ge(hg_done, g + 1)
                        for j in range(2):
                            lk(nc.vector.scalar_tensor_tensor(junk_row, pR[0:1, 0:D], 0.0, g1_row[:, j, :],
                                                              ALU.max, ALU.mult, accum_out=logit2[:, j:j + 1]))
                        lk(nc.vector.tensor_reduce(mx1, logit2, AX, ALU.max))
                        nc.vector.tensor_scalar(dl2, logit2, mx1, None, ALU.subtract).then_inc(dlt_done, 1)
                    if slot == 3:
                        dve.wait_ge(ex_done, g + 1)
                        lk(nc.vector.tensor_reduce(sm1, ex2, AX, ALU.add))
                        lk(nc.vector.reciprocal(rs1, sm1))
                        nc.vector.tensor_scalar(w2row, ex2, rs1, None, ALU.mult).then_inc(w_done, 1)
                    if slot == 4:
                        dve.wait_ge(wb_done, g + 1)
                        lk(nc.vector.tensor_copy(wbc, pR[:, 0:2]))
                        lk(nc.vector.tensor_scalar(S_out[:, :, :], S_out[:, :, :], wbc[:, 1:2], None, ALU.mult))
                        dve.wait_ge(xb_in, g * 16 + 16)
                        nc.vector.scalar_tensor_tensor(XN[:, :, :], E_out[:, :, :], wbc[:, 0:1], S_out[:, :, :],
                                                       ALU.mult, ALU.add).then_inc(y_done, 1)
                    if slot == 5:
                        dve.wait_ge(y_done, g + 1)
                        lk(nc.vector.bn_stats(bst[:, 0, :], XN[:, 0, :]))
                        lk(nc.vector.bn_stats(bst[:, 1, :], XN[:, 1, :]), held, (consts, 10))
                        lk(nc.vector.bn_aggr(mv[:, 0, :], bst[:, 0, :]), held, (consts, 10))
                        nc.vector.bn_aggr(mv[:, 1, :], bst[:, 1, :]).then_inc(bn_done, 1)
                    if slot == 6:
                        dve.wait_ge(rstd_done, g + 1)
                        dve.wait_ge(res_done, g + 1)
                        dve.wait_ge(bn_done, g + 1)
                        for t in range(TB):
                            r = nc.vector.tensor_scalar(XN[:, t, :], XN[:, t, :], mv[:, t, 0:1], rstd[:, t:t + 1],
                                                        ALU.subtract, ALU.mult)
                        r.then_inc(nrm_done, 1)
                    if slot == 7:
                        dve.wait_ge(xnt_done, g + 1)
                        nc.vector.tensor_copy(xnT[:, :, :], pM[:, :].rearrange("p (k s) -> p k s", k=KD)).then_inc(xnTc_done, 1)
                    if slot == 8:
                        dve.wait_ge(log_done, g + 1)
                        nc.vector.tensor_scalar(LG[:, bass.ds(g * TB, TB), :],
                                                pM[:, 0:TB * E].rearrange("p (t e) -> p t e", t=TB),
                                                1e4, -1e4, ALU.min, ALU.max).then_inc(lg_done, 1)

                def iteration(i):
                    first = isinstance(i, int) and i == 0
                    second = isinstance(i, int) and i == 1
                    lk = linker(dve, dve_link, (i - 1) * DVE_LINKS)
                    for p in range(NP):
                        n = i * NP + p
                        q = p % 2
                        if p == LAG and not first:
                            evac(E_out, i * NP)
                        dve.wait_ge(gelu_done, n + 1)
                        if not (first and p == 0):
                            dve.wait_ge(hl_done, n)
                        nc.vector.scalar_tensor_tensor(hid[:, :, :], pL[q][:, :].rearrange("p (c s) -> p c s", c=2),
                                                       SH / (SX * SW), gelu_g[:, :, :],
                                                       ALU.mult, ALU.mult).then_inc(h_done, 1)
                        if p == 5 and not first:
                            gate(4, i - 1, lk)

                        def split():
                            dve.wait_ge(hh_done, n + 1)
                            nc.vector.tensor_tensor(hid_hl[:, q, 1], hid[:, :, :], hid_hl[:, q, 0],
                                                    ALU.subtract).then_inc(hl_done, 1)
                        if p == PAIRS + 1:
                            split()
                            if not first:
                                dve.wait_ge(y_done, i)
                            evac(S_out, i * NP + PAIRS)
                        for m in EARLY_OF[p] if first else []:
                            early(m)
                        for u in (PIECES_0 if first else PIECES)[p]:
                            src, hi, lo, scale, b, loads = conv_piece(u, i)
                            dve.wait_ge(conv_hi, i * NCONV + u + 1)
                            nc.vector.scalar_tensor_tensor(flat3(lo), src, scale, flat3(hi),
                                                           ALU.mult, ALU.subtract).then_inc(conv_lo, 1)
                        if p != PAIRS + 1:
                            split()
                        if not first:
                            if p in SLOTS_OF_LAST:
                                gate(SLOTS_OF_LAST[p], i - 1, lk)
                            if p in SLOTS_BEFORE and not second:
                                gate(SLOTS_BEFORE[p], i - 2, lk)
                SLOTS_OF_LAST = {2: 1, 3: 2, 4: 3, 6: 5, 7: 6}
                SLOTS_BEFORE = {1: 7, 3: 8}
                iteration(0)
                dve.wait_ge(gate_in, 48)
                dve.wait_ge(consts, 10)
                iteration(1)
                with dve.Fori(2, NB) as i:
                    iteration(i)
                evac(E_out, NB * NP)
                lk = linker(dve, dve_link, (NB - 1) * DVE_LINKS)
                gate(1, NB - 1, lk)
                gate(7, NB - 2, lk)
                gate(2, NB - 1, lk)
                gate(8, NB - 2, lk)
                for slot in range(3, 9):
                    gate(slot, NB - 1, lk)

            @blk.tensor
            def _(pe):
                def up(i, p):
                    q, s = p % 2, p // PAIRS
                    n = i * NP + p
                    if not (isinstance(i, int) and i == 0 and p < 2):
                        pe.wait_ge(h_done, n - 1)
                    if p == PAIRS:
                        pe.wait_ge(conv_lo, i * NCONV + 4)
                    tok = bass.ds(i * S, S)
                    for c in range(2):
                        f = slice((2 * (p % PAIRS) + c) * P, (2 * (p % PAIRS) + c + 1) * P)
                        for bank, j in ((pG[q], 0), (pL[q], 2)):
                            o = bank[:, c * S:(c + 1) * S]
                            wh, wl = ffn_w(s, j), ffn_w(s, j + 1)
                            for k in range(KD):
                                nc.tensor.matmul(o, wh[:, k, f], XTh[:, k, tok], start=(k == 0), stop=False)
                                nc.tensor.matmul(o, wh[:, k, f], XTl[:, k, tok], start=False, stop=False)
                                last = nc.tensor.matmul(o, wl[:, k, f], XTh[:, k, tok], start=False,
                                                        stop=(k == KD - 1))
                    last.then_inc(up_done, 1)

                def down(i, p):
                    q, s = p % 2, p // PAIRS
                    n = i * NP + p
                    pe.wait_ge(hl_done, n + 1)
                    if p == 0 and not (isinstance(i, int) and i == 0):
                        pe.wait_ge(ev_done, i * 2)
                    if p == PAIRS:
                        pe.wait_ge(ev_done, i * 2 + 1)
                        pe.wait_ge(conv_lo, i * NCONV + 6)
                    woh, wol = ffn_w(s, 4), ffn_w(s, 5)
                    for t in range(TB):
                        ts = slice(t * P, (t + 1) * P)
                        for c in range(2):
                            f = 2 * (p % PAIRS) + c
                            hh, hl = hid_hl[:, q, 0, c, ts], hid_hl[:, q, 1, c, ts]
                            nc.tensor.matmul(pD[:, t, 0:D], hh, woh[:, f, :],
                                             start=(p % PAIRS == 0 and c == 0), stop=False)
                            nc.tensor.matmul(pD[:, t, 0:D], hh, wol[:, f, :], start=False, stop=False)
                            last = nc.tensor.matmul(pD[:, t, 0:D], hl, woh[:, f, :], start=False,
                                                    stop=(p % PAIRS == PAIRS - 1 and c == 1))
                    last.then_inc(dn_done, 1)

                def gate(step, g):
                    if step == "columns":
                        pe.wait_ge(ev_done, g * 2 + 2)
                        for c in range(2 * KD):
                            src = (E_out if c < KD else S_out)[0:1, 0, (c % KD) * P:(c % KD + 1) * P]
                            last = nc.tensor.matmul(pR[:, c:c + 1], src, ones[0:1, 0:1], start=True, stop=True)
                        last.then_inc(gt_done, 1)
                    if step == "hidden":
                        pe.wait_ge(gTc_done, g + 1)
                        for c in range(2 * KD):
                            last = nc.tensor.matmul(pR[0:1, 0:D], gT[:, c:c + 1], g0_sb[:, c, :],
                                                    start=(c == 0), stop=(c == 2 * KD - 1))
                        last.then_inc(hg_done, 1)
                    if step == "weights":
                        pe.wait_ge(w_done, g + 1)
                        nc.tensor.matmul(pR[:, 0:2], ones[0:1, :], w2row, start=True, stop=True).then_inc(wb_done, 1)
                    if step == "transpose":
                        pe.wait_ge(xn_ready, g + 1)
                        for t in range(TB):
                            for k in range(KD):
                                last = nc.tensor.transpose(pM[:, k * S + t * P:k * S + (t + 1) * P],
                                                           XN[:, t, k * P:(k + 1) * P], ident[:, :])
                        last.then_inc(xnt_done, 1)
                    if step == "logits":
                        pe.wait_ge(xnTc_done, g + 1)
                        for t in range(TB):
                            for k in range(KD):
                                last = nc.tensor.matmul(pM[:, t * E:(t + 1) * E], xnT[:, k, t * P:(t + 1) * P],
                                                        rw_sb[:, k, :], start=(k == 0), stop=(k == KD - 1))
                        last.then_inc(log_done, 1)

                def iteration(i):
                    first = isinstance(i, int) and i == 0
                    second = isinstance(i, int) and i == 1
                    for p in range(NP):
                        if first and p in (0, 2):
                            pe.wait_ge(early_lo, PRO + len(EARLY_OF[0]) * (p // 2))
                        up(i, p)
                        if p == 5 and not first:
                            gate("weights", i - 1)
                        if p >= LAG:
                            if first and p - LAG in (0, 2):
                                pe.wait_ge(early_lo, PRO + 3 + (p - LAG) // 2)
                            down(i, p - LAG)
                        elif not first:
                            down(i - 1, NP - LAG + p)
                        if not first:
                            if p in GATE_OF_LAST:
                                gate(GATE_OF_LAST[p], i - 1)
                            if p in GATE_BEFORE and not second:
                                gate(GATE_BEFORE[p], i - 2)
                GATE_OF_LAST = {2: "columns", 3: "hidden"}
                GATE_BEFORE = {1: "transpose", 3: "logits"}
                pe.wait_ge(consts, 10)
                iteration(0)
                pe.wait_ge(gate_in, 48)
                iteration(1)
                with pe.Fori(2, NB) as i:
                    iteration(i)
                for p in range(LAG):
                    down(NB - 1, NP - LAG + p)
                gate("columns", NB - 1)
                gate("transpose", NB - 2)
                gate("hidden", NB - 1)
                gate("logits", NB - 2)
                for step in ("weights", "transpose", "logits"):
                    gate(step, NB - 1)
        NA = TOPK * NT
        onehot_slot = xt_area[:, :].bitcast(F32).rearrange("p (a m) -> p a m", a=NA)
        blk_vals = ffn_area[:, 12 * nw // 2:12 * nw // 2 + 2 * NA * 3 * NBLK].bitcast(F32).rearrange(
            "p (a v j) -> p a v j", a=NA, v=3)
        work = stage[:, :, :].rearrange("p a b -> p (a b)")
        NTE = NT * E

        def tile_of(n, dt=F32):
            v = work[:, n * NTE:(n + 1) * NTE]
            return v if dt == F32 else v.bitcast(dt)

        def te(ap):
            return ap.rearrange("p (t e) -> p t e", e=E)

        d_t, ex_t, p_t, eq_t, oh = te(tile_of(0)), te(tile_of(1)), te(tile_of(2)), te(tile_of(3)), [
            te(tile_of(4)), te(tile_of(5))]
        M_t, cum, pos_t = te(tile_of(6)), [te(tile_of(7)), te(tile_of(8))], te(tile_of(9))
        tot_t = te(tile_of(10))
        sm = tile_of(11)
        m16, s16, r16 = sm[:, 0:NT], sm[:, NT:2 * NT], sm[:, 2 * NT:3 * NT]
        gate2 = sm[:, 64:64 + NA].rearrange("p (r t) -> p r t", r=TOPK)
        k16 = sm[:, 3 * NT:4 * NT]
        sn = tile_of(12)
        nb_f, nb_raw, start_f = sn[:, 0:E], sn[:, E:2 * E], sn[:, 2 * E:3 * E]
        bend = [sn[:, 3 * E:4 * E], sn[:, 4 * E:5 * E]]
        nb_i = tile_of(13, I32)[:, 0:E]
        POS = tile_of(14)[:, 0:NA]
        pos_i, blk_i, row_i = (tile_of(15, I32)[:, n * NA:(n + 1) * NA] for n in range(3))
        blk_f, row_f, dest_f = (tile_of(16)[:, n * NA:(n + 1) * NA] for n in range(3))
        tab = work[:, 17 * NTE:17 * NTE + 3 * NBLK].rearrange("p (v j) -> p v j", v=3)
        un_t = tile_of(18)[:, 0:NBLK]
        pad_row = tile_of(18)[:, 64:64 + NBLK]
        be_cmp = work[0:1, 19 * NTE:19 * NTE + NBLK * E].rearrange("p (j e) -> p j e", e=E)
        be_f = work[0:1, 22 * NTE:22 * NTE + NBLK]
        dest_i = xb_sb[:, 0, 0:NBLK].bitcast(I32)
        tok_i = xb_sb[:, 0, 64:64 + NBLK].bitcast(I32)
        gate_silu = xb_sb[:, 0, 128:128 + NBLK]
        gate_up_s = xb_sb[:, 0, 192:192 + NBLK]
        be_i = xb_sb[0:1, 1, 0:NBLK].bitcast(I32)
        tok_col = xb_sb[:, 1, 64:64 + UNR].bitcast(I32)
        dest_col = xb_sb[:, 1, 80:80 + UNR].bitcast(I32)

        shift_done, exp_done, mask_done, prefix_done, slots_done, vals_done, table_done, dest_ready = (
            sem(n) for n in ("shift_done", "exp_done", "mask_done", "prefix_done", "slots_done",
                             "vals_done", "table_done", "dest_ready"))
        route_link = sem("route_link")

        def over_e(ap):
            return ap.unsqueeze(2).to_broadcast([P, NT, E])

        def over_t(ap):
            return ap.unsqueeze(1).to_broadcast([P, NT, E])

        with nc.Block() as blk:
            @blk.gpsimd
            def _(pool):
                nc.gpsimd.iota(pad_row, pattern=[[P, NBLK]], base=TOPK * TOK, channel_multiplier=1,
                               allow_small_or_imprecise_dtypes=True).then_inc(dest_ready, 1)
                nc.gpsimd.iota(dest_f, pattern=[[TOK, TOPK], [P, NT]], base=0, channel_multiplier=1,
                               allow_small_or_imprecise_dtypes=True).then_inc(dest_ready, 1)

            @blk.scalar
            def _(act):
                act.wait_ge(shift_done, 1)
                nc.scalar.activation(ex_t, d_t, ACT.Exp).then_inc(exp_done, 1)
                nc.scalar.activation(tiny[:, 52:53], iota_p[:, :], ACT.Silu)

            @blk.vector
            def _(dve):
                lk = linker(dve, route_link)
                v = nc.vector
                lk(v.tensor_reduce(m16, LG[:, :, :], AX, ALU.max))
                v.tensor_tensor(d_t, LG[:, :, :], over_e(m16), ALU.subtract).then_inc(shift_done, 1)
                dve.wait_ge(exp_done, 1)
                lk(v.tensor_reduce(s16, ex_t, AX, ALU.add))
                lk(v.tensor_scalar(s16, s16, 1e-8, None, ALU.add))
                lk(v.reciprocal(r16, s16))
                lk(v.tensor_tensor(p_t, ex_t, over_e(r16), ALU.mult))
                lk(v.tensor_scalar(p_t, p_t, 1e-8, 1.0, ALU.max, ALU.min))
                for r in range(TOPK):
                    lk(v.tensor_reduce(gate2[:, r, :], p_t, AX, ALU.max))
                    lk(v.tensor_tensor(eq_t, p_t, over_e(gate2[:, r, :]), ALU.is_equal))
                    lk(v.tensor_tensor(eq_t, eq_t, over_t(rev_e[:, :]), ALU.mult))
                    lk(v.tensor_reduce(k16, eq_t, AX, ALU.max))
                    lk(v.tensor_tensor(oh[r], over_t(rev_e[:, :]), over_e(k16), ALU.is_equal))
                    if r == 0:
                        lk(v.scalar_tensor_tensor(p_t, oh[0], -4.0, p_t, ALU.mult, ALU.add))
                v.tensor_tensor(M_t, oh[0], oh[1], ALU.add).then_inc(mask_done, 1)
                dve.wait_ge(prefix_done, 1)
                lk(v.tensor_copy(tot_t, te(pL[0][:, 0:NTE])))
                lk(v.tensor_copy(cum[0], tot_t))
                b, sh = 0, 1
                while sh < NT:
                    lk(v.tensor_tensor(cum[1 - b][:, sh:, :], cum[b][:, sh:, :], cum[b][:, :NT - sh, :], ALU.add))
                    lk(v.tensor_copy(cum[1 - b][:, :sh, :], cum[b][:, :sh, :]))
                    b, sh = 1 - b, 2 * sh
                incl = cum[b]
                lk(v.tensor_scalar(nb_i, incl[:, NT - 1, :], float(P - 1), None, ALU.add))
                lk(v.tensor_scalar(nb_i, nb_i, 7, None, ALU.logical_shift_right))
                lk(v.tensor_copy(nb_f, nb_i))
                lk(v.tensor_copy(bend[0], nb_f))
                c, sh = 0, 1
                while sh < E:
                    lk(v.tensor_tensor(bend[1 - c][:, sh:], bend[c][:, sh:], bend[c][:, :E - sh], ALU.add))
                    lk(v.tensor_copy(bend[1 - c][:, :sh], bend[c][:, :sh]))
                    c, sh = 1 - c, 2 * sh
                lk(v.tensor_tensor(start_f, bend[c], nb_f, ALU.subtract))
                lk(v.tensor_scalar(start_f, start_f, float(P), None, ALU.mult))
                lk(v.tensor_tensor(pos_t, incl, tot_t, ALU.subtract))
                lk(v.tensor_tensor(pos_t, pos_t, te(pG[0][:, 0:NTE]), ALU.add))
                lk(v.tensor_tensor(pos_t, pos_t, over_t(start_f), ALU.add))
                for r in range(TOPK):
                    lk(v.tensor_tensor(eq_t, pos_t, oh[r], ALU.mult))
                    lk(v.tensor_reduce(POS[:, r * NT:(r + 1) * NT], eq_t, AX, ALU.add))
                lk(v.tensor_copy(pos_i, POS))
                lk(v.tensor_scalar(blk_i, pos_i, 7, None, ALU.logical_shift_right))
                lk(v.tensor_scalar(row_i, pos_i, P - 1, None, ALU.bitwise_and))
                lk(v.tensor_copy(blk_f, blk_i))
                lk(v.tensor_copy(row_f, row_i))
                dve.wait_ge(dest_ready, 2)
                shape = [P, NA, NBLK]
                lk(v.tensor_tensor(blk_vals[:, :, 2, :], iota_row[:, 0:NBLK].unsqueeze(1).to_broadcast(shape),
                                   blk_f.unsqueeze(2).to_broadcast(shape), ALU.is_equal))
                lk(v.tensor_tensor(blk_vals[:, :, 0, :], blk_vals[:, :, 2, :],
                                   dest_f.unsqueeze(2).to_broadcast(shape), ALU.mult))
                v.tensor_tensor(blk_vals[:, :, 1, :], blk_vals[:, :, 2, :],
                                sm[:, 64:64 + NA].unsqueeze(2).to_broadcast(shape), ALU.mult).then_inc(vals_done, 1)
                for a in range(0, NA, 8):
                    shape = [P, 8, P]
                    v.tensor_tensor(onehot_slot[:, a:a + 8, :], iota_row[:, :].unsqueeze(1).to_broadcast(shape),
                                    row_f[:, a:a + 8].unsqueeze(2).to_broadcast(shape),
                                    ALU.is_equal).then_inc(slots_done, 1)
                shape = [1, NBLK, E]
                lk(v.tensor_tensor(be_cmp, bend[c][0:1, :].unsqueeze(1).to_broadcast(shape),
                                   iota_row[0:1, 0:NBLK].unsqueeze(2).to_broadcast(shape), ALU.is_le))
                lk(v.tensor_reduce(be_f, be_cmp, AX, ALU.add))
                lk(v.tensor_scalar(be_i, be_f, float(E - 1), None, ALU.min))
                dve.wait_ge(table_done, 1)
                lk(v.tensor_copy(tab, pR[:, 0:3 * NBLK].rearrange("p (v j) -> p v j", v=3)))
                lk(v.tensor_scalar(un_t, tab[:, 2, :], -1.0, 1.0, ALU.mult, ALU.add))
                lk(v.tensor_tensor(un_t, un_t, pad_row, ALU.mult))
                lk(v.tensor_tensor(dest_i, tab[:, 0, :], un_t, ALU.add))
                lk(v.tensor_scalar(tok_i, dest_i, TOK - 1, None, ALU.bitwise_and))
                lk(v.tensor_scalar(gate_silu, tab[:, 1, :], 1.0 / (SN * SE), None, ALU.mult))
                lk(v.tensor_scalar(gate_up_s, tab[:, 1, :], SHE / (SN * SE), None, ALU.mult))

            @blk.tensor
            def _(pe):
                pe.wait_ge(mask_done, 1)
                m = M_t.rearrange("p t e -> p (t e)")
                nc.tensor.matmul(pG[0][:, 0:NTE], upper[:, :], m, start=True, stop=True)
                nc.tensor.matmul(pL[0][:, 0:NTE], ones[:, :], m, start=True, stop=True).then_inc(prefix_done, 1)
                pe.wait_ge(vals_done, 1)
                for a in range(NA):
                    if a % 8 == 0:
                        pe.wait_ge(slots_done, a // 8 + 1)
                    last = nc.tensor.matmul(pR[:, 0:3 * NBLK], onehot_slot[:, a, :],
                                            blk_vals[:, a].rearrange("p v j -> p (v j)"),
                                            start=(a == 0), stop=(a == NA - 1))
                last.then_inc(table_done, 1)

        mix = ffn_area[:, 0:12 * nw // 2].bitcast(F32)
        xg = [mix[:, u * D:(u + 1) * D] for u in range(UNR)]
        orow = [mix[:, (UNR + u) * D:(UNR + u + 1) * D] for u in range(UNR)]
        sg = gelu_g[:, :, :].rearrange("p c s -> p (c s)")
        hm = hid[:, :, :].rearrange("p c s -> p (c s)")
        xgT = S_out[:, :, :].rearrange("p t d -> p (t d)").bitcast(F16).rearrange(
            "p (h k s) -> p h k s", h=4, k=KD)
        hT = hid_hl[:, 0].rearrange("p h c s -> p h (c s)").rearrange("p h (k s) -> p h k s", k=KE)
        pX, pH = pG[1], pL[1]
        xg_in, moe_stored = [sem(f"xg_in{u}") for u in range(UNR)], [sem(f"moe_stored{u}") for u in range(UNR)]
        xt_done, xh_done, xl_done, gu_done, silu_done, hm_done, ht_done, hth_done, htl_done, dnb_done, out_ready = (
            sem(n) for n in ("xt_done", "xh_done", "xl_done", "gu_done", "silu_done", "hm_done", "ht_done",
                             "hth_done", "htl_done", "dnb_done", "out_ready"))
        mix_link = sem("mix_link")
        NI = NBLK // UNR

        adapt = ffn_area[:, :].bitcast(F32)
        base = 2 * UNR * D
        per = KD * A + D + 2 * KD
        aRows = adapt[:, base:base + NB * per].rearrange("p (b v) -> p b v", b=NB)
        aW1 = aRows[:, :, 0:KD * A].rearrange("p b (k a) -> p b k a", k=KD)
        aW2 = aRows[0:A + 1, :, KD * A:KD * A + D]
        aGam = aRows[:, :, KD * A + D:KD * A + D + KD]
        aBet = aRows[:, :, KD * A + D + KD:per]
        base += NB * per
        aB1 = adapt[0:A, base:base + NB]
        base += NB
        RB = 4
        rr = adapt[:, base:base + RB * TOPK * TB * D].rearrange("p (q r t d) -> p q r t d", q=RB, r=TOPK, t=TB)
        base += RB * TOPK * TB * D
        x2T = adapt[:, base:base + KD * S].rearrange("p (k s) -> p k s", k=KD)
        base += KD * S
        aH = adapt[0:A + 1, base:base + S]
        assert base + S <= 12 * nw // 2, (base + S, 12 * nw // 2)
        X = stage[:, :, :].rearrange("p a b -> p (a b)").rearrange("p (n d) -> p n d", n=NT)
        w1_in = xt_area[:, 0:2 * KD * F].bitcast(F32).rearrange("p (k f) -> p k f", k=KD)
        w2_in = xt_area[:, 2 * KD * F:].bitcast(F32).rearrange("p (c d) -> p c d", c=FC)
        b1_sb = tiny[:, 44:44 + FC]
        b2_sb = gam[:, :]
        adapt_in, ffn1_in = sem("adapt_in"), sem("ffn1_in")
        wq_link, wt_ready, wt_done, wd_ready, wd_done, w_scaled = (sem(n) for n in (
            "wq_link", "wt_ready", "wt_done", "wd_ready", "wd_done", "w_scaled"))
        stats = sb("stats", [P, 6 * NT])
        mv_all = sb("mv_all", [P, 2 * NT])
        mvv = mv_all[:, :].rearrange("p (n s) -> p n s", s=2)
        rstd_all = sb("rstd_all", [P, 2 * NT])
        nmr_all = rstd_all[:, NT:]
        amax = sb("amax", [P, 2 * NB])
        spread = sb("spread", [P, 64])
        wmax, wtop, wdiag, wall = spread[:, 0:2], spread[0:2, 2:3], spread[0:2, 4:6], spread[:, 6:8]
        wstep, winv = spread[:, 8:10], spread[:, 10:12]
        xmax, xtop, xdiag, xall, xstep, xinv = (spread[:, 12 + n:13 + n] for n in range(6))
        hmax, htop, hdiag, hall, hstep, hinv = (spread[:, 18 + n:19 + n] for n in range(6))
        s1, s2, b1s = spread[:, 24:25], spread[:, 25:26], spread[:, 32:32 + FC]
        pW = pM

        def top_of(dve, link, bank, n, top, diag, t_done, d_ready):
            dve.wait_ge(t_done, 1)
            link(nc.vector.tensor_reduce(top, bank[0:n, 0:P], AX, ALU.max))
            nc.vector.tensor_scalar(diag, ident[0:n, 0:n], top, None, ALU.mult).then_inc(d_ready, 1)

        def step_of(dve, link, bank, n, full, step, inv, d_done):
            dve.wait_ge(d_done, 1)
            link(nc.vector.tensor_copy(full, bank[:, P:P + n]))
            link(nc.vector.tensor_scalar(step, full, 1e-6, 1.0 / 127.0, ALU.max, ALU.mult))
            link(nc.vector.reciprocal(inv, step))

        def turn_max(pe, part, bank, n, t_ready, t_done):
            pe.wait_ge(t_ready, 1)
            nc.tensor.transpose(bank[0:n, 0:P], part, ident[:, :]).then_inc(t_done, 1)

        def spread_max(pe, diag, bank, n, d_ready, d_done):
            pe.wait_ge(d_ready, 1)
            nc.tensor.matmul(bank[:, P:P + n], ones[0:n, :], diag, start=True, stop=True).then_inc(d_done, 1)


        with nc.Block() as blk:
            @blk.gpsimd
            def _(pool):
                held = pool.alloc_register("held_pool")
                def gather(i, u, links, wait=True):
                    j = i * UNR + u
                    if wait:
                        pool.wait_ge(xt_done, j - UNR + 1)
                    nc.gpsimd.tensor_copy(tok_col[:, u:u + 1], tok_i[:, bass.ds(j, 1)]).then_inc(mix_link, 1)
                    hold(pool, held, mix_link, links, (consts, 10))
                    nc.gpsimd.indirect_dma_start(xg[u], None, xn_dram, bass.IndirectOffsetOnAxis(
                        ap=tok_col[:, u:u + 1], axis=0)).then_inc(xg_in[u], 16)

                def scatter(i, u, links):
                    j = i * UNR + u
                    if not (isinstance(i, int) and i == 0):
                        pool.wait_ge(moe_stored[u], i * 16)
                    nc.gpsimd.tensor_copy(dest_col[:, u:u + 1], dest_i[:, bass.ds(j, 1)]).then_inc(mix_link, 1)
                    pool.wait_ge(mix_link, links)
                    hold(pool, held, out_ready, j + 1, (consts, 10))
                    nc.gpsimd.indirect_dma_start(moe_dram, bass.IndirectOffsetOnAxis(
                        ap=dest_col[:, u:u + 1], axis=0), orow[u], None).then_inc(moe_stored[u], 16)
                for u in range(UNR):
                    gather(0, u, u + 1, wait=False)
                for u in range(UNR):
                    gather(1, u, UNR + 2 * u + 1)
                    scatter(0, u, UNR + 2 * u + 2)
                with pool.Fori(1, NI - 1) as i:
                    for u in range(UNR):
                        gather(i + 1, u, UNR + i * 2 * UNR + 2 * u + 1)
                        scatter(i, u, UNR + i * 2 * UNR + 2 * u + 2)
                for u in range(UNR):
                    scatter(NI - 1, u, UNR + (NI - 1) * 2 * UNR + u + 1)
                for u in range(UNR):
                    pool.wait_ge(moe_stored[u], NI * 16)

            @blk.scalar
            def _(act):
                def split_x(j):
                    act.wait_ge(xt_done, j + 1)
                    nc.scalar.activation(xgT[:, 0], pX[:, 0:D].rearrange("p (k s) -> p k s", k=KD), ACT.Copy,
                                         scale=SN).then_inc(xh_done, 1)

                def block(j, last=False):
                    act.wait_ge(gu_done, 2 * j + 1)
                    nc.scalar.activation(sg, pG[0][:, :], ACT.Silu,
                                         scale=gate_silu[:, bass.ds(j, 1)]).then_inc(silu_done, 1)
                    if not last:
                        split_x(j + 1)
                    act.wait_ge(ht_done, j + 1)
                    nc.scalar.activation(hT[:, 0], pH[:, :].rearrange("p (k s) -> p k s", k=KE),
                                         ACT.Copy).then_inc(hth_done, 1)
                split_x(0)
                for u in range(UNR):
                    block(u)
                with act.Fori(1, NI - 1) as i:
                    for u in range(UNR):
                        block(i * UNR + u)
                for u in range(UNR):
                    block((NI - 1) * UNR + u, last=(u == UNR - 1))

            @blk.sync
            def _(sp):
                with sp.Fori(0, NB) as b:
                    n = sp.value_load(itC[0:1, bass.ds(b, 1)], min_val=0, max_val=NL - 1)
                    one = bass.ds(n, 1)
                    at = bass.ds(b, 1)
                    sp.dma_start(aW1[:, at], cW1[one, :, :].rearrange("l (k p) a -> p l k a", p=P)).then_inc(adapt_in, 16)
                    sp.dma_start(aW2[0:A, at, :], cW2[one, :, :].rearrange("l a d -> a l d")).then_inc(adapt_in, 16)
                    sp.dma_start(aW2[A:A + 1, at, :], cb2[one, :].unsqueeze(0)).then_inc(adapt_in, 16)
                    sp.dma_start(aB1[:, at], cb1T[one, :, :].rearrange("l a o -> (l a) o")).then_inc(adapt_in, 16)
                    sp.dma_start(aGam[:, at, :], cgammaT[one, :, :].rearrange("l p k -> p l k")).then_inc(adapt_in, 16)
                    sp.dma_start(aBet[:, at, :], cbetaT[one, :, :].rearrange("l p k -> p l k")).then_inc(adapt_in, 16)
                sp.dma_start(w1_in, w1T.rearrange("(k p) f -> p k f", p=P)).then_inc(ffn1_in, 16)
                sp.dma_start(w2_in, w2T.rearrange("(c p) d -> p c d", p=P)).then_inc(ffn1_in, 16)
                sp.dma_start(b1_sb, b1T).then_inc(ffn1_in, 16)
                sp.dma_start(b2_sb, b2.partition_broadcast(P)).then_inc(ffn1_in, 16)
                sp.dma_start(X, res_dram.rearrange("(n p) d -> p n d", p=P)).then_inc(ffn1_in, 16)
                sp.wait_ge(adapt_in, 6 * 16 * NB)
                sp.wait_ge(ffn1_in, 80)

            @blk.vector
            def _(dve):
                def split_x(j):
                    dve.wait_ge(xh_done, j + 1)
                    nc.vector.scalar_tensor_tensor(xgT[:, 1], pX[:, 0:D].rearrange("p (k s) -> p k s", k=KD), SN,
                                                   xgT[:, 0], ALU.mult, ALU.subtract).then_inc(xl_done, 1)

                def emit(i, u):
                    dve.wait_ge(dnb_done, i * UNR + u + 1)
                    if not (isinstance(i, int) and i == 0):
                        dve.wait_ge(moe_stored[u], i * 16)
                    nc.vector.tensor_scalar(orow[u], pD[:, 0, 0:D], 1.0 / (SHE * SE), None,
                                            ALU.mult).then_inc(out_ready, 1)

                def block(i, u, first=False, last=False):
                    j = i * UNR + u
                    dve.wait_ge(silu_done, j + 1)
                    dve.wait_ge(gu_done, 2 * j + 2)
                    nc.vector.scalar_tensor_tensor(hm, pL[0][:, :], gate_up_s[:, bass.ds(j, 1)], sg,
                                                   ALU.mult, ALU.mult).then_inc(hm_done, 1)
                    if not last:
                        split_x(j + 1)
                    if not first:
                        emit(i if u else i - 1, (u - 1) % UNR)
                    dve.wait_ge(hth_done, j + 1)
                    nc.vector.tensor_tensor(hT[:, 1], pH[:, :].rearrange("p (k s) -> p k s", k=KE), hT[:, 0],
                                            ALU.subtract).then_inc(htl_done, 1)
                split_x(0)
                for u in range(UNR):
                    block(0, u, first=(u == 0))
                with dve.Fori(1, NI - 2) as i:
                    for u in range(UNR):
                        block(i, u)
                lk = linker(dve, wq_link)
                block(NI - 2, 0)
                dve.wait_ge(ffn1_in, 80)
                lk(nc.vector.tensor_reduce(wmax[:, 0:1], w1_in.rearrange("p k f -> p (k f)"), AX, ALU.max,
                                           apply_absolute_value=True))
                block(NI - 2, 1)
                nc.vector.tensor_reduce(wmax[:, 1:2], w2_in.rearrange("p c d -> p (c d)"), AX, ALU.max,
                                        apply_absolute_value=True).then_inc(wt_ready, 1)
                block(NI - 2, 2)
                block(NI - 1, 0)
                top_of(dve, lk, pW, 2, wtop, wdiag, wt_done, wd_ready)
                block(NI - 1, 1)
                step_of(dve, lk, pW, 2, wall, wstep, winv, wd_done)
                block(NI - 1, 2, last=True)
                emit(NI - 1, UNR - 1)
                for j, w in enumerate((w1_in, w2_in)):
                    nc.vector.tensor_scalar(w, w, winv[:, j:j + 1], MAGIC, ALU.mult, ALU.add).then_inc(w_scaled, 1)

            @blk.tensor
            def _(pe):
                def transpose_x(i, u):
                    pe.wait_ge(xg_in[u], i * 16 + 16)
                    if not (isinstance(i, int) and i * UNR + u == 0):
                        pe.wait_ge(xl_done, i * UNR + u)
                    for k in range(KD):
                        last = nc.tensor.transpose(pX[:, k * P:(k + 1) * P], xg[u][:, k * P:(k + 1) * P], ident[:, :])
                    last.then_inc(xt_done, 1)

                def gate_up(i, u):
                    j = i * UNR + u
                    e = pe.snap(expert[u], min_val=0, max_val=E - 1)
                    pe.wait_ge(xl_done, j + 1)
                    if not (isinstance(j, int) and j == 0):
                        pe.wait_ge(hm_done, j)
                    for h, bank in enumerate((pG[0], pL[0])):
                        for k in range(KD):
                            wh = GUh[:, k, bass.ds(e, 1), h * FE:(h + 1) * FE].rearrange("p e f -> p (e f)")
                            wl = GUl[:, k, bass.ds(e, 1), h * FE:(h + 1) * FE].rearrange("p e f -> p (e f)")
                            nc.tensor.matmul(bank[:, :], xgT[:, 0, k, :], wh, start=(k == 0), stop=False)
                            nc.tensor.matmul(bank[:, :], xgT[:, 1, k, :], wh, start=False, stop=False)
                            last = nc.tensor.matmul(bank[:, :], xgT[:, 0, k, :], wl, start=False, stop=(k == KD - 1))
                        last.then_inc(gu_done, 1)

                def transpose_h(j):
                    pe.wait_ge(hm_done, j + 1)
                    if not (isinstance(j, int) and j == 0):
                        pe.wait_ge(htl_done, j)
                    for k in range(KE):
                        last = nc.tensor.transpose(pH[:, k * P:(k + 1) * P], hm[:, k * P:(k + 1) * P], ident[:, :])
                    last.then_inc(ht_done, 1)

                def down(i, u):
                    j = i * UNR + u
                    e = pe.snap(expert[u % UNR], min_val=0, max_val=E - 1)
                    pe.wait_ge(htl_done, j + 1)
                    if not (isinstance(j, int) and j == 0):
                        pe.wait_ge(out_ready, j)
                    for k in range(KE):
                        wh = DNh[:, k, bass.ds(e, 1), :].rearrange("p e d -> p (e d)")
                        wl = DNl[:, k, bass.ds(e, 1), :].rearrange("p e d -> p (e d)")
                        o = pD[:, 0, 0:D]
                        nc.tensor.matmul(o, hT[:, 0, k, :], wh, start=(k == 0), stop=False)
                        nc.tensor.matmul(o, hT[:, 1, k, :], wh, start=False, stop=False)
                        last = nc.tensor.matmul(o, hT[:, 0, k, :], wl, start=False, stop=(k == KE - 1))
                    last.then_inc(dnb_done, 1)

                def block(i, u, first=False, last=False):
                    j = i * UNR + u
                    gate_up(i, u)
                    if not last:
                        pe.reg_load(expert[(u + 1) % UNR], be_i[0:1, bass.ds(j + 1, 1)])
                        transpose_x(i + 1 if u == UNR - 1 else i, (u + 1) % UNR)
                    if not first:
                        down(i, u - 1)
                    transpose_h(j)
                expert = [pe.alloc_register(f"expert{u}") for u in range(UNR)]
                pe.reg_load(expert[0], be_i[0:1, 0:1])
                transpose_x(0, 0)
                for u in range(UNR):
                    block(0, u, first=(u == 0))
                with pe.Fori(1, NI - 1) as i:
                    for u in range(UNR):
                        block(i, u)
                for u in range(UNR):
                    block(NI - 1, u, last=(u == UNR - 1))
                    if u == 0:
                        turn_max(pe, wmax, pW, 2, wt_ready, wt_done)
                    if u == 1:
                        spread_max(pe, wdiag, pW, 2, wd_ready, wd_done)
                down(NI - 1, UNR - 1)
        big = moe_area[:, :].bitcast(F32)
        h_all = big[:, 0:FC * TOK].rearrange("p (f n) -> p f n", f=FC)
        o = FC * TOK
        X3 = big[:, o:o + NT * D].rearrange("p (n d) -> p n d", n=NT)
        o += NT * D
        x3q = big[:, o:o + KD * TOK // 2].bitcast(BF16).rearrange("p (k n) -> p k n", k=KD)
        x3T = xt_area[:, :].bitcast(F32).rearrange("p (k n) -> p k n", k=KD)
        hq = ffn_area[:, 0:FC * TOK].bitcast(BF16).rearrange("p (f n) -> p f n", f=FC)
        w1q = g0_sb[:, :, :].rearrange("p c d -> p (c d)").bitcast(BF16).rearrange("p (k f) -> p k f", k=KD)
        w2q = [t[:, :, :].rearrange("p t d -> p (t d)").bitcast(BF16).rearrange("p (c d) -> p c d", d=D)
               for t in (E_out, XN)]
        b2s = bet[:, :]

        rows_in = [sem(f"rows_in{q}") for q in range(RB)]
        rows_used, t2_done, t2c_done, m1_done, relu_done, m2_done, pre_done, pre_link = (sem(n) for n in (
            "rows_used", "t2_done", "t2c_done", "m1_done", "relu_done", "m2_done", "pre_done", "pre_link"))
        sum_done, bn2_done, rstd2_done, nmr_done, nrm2_done, t3_done, t3c_done, max_done, cp_link = (sem(n) for n in (
            "sum_done", "bn2_done", "rstd2_done", "nmr_done", "nrm2_done", "t3_done", "t3c_done", "max_done", "cp_link"))
        one_row = sem("one_row")
        pT2, pA, pT3 = pR, pG[1], pG[0]

        with nc.Block() as blk:
            @blk.sync
            def _(sp):
                rank_rows = moe_dram[0:TOPK * TOK, :].rearrange("(r b t p) d -> p b r t d", r=TOPK, t=TB, p=P)
                for b in range(NB):
                    if b >= RB:
                        sp.wait_ge(rows_used, b - RB + 1)
                    for r in range(TOPK):
                        sp.dma_start(rr[:, b % RB, r], rank_rows[:, b, r]).then_inc(rows_in[b % RB], 16)

            @blk.gpsimd
            def _(pool):
                lk = linker(pool, cp_link)
                nc.gpsimd.memset(aH[A:A + 1, :], 1.0).then_inc(one_row, 1)
                pool.wait_ge(one_row, 1)
                def add_rows(b):
                    q = b % RB
                    pool.wait_ge(rows_in[q], 32 * (b // RB + 1))
                    nc.gpsimd.tensor_tensor(rr[:, q, 0], rr[:, q, 0], rr[:, q, 1], ALU.add).then_inc(sum_done, 1)
                for b in range(3):
                    add_rows(b)
                for b in range(NB):
                    if b + 3 < NB:
                        add_rows(b + 3)
                    t = slice(b * TB, (b + 1) * TB)
                    pool.wait_ge(bn2_done, b + 1)
                    lk(nc.gpsimd.tensor_tensor(rstd_all[:, t], mvv[:, t, 1], eps2, ALU.add))
                    nc.gpsimd.tensor_tensor(rstd_all[:, t], rstd_all[:, t], mhalf, ALU.pow).then_inc(rstd2_done, 1)

            @blk.scalar
            def _(act):
                nc.scalar.activation(w1q, w1_in, ACT.Copy, bias=-MAGIC)
                for n, part in enumerate(w2q):
                    nc.scalar.activation(part, w2_in[:, n * 4:(n + 1) * 4, :], ACT.Copy, bias=-MAGIC)
                for step in range(-1, NB + 3):
                    b = step
                    if 0 <= b < NB:
                        act.wait_ge(m1_done, b + 1)
                        if b:
                            act.wait_ge(m2_done, b)
                        nc.scalar.activation(aH[0:A, :], pA[0:A, 0:S], ACT.Relu, bias=aB1[:, b:b + 1]).then_inc(relu_done, 1)
                    b = step + 1
                    if b < NB:
                        act.wait_ge(t2_done, b + 1)
                        if b:
                            act.wait_ge(m1_done, b)
                        nc.scalar.activation(x2T, pT2.rearrange("p (k s) -> p k s", k=KD), ACT.Copy).then_inc(t2c_done, 1)
                    b = step - 2
                    if 0 <= b < NB:
                        act.wait_ge(nmr_done, b + 1)
                        for n in range(b * TB, (b + 1) * TB):
                            last = nc.scalar.activation(X3[:, n, :], X3[:, n, :], ACT.Identity,
                                                        bias=nmr_all[:, n:n + 1], scale=rstd_all[:, n:n + 1])
                        last.then_inc(nrm2_done, 1)
                    b = step - 3
                    if 0 <= b < NB:
                        act.wait_ge(t3_done, b + 1)
                        for k in range(KD):
                            last = nc.scalar.activation(x3T[:, k, b * S:(b + 1) * S], pT3[:, k * S:(k + 1) * S],
                                                        ACT.Identity, bias=aBet[:, b, k:k + 1], scale=aGam[:, b, k:k + 1])
                        last.then_inc(t3c_done, 1)

            @blk.vector
            def _(dve):
                v = nc.vector
                st = stats[:, :].rearrange("p (n s) -> p n s", s=6)
                for step in range(-1, NB + 4):
                    b = step + 1
                    if b < NB:
                        dve.wait_ge(sum_done, b + 1)
                        t = slice(b * TB, (b + 1) * TB)
                        v.tensor_tensor(X[:, t, :], X[:, t, :], rr[:, b % RB, 0], ALU.add).then_inc(rows_used, 1)
                    b = step - 1
                    if 0 <= b < NB:
                        t = slice(b * TB, (b + 1) * TB)
                        dve.wait_ge(m2_done, b + 1)
                        dve.wait_ge(rows_used, b + 1)
                        v.tensor_tensor(X3[:, t, :], pD[:, :, 0:D], X[:, t, :], ALU.add).then_inc(pre_done, 1)
                        dve.wait_ge(pre_done, b + 1)
                        for n in range(b * TB, (b + 1) * TB):
                            v.bn_stats(st[:, n, :], X3[:, n, :]).then_inc(pre_link, 1)
                        for n in range(TB):
                            dve.wait_ge(pre_link, b * TB + n + 1)
                            last = v.bn_aggr(mvv[:, b * TB + n, :], st[:, b * TB + n, :])
                        last.then_inc(bn2_done, 1)
                    b = step - 2
                    if 0 <= b < NB:
                        t = slice(b * TB, (b + 1) * TB)
                        dve.wait_ge(rstd2_done, b + 1)
                        dve.wait_ge(bn2_done, b + 1)
                        v.scalar_tensor_tensor(nmr_all[:, t], mvv[:, t, 0], -1.0, rstd_all[:, t],
                                               ALU.mult, ALU.mult).then_inc(nmr_done, 1)
                    b = step - 4
                    if 0 <= b < NB:
                        dve.wait_ge(t3c_done, b + 1)
                        v.tensor_reduce(amax[:, b:b + 1], x3T[:, :, b * S:(b + 1) * S], mybir.AxisListType.XY, ALU.max,
                                        apply_absolute_value=True).then_inc(max_done, 1)

            @blk.tensor
            def _(pe):
                pe.wait_ge(one_row, 1)
                for step in range(-1, NB + 3):
                    b = step
                    if 0 <= b < NB:
                        pe.wait_ge(t2c_done, b + 1)
                        if b:
                            pe.wait_ge(relu_done, b)
                        for k in range(KD):
                            last = nc.tensor.matmul(pA[0:A, 0:S], aW1[:, b, k, :], x2T[:, k, :],
                                                    start=(k == 0), stop=(k == KD - 1))
                        last.then_inc(m1_done, 1)
                    b = step + 1
                    if b < NB:
                        pe.wait_ge(rows_used, b + 1)
                        if b:
                            pe.wait_ge(t2c_done, b)
                        for t in range(TB):
                            for k in range(KD):
                                last = nc.tensor.transpose(pT2[:, k * S + t * P:k * S + (t + 1) * P],
                                                           X[:, b * TB + t, k * P:(k + 1) * P], ident[:, :])
                        last.then_inc(t2_done, 1)
                    b = step - 3
                    if 0 <= b < NB:
                        pe.wait_ge(nrm2_done, b + 1)
                        if b:
                            pe.wait_ge(t3c_done, b)
                        for t in range(TB):
                            for k in range(KD):
                                last = nc.tensor.transpose(pT3[:, k * S + t * P:k * S + (t + 1) * P],
                                                           X3[:, b * TB + t, k * P:(k + 1) * P], ident[:, :])
                        last.then_inc(t3_done, 1)
                    b = step
                    if 0 <= b < NB:
                        pe.wait_ge(relu_done, b + 1)
                        if b:
                            pe.wait_ge(pre_done, b)
                        for t in range(TB):
                            last = nc.tensor.matmul(pD[:, t, 0:D], aH[:, t * P:(t + 1) * P], aW2[:, b, :],
                                                    start=True, stop=True)
                        last.then_inc(m2_done, 1)

        NCH = 4
        CH = TOK // NCH
        d_link, xt_rdy, xt_dn, xd_rdy, xd_dn = (sem(n) for n in ("d_link", "xt_rdy", "xt_dn", "xd_rdy", "xd_dn"))
        s1_done, r1_done, q1_done, mm1_done, g_done, gmax_done = (sem(n) for n in (
            "s1_done", "r1_done", "q1_done", "mm1_done", "g_done", "gmax_done"))
        ht_rdy, ht_dn, hd_rdy, hd_dn, s2_done, b2_done, z_done, rh_done, qh_act, qh_dve, acc_done, o_done, out_stored = (
            sem(n) for n in ("ht_rdy", "ht_dn", "hd_rdy", "hd_dn", "s2_done", "b2_done", "z_done", "rh_done",
                             "qh_act", "qh_dve", "acc_done", "o_done", "out_stored"))
        act_chunks = [1, 3, 5]
        acc = [halves[t // 8][:, (t % 8) // 2, (t % 2) * D:(t % 2 + 1) * D] for t in range(NT)]

        with nc.Block() as blk:
            @blk.sync
            def _(sp):
                o_rows = out.rearrange("b (t p) d -> p b t d", p=P)
                for b in range(NB):
                    sp.wait_ge(o_done, b + 1)
                    sp.dma_start(o_rows[:, b], X3[:, b * TB:(b + 1) * TB, :]).then_inc(out_stored, 16)
                sp.wait_ge(out_stored, 16 * NB)

            @blk.gpsimd
            def _(pool):
                pool.wait_ge(b2_done, 1)
                for b in range(NB):
                    xb = X[:, b * TB:(b + 1) * TB, :]
                    nc.gpsimd.tensor_tensor(xb, xb, b2s.unsqueeze(1).to_broadcast([P, TB, D]), ALU.add).then_inc(z_done, 1)

            @blk.scalar
            def _(act):
                nc.scalar.activation(tiny[:, 52:53], iota_p[:, :], ACT.Gelu)
                for c in range(NCH):
                    act.wait_ge(r1_done, c + 1)
                    nc.scalar.activation(x3q[:, :, c * CH:(c + 1) * CH], x3T[:, :, c * CH:(c + 1) * CH], ACT.Copy,
                                         bias=-MAGIC).then_inc(q1_done, 1)
                act.wait_ge(s1_done, 1)
                for f in range(FC):
                    act.wait_ge(mm1_done, f + 1)
                    nc.scalar.activation(h_all[:, f, :], halves[f % 2][:, :, :].rearrange("p b n -> p (b n)"), ACT.Gelu,
                                         bias=b1s[:, f:f + 1], scale=s1).then_inc(g_done, 1)
                for n, f in enumerate(act_chunks):
                    act.wait_ge(rh_done, f + 1)
                    nc.scalar.activation(hq[:, f, :], h_all[:, f, :], ACT.Copy, bias=-MAGIC).then_inc(qh_act, 1)

            @blk.vector
            def _(dve):
                v = nc.vector
                lk = linker(dve, d_link)
                v.tensor_reduce(xmax, amax[:, 0:NB], AX, ALU.max).then_inc(xt_rdy, 1)
                top_of(dve, lk, pR, 1, xtop[0:1], xdiag[0:1], xt_dn, xd_rdy)
                step_of(dve, lk, pR, 1, xall, xstep, xinv, xd_dn)
                for c in range(NCH):
                    xc = x3T[:, :, c * CH:(c + 1) * CH]
                    v.tensor_scalar(xc, xc, xinv, MAGIC, ALU.mult, ALU.add).then_inc(r1_done, 1)
                lk(v.tensor_tensor(s1, xstep, wstep[:, 0:1], ALU.mult))
                v.tensor_scalar(b1s, b1_sb, s1, None, ALU.mult).then_inc(s1_done, 1)
                for f in range(FC):
                    dve.wait_ge(g_done, f + 1)
                    lk(v.tensor_reduce(amax[:, NB + f:NB + f + 1], h_all[:, f, :], AX, ALU.max, apply_absolute_value=True))
                v.tensor_reduce(hmax, amax[:, NB:NB + FC], AX, ALU.max).then_inc(ht_rdy, 1)
                top_of(dve, lk, pR, 1, htop[0:1], hdiag[0:1], ht_dn, hd_rdy)
                step_of(dve, lk, pR, 1, hall, hstep, hinv, hd_dn)

                def to_grid(f):
                    v.tensor_scalar(h_all[:, f, :], h_all[:, f, :], hinv, MAGIC, ALU.mult, ALU.add).then_inc(rh_done, 1)
                to_grid(0)
                lk(v.tensor_tensor(s2, hstep, wstep[:, 1:2], ALU.mult))
                v.tensor_scalar(b2s, b2_sb, s2, None, ALU.mult).then_inc(b2_done, 1)
                for f in range(FC):
                    if f + 1 < FC:
                        to_grid(f + 1)
                    if f not in act_chunks:
                        dve.wait_ge(rh_done, f + 1)
                        v.tensor_scalar(hq[:, f, :], h_all[:, f, :], MAGIC, None, ALU.subtract).then_inc(qh_dve, 1)
                for b in range(NB):
                    dve.wait_ge(acc_done, b + 1)
                    dve.wait_ge(z_done, b + 1)
                    bank = halves[b // 4][:, b % 4, :].rearrange("p (t d) -> p t d", t=TB)
                    v.scalar_tensor_tensor(X3[:, b * TB:(b + 1) * TB, :], bank, s2, X[:, b * TB:(b + 1) * TB, :],
                                           ALU.mult, ALU.add).then_inc(o_done, 1)

            @blk.tensor
            def _(pe):
                turn_max(pe, xmax, pR, 1, xt_rdy, xt_dn)
                spread_max(pe, xdiag[0:1], pR, 1, xd_rdy, xd_dn)
                for f in range(FC):
                    if f >= 2:
                        pe.wait_ge(g_done, f - 1)
                    for c in range(NCH):
                        if f == 0:
                            pe.wait_ge(q1_done, c + 1)
                        if f == 1 and c == 0:
                            pe.wait_ge(d_link, 3)
                        for k in range(KD):
                            last = nc.tensor.matmul(halves[f % 2][:, c, :], w1q[:, k, f * P:(f + 1) * P],
                                                    x3q[:, k, c * CH:(c + 1) * CH], start=(k == 0), stop=(k == KD - 1))
                    last.then_inc(mm1_done, 1)
                pe.wait_ge(g_done, FC)
                turn_max(pe, hmax, pR, 1, ht_rdy, ht_dn)
                spread_max(pe, hdiag[0:1], pR, 1, hd_rdy, hd_dn)
                def ready(f):
                    if f in act_chunks:
                        pe.wait_ge(qh_act, act_chunks.index(f) + 1)
                    else:
                        pe.wait_ge(qh_dve, f + 1 - sum(a < f for a in act_chunks))

                def second(t, f):
                    return nc.tensor.matmul(acc[t], hq[:, f, t * P:(t + 1) * P], w2q[f // 4][:, f % 4, :],
                                            start=(f == 0 and t % 2 == 0), stop=(f == FC - 1 and t % 2 == 1),
                                            skip_group_check=True)
                for f in range(FC - 3):
                    ready(f)
                    for t in range(NT):
                        second(t, f)
                for f in range(FC - 3, FC):
                    ready(f)
                for b in range(NB):
                    for f in range(FC - 3, FC):
                        for t in range(b * TB, (b + 1) * TB):
                            last = second(t, f)
                    last.then_inc(acc_done, 1)


def kernel(**inputs):
    import concourse.bacc as bacc
    from concourse.bass_utils import run_bass_kernel_spmd

    def host(name):
        return np.asarray(inputs[name])

    def swap(name):
        return np.ascontiguousarray(np.swapaxes(host(name), -1, -2))

    def columns(name):
        return np.ascontiguousarray(host(name).reshape(host(name).shape[0], -1, P).transpose(0, 2, 1))

    arrays = {
        "x": host("x"), "xT": swap("x"), "itokA": host("itok_B_0_2"), "itokC": host("itok_B_0_8"),
        "Wi0": host("L0_cond_Wi0"), "Wi1": host("L0_cond_Wi1"), "Wo": host("L0_cond_Wo"),
        "sWi0": host("L0_cond_sWi0"), "sWi1": host("L0_cond_sWi1"), "sWo": host("L0_cond_sWo"),
        "g0": host("L0_cond_g0"), "g1T": swap("L0_cond_g1"),
        "gamma0": host("L0_ffn_ln_gamma"), "beta0": host("L0_ffn_ln_beta"), "routerT": swap("L0_ffn_router_w"),
        "guT": swap("L0_ffn_gate_up_w"), "dnT": swap("L0_ffn_down_w"),
        "cW1": host("L1_cond_W1"), "cb1T": host("L1_cond_b1")[:, :, None],
        "cW2": host("L1_cond_W2"), "cb2": host("L1_cond_b2"),
        "cgammaT": columns("L1_cond_gamma"), "cbetaT": columns("L1_cond_beta"),
        "w1T": swap("L1_ffn_w1"), "b1T": np.ascontiguousarray(host("L1_ffn_b1").reshape(-1, P).T),
        "w2T": swap("L1_ffn_w2"), "b2": host("L1_ffn_b2"),
    }
    arrays = {"in_" + k: np.ascontiguousarray(v) for k, v in arrays.items()}
    nc = bacc.Bacc("TRN2", target_bir_lowering=False, num_devices=1)
    args = [nc.dram_tensor(k, v.shape, mybir.dt.from_np(v.dtype), kind="ExternalInput").ap()
            for k, v in arrays.items()]
    out = nc.dram_tensor("out_0", host("x").shape, F32, kind="ExternalOutput").ap()
    build(nc, *args, out)
    return run_bass_kernel_spmd(nc, [arrays], core_ids=[0]).results[0]["out_0"]
```

```python
from contextlib import ExitStack

import numpy as np

import concourse.bass as bass
from concourse import mybir

P = 128
F32, F16, BF16, I32 = mybir.dt.float32, mybir.dt.float16, mybir.dt.bfloat16, mybir.dt.int32
ALU = mybir.AluOpType
ACT = mybir.ActivationFunctionType
AX = mybir.AxisListType.X

SX, SW = 16.0, 1024.0
SH = 256.0
SN, SE, SHE = 8.0, 256.0, 64.0
MAGIC = 1.5 * 2.0 ** 23


def hold(eng, reg, sem, value, met):
    if isinstance(value, int):
        eng.wait_ge(sem, value)
        return
    eng.reg_mov(reg, value)
    eng.wait_ge(*met)
    eng.wait_ge(sem, reg)


def linker(eng, sem, base=0):
    n = [0]

    def link(ins, reg=None, met=None):
        n[0] += 1
        ins.then_inc(sem, 1)
        if reg is None:
            eng.wait_ge(sem, base + n[0])
        else:
            hold(eng, reg, sem, base + n[0], met)
    link.n = n
    return link


def build(nc, x, xT, itokA, itokC, Wi0, Wi1, Wo, sWi0, sWi1, sWo, g0, g1T, gamma0, beta0, routerT, guT, dnT,
          cW1, cb1T, cW2, cb2, cgammaT, cbetaT, w1T, b1T, w2T, b2, out):
    NB, S, D = x.shape
    TOK = NB * S
    NT = TOK // P
    TB = S // P
    KD = D // P
    NEA, _, F = Wi0.shape
    FC = F // P
    PAIRS = FC // 2
    NP = 2 * PAIRS
    E, _, F2 = guT.shape
    FE = F2 // 2
    KE = FE // P
    NL, _, A = cW1.shape
    TOPK = 2
    NBLK = (TOPK * TOK + E * (P - 1)) // P
    UNR = 3
    assert (D, F, S, FE, NBLK % UNR) == (256, 1024, 256, 512, 0)

    xn_dram = nc.dram_tensor("xn_rows", [TOK, D], F32).ap()
    res_dram = nc.dram_tensor("residual_rows", [TOK, D], F32).ap()
    moe_dram = nc.dram_tensor("moe_rows", [TOPK * TOK + NBLK * P, D], F32).ap()

    with ExitStack() as ctx:
        def sb(name, shape, dt=F32):
            return ctx.enter_context(nc.sbuf_tensor(name, shape, dt))

        def pb(name, shape):
            return ctx.enter_context(nc.psum_tensor(name, shape, F32))

        def sem(name):
            return ctx.enter_context(nc.semaphore(name))

        xb_sb = sb("xb_sb", [P, TB, D])
        xt_area = sb("xt_area", [P, 2 * KD * TOK], F16)
        moe_area = sb("moe_area", [P, 2 * (KD * E * F2 + KE * E * D)], F16)
        ffn_area = sb("ffn_area", [P, 4 * (KD * F * 2 + FC * D) // 1], F16)
        stage = sb("stage", [P, 2, KD * F])
        gelu_g = sb("gelu_g", [P, 2, S])
        hid = sb("hid", [P, 2, S])
        hid_hl = sb("hid_hl", [P, 2, 2, 2, S], F16)
        S_out = sb("S_out", [P, TB, D])
        E_out = sb("E_out", [P, TB, D])
        XN = sb("XN", [P, TB, D])
        xnT = sb("xnT", [P, KD, S])
        gam = sb("gam", [P, D])
        bet = sb("bet", [P, D])
        g0_sb = sb("g0_sb", [P, 2 * KD, D])
        rw_sb = sb("rw_sb", [P, KD, E])
        LG = sb("LG", [P, NT, E])
        ident = sb("ident", [P, P])
        upper = sb("upper", [P, P])
        ones = sb("ones", [P, P])
        upper_h = sb("upper_h", [P, P], BF16)
        ones_h = sb("ones_h", [P, P], BF16)
        iota_row = sb("iota_row", [P, P])
        iota_p = sb("iota_p", [P, 1])
        rev_e = sb("rev_e", [P, E])
        itA = sb("itA", [1, NB], I32)
        itC = sb("itC", [1, NB], I32)
        row = sb("row", [1, 3 * D])
        g1_row, junk_row = row[0:1, 0:2 * D].rearrange("p (j d) -> p j d", j=2), row[0:1, 2 * D:3 * D]
        tiny = sb("tiny", [P, 64])
        gT = tiny[:, 0:4]
        logit2, mx1, dl2, ex2 = tiny[0:1, 4:6], tiny[0:1, 6:7], tiny[0:1, 8:10], tiny[0:1, 10:12]
        sm1, rs1, w2row, ebase = tiny[0:1, 12:13], tiny[0:1, 13:14], tiny[0:1, 14:16], tiny[0:1, 16:18]
        wbc, rstd, vpe = tiny[:, 18:20], tiny[:, 20:22], tiny[:, 22:24]
        mhalf, eps2 = tiny[:, 24:26], tiny[:, 42:44]
        mv = tiny[:, 26:30].rearrange("p (t s) -> p t s", t=2)
        bst = tiny[:, 30:42].rearrange("p (t s) -> p t s", t=2)

        XTh = xt_area[:, 0:KD * TOK].rearrange("p (k n) -> p k n", k=KD)
        XTl = xt_area[:, KD * TOK:].rearrange("p (k n) -> p k n", k=KD)
        ng, nd = KD * E * F2, KE * E * D
        GUh = moe_area[:, 0:ng].rearrange("p (k e f) -> p k e f", k=KD, e=E)
        GUl = moe_area[:, ng:2 * ng].rearrange("p (k e f) -> p k e f", k=KD, e=E)
        DNh = moe_area[:, 2 * ng:2 * ng + nd].rearrange("p (k e d) -> p k e d", k=KE, e=E)
        DNl = moe_area[:, 2 * ng + nd:].rearrange("p (k e d) -> p k e d", k=KE, e=E)
        nw = KD * F

        def ffn_w(s, j):
            v = ffn_area[:, (6 * s + j) * nw:(6 * s + j + 1) * nw]
            return v.rearrange("p (k f) -> p k f", k=KD) if j < 4 else v.rearrange("p (c d) -> p c d", c=FC)

        early = moe_area[:, ng:].bitcast(F32)
        xT_in = early[:, 0:KD * TOK].rearrange("p (u k n) -> p u k n", u=4, k=KD)
        sW_in = early[:, KD * TOK:KD * TOK + 3 * nw].rearrange("p (j v) -> p j v", j=3)

        halves = [pb(f"psum_half{i}", [P, 4, 512]) for i in range(2)]
        pG = [halves[0][:, i, :] for i in range(2)]
        pL = [halves[0][:, 2 + i, :] for i in range(2)]
        pD = halves[1][:, 0:2, :]
        pM, pR = halves[1][:, 2, :], halves[1][:, 3, :]

        def keep_warm(pe, bank, n):
            moving = ones_h[:, :].unsqueeze(1).to_broadcast([P, 4, P])
            with pe.Fori(0, n // 2) as _:
                for _ in range(2):
                    nc.tensor.matmul(bank.rearrange("p (a b) -> p a b", a=4), ones_h[:, :], moving,
                                     start=True, stop=True)

        x_in = [sem(f"x_in{u}") for u in range(4)]
        w_in = [sem(f"w_in{u}") for u in range(6)]
        small_in, ids_in = sem("small_in"), sem("ids_in")
        xb_in, gate_in, res_stored = sem("xb_in"), sem("gate_in"), sem("res_stored")
        buf_in = [sem("buf0_in"), sem("buf1_in")]
        conv_hi, conv_lo, early_hi, early_lo = (sem(n) for n in ("conv_hi", "conv_lo", "early_hi", "early_lo"))
        up_done, dn_done = sem("up_done"), sem("dn_done")
        gelu_done, h_done, hh_done, hl_done = sem("gelu_done"), sem("h_done"), sem("hh_done"), sem("hl_done")
        ev_done = sem("ev_done")
        gt_done, hg_done, wb_done, xnt_done, log_done = (sem(n) for n in (
            "gt_done", "hg_done", "wb_done", "xnt_done", "log_done"))
        gTc_done, dlt_done, w_done, y_done, bn_done, nrm_done, xnTc_done, lg_done = (sem(n) for n in (
            "gTc_done", "dlt_done", "w_done", "y_done", "bn_done", "nrm_done", "xnTc_done", "lg_done"))
        ex_done, res_done, rstd_done, xn_ready, xn_stored = (sem(n) for n in (
            "ex_done", "res_done", "rstd_done", "xn_ready", "xn_stored"))
        last_xn_ready, warm_ready = sem("last_xn_ready"), sem("warm_ready")
        consts, dve_link, pool_link = sem("consts"), sem("dve_link"), sem("pool_link")

        LAG = 2
        NCONV = 9
        PIECES = [[0, 1], [2], [3], [4], [5], [6], [7], [8]]
        PIECES_0 = [[], [0, 1], [2, 3], [4], [5], [6], [7], [8]]
        EARLY = ["x0", "w0", "w2", "w1", "w3", "w4", "w5", "x1", "x2", "x3"]
        PRO = 3
        EARLY_OF = {0: {0: [3, 4], 1: [5], 2: [6]}, 1: {0: [7], 4: [8], 6: [9]}}
        DVE_LINKS, POOL_LINKS = 8 + 2, 2

        def conv_piece(u, i):
            half = FC // 2
            if u < 4:
                j, h = 1 - u // 2, u % 2
                src = stage[:, j, :].rearrange("p (k f) -> p k f", k=KD)[:, :, h * 512:h * 512 + 512]
                hi, lo = (ffn_w(1, 2 * j + q)[:, :, h * 512:h * 512 + 512] for q in range(2))
                return src, hi, lo, SW, j, (3 * i + 1 if j == 0 else 2 * i + 1)
            if u < 6:
                h = u - 4
                src = stage[:, 0, :].rearrange("p (c d) -> p c d", c=FC)[:, h * half:(h + 1) * half, :]
                hi, lo = (ffn_w(1, 4 + q)[:, h * half:(h + 1) * half, :] for q in range(2))
                return src, hi, lo, SW, 0, 3 * i + 2
            if u < 8:
                h = u - 6
                src = stage[:, 1, :].rearrange("p (k f) -> p k f", k=KD)[:, :, h * 512:h * 512 + 512]
                hi, lo = (w[:, :, bass.ds(i, 1), h * 512:h * 512 + 512] for w in (GUh, GUl))
                return src, hi, lo, SE, 1, 2 * i + 2
            src = stage[:, 0, 0:KE * D].rearrange("p (k d) -> p k d", k=KE)
            hi, lo = (w[:, :, bass.ds(i, 1), :] for w in (DNh, DNl))
            return src, hi, lo, SE, 0, 3 * i + 3

        def early_of(i, p):
            return EARLY_OF.get(i, {}).get(p, []) if isinstance(i, int) else []

        def early_piece(n):
            kind, u = EARLY[n][0], int(EARLY[n][1])
            if kind == "x":
                tok = slice(u * 512, u * 512 + 512)
                return xT_in[:, u], XTh[:, :, tok], XTl[:, :, tok], SX, x_in[u]
            j, h = u // 2, u % 2
            if j < 2:
                src = sW_in[:, j, :].rearrange("p (k f) -> p k f", k=KD)[:, :, h * 512:h * 512 + 512]
                hi, lo = (ffn_w(0, 2 * j + q)[:, :, h * 512:h * 512 + 512] for q in range(2))
            else:
                src = sW_in[:, j, :].rearrange("p (c d) -> p c d", c=FC)[:, h * 4:h * 4 + 4, :]
                hi, lo = (ffn_w(0, 4 + q)[:, h * 4:h * 4 + 4, :] for q in range(2))
            return src, hi, lo, SW, w_in[u]

        def flat3(ap):
            return ap.rearrange("p k e f -> p k (e f)") if len(ap.shape) == 4 else ap

        with nc.Block() as blk:
            @blk.sync
            def _(sp):
                sp.dma_start(itA[0:1, :], itokA.rearrange("(a n) -> a n", a=1)).then_inc(ids_in, 16)
                sp.dma_start(itC[0:1, :], itokC.rearrange("(a n) -> a n", a=1)).then_inc(ids_in, 16)
                def w_of(w, e):
                    return w[bass.ds(e, 1), :, :]

                def in_k(buf):
                    return stage[:, buf, :].rearrange("p (k f) -> p k f", k=KD)

                def expert_of(i):
                    return sp.value_load(itA[0:1, bass.ds(i, 1)], min_val=0, max_val=NEA - 1)

                def wi_in(i):
                    e = expert_of(i)
                    if not (isinstance(i, int) and i == 0):
                        sp.wait_ge(conv_lo, i * NCONV - 1)
                    sp.dma_start(in_k(1), w_of(Wi1, e).rearrange("e (k p) f -> p (e k) f", p=P)).then_inc(buf_in[1], 16)
                    if not (isinstance(i, int) and i == 0):
                        sp.wait_ge(conv_lo, i * NCONV)
                    sp.dma_start(in_k(0), w_of(Wi0, e).rearrange("e (k p) f -> p (e k) f", p=P)).then_inc(buf_in[0], 16)

                def more_in(i):
                    e = expert_of(i)
                    sp.wait_ge(conv_lo, i * NCONV + 2)
                    sp.dma_start(in_k(1), guT[bass.ds(i, 1), :, :].rearrange("e (k p) f -> p (e k) f", p=P)
                                 ).then_inc(buf_in[1], 16)
                    sp.wait_ge(conv_lo, i * NCONV + 4)
                    sp.dma_start(stage[:, 0, :].rearrange("p (c d) -> p c d", c=FC),
                                 w_of(Wo, e).rearrange("e (c p) d -> p (e c) d", p=P)).then_inc(buf_in[0], 16)

                xT_v = xT.rearrange("(u v) (k p) s -> u p k v s", u=4, p=P)
                def early_in(n):
                    kind, u = EARLY[n][0], int(EARLY[n][1])
                    if kind == "x":
                        for k in range(KD):
                            sp.dma_start(xT_in[:, u, k].rearrange("p (v s) -> p v s", v=2),
                                         xT_v[u, :, k]).then_inc(x_in[u], 16)
                    else:
                        j, h = u // 2, u % 2
                        if j < 2:
                            w = (sWi0, sWi1)[j].rearrange("(k p) f -> p k f", p=P)[:, :, h * 512:h * 512 + 512]
                            dst = sW_in[:, j, :].rearrange("p (k f) -> p k f", k=KD)[:, :, h * 512:h * 512 + 512]
                        else:
                            w = sWo.rearrange("(c p) d -> p c d", p=P)[:, h * 4:h * 4 + 4, :]
                            dst = sW_in[:, j, :].rearrange("p (c d) -> p c d", c=FC)[:, h * 4:h * 4 + 4, :]
                        sp.dma_start(dst, w).then_inc(w_in[u], 16)
                for n in range(7):
                    early_in(n)
                sp.wait_ge(ids_in, 32)
                wi_in(0)
                sp.dma_start(g0_sb[:, :, :], g0.rearrange("(c p) d -> p c d", p=P)).then_inc(gate_in, 16)
                sp.dma_start(g1_row, g1T.rearrange("(a j) d -> a j d", a=1)).then_inc(gate_in, 16)
                sp.dma_start(rw_sb[:, :, :], routerT.rearrange("(k p) e -> p k e", p=P)).then_inc(gate_in, 16)
                sp.dma_start(gam[:, :], gamma0.partition_broadcast(P)).then_inc(small_in, 16)
                sp.dma_start(bet[:, :], beta0.partition_broadcast(P)).then_inc(small_in, 16)

                def load_down(i):
                    sp.wait_ge(conv_lo, i * NCONV + 6)
                    sp.dma_start(stage[:, 0, 0:KE * D].rearrange("p (k d) -> p k d", k=KE),
                                 dnT[bass.ds(i, 1), :, :].rearrange("e (k p) d -> p (e k) d", p=P)).then_inc(buf_in[0], 16)

                def load_residual(g, first=False):
                    if not first:
                        sp.wait_ge(res_stored, g * 16)
                        sp.wait_ge(xn_stored, g * 16)
                    sp.dma_start(xb_sb[:, :, :], x.rearrange("b (t p) d -> p b t d", p=P)[:, bass.ds(g, 1)]
                                 ).then_inc(xb_in, 16)

                def store_xn(g):
                    sp.wait_ge(res_done, g + 1)
                    sp.dma_start(res_dram.rearrange("(b t p) d -> p b t d", t=TB, p=P)[:, bass.ds(g, 1)],
                                 xb_sb[:, :, :]).then_inc(res_stored, 16)
                    if isinstance(g, int) and g == NB - 1:
                        sp.wait_ge(last_xn_ready, 1)
                    else:
                        sp.wait_ge(xn_ready, g + 1)
                    sp.dma_start(xn_dram.rearrange("(b t p) d -> p b t d", t=TB, p=P)[:, bass.ds(g, 1)],
                                 XN[:, :, :]).then_inc(xn_stored, 16)
                load_residual(0, first=True)
                more_in(0)
                load_down(0)
                for n in range(7, len(EARLY)):
                    early_in(n)
                wi_in(1)
                more_in(1)
                load_down(1)
                with sp.Fori(2, NB) as i:
                    wi_in(i)
                    more_in(i)
                    store_xn(i - 2)
                    load_residual(i - 1)
                    load_down(i)
                store_xn(NB - 2)
                load_residual(NB - 1)
                store_xn(NB - 1)
                sp.wait_ge(xn_stored, 16 * NB)
                sp.wait_ge(res_stored, 16 * NB)

            @blk.gpsimd
            def _(pool):
                link = linker(pool, consts)
                link(nc.gpsimd.memset(ident[:, :], 0.0))
                link(nc.gpsimd.memset(ones[:, :], 1.0))
                link(nc.gpsimd.memset(tiny[:, 16:26], -0.5))
                link(nc.gpsimd.memset(ebase, float(np.e)))
                link(nc.gpsimd.memset(eps2, 1e-5))
                link(nc.gpsimd.affine_select(out=ident[:, :], in_=ident[:, :], compare_op=ALU.not_equal, fill=1.0,
                                             base=0, pattern=[[-1, P]], channel_multiplier=1))
                link(nc.gpsimd.affine_select(out=upper[:, :], in_=ones[:, :], compare_op=ALU.is_gt, fill=0.0,
                                             base=0, pattern=[[1, P]], channel_multiplier=-1))
                link(nc.gpsimd.iota(iota_row[:, :], pattern=[[1, P]], base=0, channel_multiplier=0,
                                    allow_small_or_imprecise_dtypes=True))
                link(nc.gpsimd.iota(iota_p[:, :], pattern=[[1, 1]], base=0, channel_multiplier=1,
                                    allow_small_or_imprecise_dtypes=True))
                link(nc.gpsimd.iota(rev_e[:, :], pattern=[[-1, E]], base=E, channel_multiplier=0,
                                    allow_small_or_imprecise_dtypes=True))
                assert link.n[0] == 10
                nc.gpsimd.tensor_copy(upper_h[:, :], upper[:, :])
                nc.gpsimd.tensor_copy(ones_h[:, :], ones[:, :]).then_inc(warm_ready, 1)
                pool.wait_ge(small_in, 32)

                def gate(g):
                    lk = linker(pool, pool_link, g * POOL_LINKS)
                    pool.wait_ge(dlt_done, g + 1)
                    nc.gpsimd.tensor_tensor(ex2, ebase, dl2, ALU.pow).then_inc(ex_done, 1)
                    pool.wait_ge(y_done, g + 1)
                    pool.wait_ge(xb_in, g * 16 + 16)
                    xb = xb_sb[:, :, :]
                    nc.gpsimd.tensor_tensor(xb, xb, XN[:, :, :], ALU.add).then_inc(res_done, 1)
                    pool.wait_ge(bn_done, g + 1)
                    lk(nc.gpsimd.tensor_tensor(vpe, mv[:, :, 1], eps2, ALU.add))
                    nc.gpsimd.tensor_tensor(rstd, vpe, mhalf, ALU.pow).then_inc(rstd_done, 1)
                    if isinstance(g, int) and g == NB - 1:
                        return
                    pool.wait_ge(nrm_done, g + 1)
                    gb = gam[:, :].unsqueeze(1).to_broadcast([P, TB, D])
                    bb = bet[:, :].unsqueeze(1).to_broadcast([P, TB, D])
                    lk(nc.gpsimd.tensor_tensor(XN[:, :, :], XN[:, :, :], gb, ALU.mult))
                    nc.gpsimd.tensor_tensor(XN[:, :, :], XN[:, :, :], bb, ALU.add).then_inc(xn_ready, 1)
                    assert lk.n[0] == POOL_LINKS
                gate(0)
                with pool.Fori(1, NB - 1) as g:
                    gate(g)
                gate(NB - 1)

            @blk.scalar
            def _(act):
                def early(n):
                    src, hi, lo, scale, arrived = early_piece(n)
                    act.wait_ge(arrived, 32 if arrived in x_in else 16)
                    nc.scalar.activation(hi, src, ACT.Copy, scale=scale).then_inc(early_hi, 1)

                def iteration(i):
                    first = isinstance(i, int) and i == 0
                    for p in range(NP):
                        n = i * NP + p
                        q = p % 2
                        act.wait_ge(up_done, n + 1)
                        if not (first and p == 0):
                            act.wait_ge(h_done, n)
                        nc.scalar.activation(gelu_g[:, :, :], pG[q][:, :].rearrange("p (c s) -> p c s", c=2),
                                             ACT.Gelu_apprx_tanh, scale=1.0 / (SX * SW)).then_inc(gelu_done, 1)
                        for m in early_of(i, p):
                            early(m)
                        for u in (PIECES_0 if first else PIECES)[p]:
                            src, hi, lo, scale, b, loads = conv_piece(u, i)
                            act.wait_ge(buf_in[b], loads * 16)
                            if u == 0 and not first:
                                act.wait_ge(up_done, i * NP)
                            if u == 4 and not first:
                                act.wait_ge(dn_done, i * NP)
                            if u == 6 and first:
                                act.wait_ge(early_lo, 7)
                            nc.scalar.activation(hi, src, ACT.Copy, scale=scale).then_inc(conv_hi, 1)
                        act.wait_ge(h_done, n + 1)
                        if not (first and p < 2):
                            act.wait_ge(dn_done, n - 1)
                        nc.scalar.activation(hid_hl[:, q, 0], hid[:, :, :], ACT.Copy).then_inc(hh_done, 1)
                act.wait_ge(consts, 2)
                nc.scalar.activation(tiny[:, 52:53], ones[:, 0:1], ACT.Gelu_apprx_tanh)
                for n in range(PRO):
                    early(n)
                iteration(0)
                iteration(1)
                with act.Fori(2, NB) as i:
                    iteration(i)
                nc.scalar.activation(tiny[:, 52:53], ones[:, 0:1], ACT.Exp)

            @blk.vector
            def _(dve):
                held = dve.alloc_register("held_dve")
                def early(n):
                    src, hi, lo, scale, arrived = early_piece(n)
                    dve.wait_ge(early_hi, n + 1)
                    nc.vector.scalar_tensor_tensor(lo, src, scale, hi, ALU.mult, ALU.subtract).then_inc(early_lo, 1)
                for n in range(PRO):
                    early(n)

                def evac(dst, count):
                    dve.wait_ge(dn_done, count)
                    nc.vector.tensor_scalar(dst[:, :, :], pD[:, :, 0:D], 1.0 / (SH * SW), None,
                                            ALU.mult).then_inc(ev_done, 1)

                def gate(slot, g, lk):
                    if slot == 1:
                        dve.wait_ge(gt_done, g + 1)
                        nc.vector.tensor_copy(gT, pR[:, 0:4]).then_inc(gTc_done, 1)
                    if slot == 2:
                        dve.wait_ge(hg_done, g + 1)
                        for j in range(2):
                            lk(nc.vector.scalar_tensor_tensor(junk_row, pR[0:1, 0:D], 0.0, g1_row[:, j, :],
                                                              ALU.max, ALU.mult, accum_out=logit2[:, j:j + 1]))
                        lk(nc.vector.tensor_reduce(mx1, logit2, AX, ALU.max))
                        nc.vector.tensor_scalar(dl2, logit2, mx1, None, ALU.subtract).then_inc(dlt_done, 1)
                    if slot == 3:
                        dve.wait_ge(ex_done, g + 1)
                        lk(nc.vector.tensor_reduce(sm1, ex2, AX, ALU.add))
                        lk(nc.vector.reciprocal(rs1, sm1))
                        nc.vector.tensor_scalar(w2row, ex2, rs1, None, ALU.mult).then_inc(w_done, 1)
                    if slot == 4:
                        dve.wait_ge(wb_done, g + 1)
                        lk(nc.vector.tensor_copy(wbc, pR[:, 0:2]))
                        lk(nc.vector.tensor_scalar(S_out[:, :, :], S_out[:, :, :], wbc[:, 1:2], None, ALU.mult))
                        dve.wait_ge(xb_in, g * 16 + 16)
                        nc.vector.scalar_tensor_tensor(XN[:, :, :], E_out[:, :, :], wbc[:, 0:1], S_out[:, :, :],
                                                       ALU.mult, ALU.add).then_inc(y_done, 1)
                    if slot == 5:
                        dve.wait_ge(y_done, g + 1)
                        lk(nc.vector.bn_stats(bst[:, 0, :], XN[:, 0, :]))
                        lk(nc.vector.bn_stats(bst[:, 1, :], XN[:, 1, :]), held, (consts, 10))
                        lk(nc.vector.bn_aggr(mv[:, 0, :], bst[:, 0, :]), held, (consts, 10))
                        nc.vector.bn_aggr(mv[:, 1, :], bst[:, 1, :]).then_inc(bn_done, 1)
                    if slot == 6:
                        dve.wait_ge(rstd_done, g + 1)
                        dve.wait_ge(res_done, g + 1)
                        dve.wait_ge(bn_done, g + 1)
                        for t in range(TB):
                            r = nc.vector.tensor_scalar(XN[:, t, :], XN[:, t, :], mv[:, t, 0:1], rstd[:, t:t + 1],
                                                        ALU.subtract, ALU.mult)
                        r.then_inc(nrm_done, 1)
                        if isinstance(g, int) and g == NB - 1:
                            dve.wait_ge(nrm_done, NB)
                            gb = gam[:, :].unsqueeze(1).to_broadcast([P, TB, D])
                            bb = bet[:, :].unsqueeze(1).to_broadcast([P, TB, D])
                            lk(nc.vector.tensor_tensor(XN[:, :, :], XN[:, :, :], gb, ALU.mult))
                            nc.vector.tensor_tensor(XN[:, :, :], XN[:, :, :], bb, ALU.add).then_inc(last_xn_ready, 1)
                    if slot == 7:
                        dve.wait_ge(xnt_done, g + 1)
                        nc.vector.tensor_copy(xnT[:, :, :], pM[:, :].rearrange("p (k s) -> p k s", k=KD)
                                              ).then_inc(xnTc_done, 1)
                    if slot == 8:
                        dve.wait_ge(log_done, g + 1)
                        nc.vector.tensor_scalar(LG[:, bass.ds(g * TB, TB), :],
                                                pM[:, 0:TB * E].rearrange("p (t e) -> p t e", t=TB),
                                                1e4, -1e4, ALU.min, ALU.max).then_inc(lg_done, 1)

                def iteration(i):
                    first = isinstance(i, int) and i == 0
                    second = isinstance(i, int) and i == 1
                    lk = linker(dve, dve_link, (i - 1) * DVE_LINKS)
                    for p in range(NP):
                        n = i * NP + p
                        q = p % 2
                        if p == LAG and not first:
                            evac(E_out, i * NP)
                        dve.wait_ge(gelu_done, n + 1)
                        if not (first and p == 0):
                            dve.wait_ge(hl_done, n)
                        nc.vector.scalar_tensor_tensor(hid[:, :, :], pL[q][:, :].rearrange("p (c s) -> p c s", c=2),
                                                       SH / (SX * SW), gelu_g[:, :, :],
                                                       ALU.mult, ALU.mult).then_inc(h_done, 1)
                        if p == 4 and not first:
                            gate(3, i - 1, lk)
                        if p == 5 and not first:
                            gate(4, i - 1, lk)

                        def split():
                            dve.wait_ge(hh_done, n + 1)
                            nc.vector.tensor_tensor(hid_hl[:, q, 1], hid[:, :, :], hid_hl[:, q, 0],
                                                    ALU.subtract).then_inc(hl_done, 1)
                        if p == PAIRS + 1:
                            if not first:
                                dve.wait_ge(y_done, i)
                            evac(S_out, i * NP + PAIRS)
                            split()
                        for m in early_of(i, p):
                            early(m)
                        for u in (PIECES_0 if first else PIECES)[p]:
                            src, hi, lo, scale, b, loads = conv_piece(u, i)
                            dve.wait_ge(conv_hi, i * NCONV + u + 1)
                            nc.vector.scalar_tensor_tensor(flat3(lo), src, scale, flat3(hi),
                                                           ALU.mult, ALU.subtract).then_inc(conv_lo, 1)
                        if p != PAIRS + 1:
                            split()
                        if not first:
                            if p in SLOTS_OF_LAST:
                                gate(SLOTS_OF_LAST[p], i - 1, lk)
                            if p in SLOTS_BEFORE and not second:
                                gate(SLOTS_BEFORE[p], i - 2, lk)
                SLOTS_OF_LAST = {2: 1, 3: 2, 6: 5, 7: 6}
                SLOTS_BEFORE = {2: 7, 4: 8}
                iteration(0)
                dve.wait_ge(gate_in, 48)
                dve.wait_ge(consts, 10)
                iteration(1)
                with dve.Fori(2, NB) as i:
                    iteration(i)
                evac(E_out, NB * NP)
                lk = linker(dve, dve_link, (NB - 1) * DVE_LINKS)
                gate(1, NB - 1, lk)
                gate(7, NB - 2, lk)
                gate(2, NB - 1, lk)
                gate(8, NB - 2, lk)
                for slot in range(3, 9):
                    gate(slot, NB - 1, lk)

            @blk.tensor
            def _(pe):
                held = pe.alloc_register("held_pe")

                def up(i, p):
                    q, s = p % 2, p // PAIRS
                    n = i * NP + p
                    if not (isinstance(i, int) and i == 0 and p < 2):
                        pe.wait_ge(h_done, n - 1)
                    if p == PAIRS:
                        pe.wait_ge(conv_lo, i * NCONV + 4)
                    tok = bass.ds(i * S, S)
                    for c in range(2):
                        f = slice((2 * (p % PAIRS) + c) * P, (2 * (p % PAIRS) + c + 1) * P)
                        for bank, j in ((pG[q], 0), (pL[q], 2)):
                            o = bank[:, c * S:(c + 1) * S]
                            wh, wl = ffn_w(s, j), ffn_w(s, j + 1)
                            for k in range(KD):
                                nc.tensor.matmul(o, wh[:, k, f], XTh[:, k, tok], start=(k == 0), stop=False)
                                nc.tensor.matmul(o, wh[:, k, f], XTl[:, k, tok], start=False, stop=False)
                                last = nc.tensor.matmul(o, wl[:, k, f], XTh[:, k, tok], start=False,
                                                        stop=(k == KD - 1))
                    last.then_inc(up_done, 1)

                def down(i, p):
                    q, s = p % 2, p // PAIRS
                    n = i * NP + p
                    pe.wait_ge(hl_done, n + 1)
                    if p == 0 and not (isinstance(i, int) and i == 0):
                        pe.wait_ge(ev_done, i * 2)
                    if p == PAIRS:
                        pe.wait_ge(ev_done, i * 2 + 1)
                        pe.wait_ge(conv_lo, i * NCONV + 6)
                    woh, wol = ffn_w(s, 4), ffn_w(s, 5)
                    for t in range(TB):
                        ts = slice(t * P, (t + 1) * P)
                        for c in range(2):
                            f = 2 * (p % PAIRS) + c
                            hh, hl = hid_hl[:, q, 0, c, ts], hid_hl[:, q, 1, c, ts]
                            nc.tensor.matmul(pD[:, t, 0:D], hh, woh[:, f, :],
                                             start=(p % PAIRS == 0 and c == 0), stop=False)
                            nc.tensor.matmul(pD[:, t, 0:D], hh, wol[:, f, :], start=False, stop=False)
                            last = nc.tensor.matmul(pD[:, t, 0:D], hl, woh[:, f, :], start=False,
                                                    stop=(p % PAIRS == PAIRS - 1 and c == 1))
                    last.then_inc(dn_done, 1)

                def gate(step, g):
                    if step == "columns":
                        hold(pe, held, ev_done, g * 2 + 2, (warm_ready, 1))
                        for c in range(2 * KD):
                            src = (E_out if c < KD else S_out)[0:1, 0, (c % KD) * P:(c % KD + 1) * P]
                            last = nc.tensor.transpose(pR[:, c:c + 1], src, ident[0:1, 0:1])
                        last.then_inc(gt_done, 1)
                    if step == "hidden":
                        pe.wait_ge(gTc_done, g + 1)
                        for c in range(2 * KD):
                            last = nc.tensor.matmul(pR[0:1, 0:D], gT[:, c:c + 1], g0_sb[:, c, :],
                                                    start=(c == 0), stop=(c == 2 * KD - 1))
                        last.then_inc(hg_done, 1)
                    if step == "weights":
                        pe.wait_ge(w_done, g + 1)
                        nc.tensor.matmul(pR[:, 0:2], ones[0:1, :], w2row, start=True, stop=True).then_inc(wb_done, 1)
                    if step == "transpose":
                        if isinstance(g, int) and g == NB - 1:
                            pe.wait_ge(last_xn_ready, 1)
                        else:
                            pe.wait_ge(xn_ready, g + 1)
                        for t in range(TB):
                            for k in range(KD):
                                last = nc.tensor.transpose(pM[:, k * S + t * P:k * S + (t + 1) * P],
                                                           XN[:, t, k * P:(k + 1) * P], ident[:, :])
                        last.then_inc(xnt_done, 1)
                    if step == "logits":
                        pe.wait_ge(xnTc_done, g + 1)
                        for t in range(TB):
                            for k in range(KD):
                                last = nc.tensor.matmul(pM[:, t * E:(t + 1) * E], xnT[:, k, t * P:(t + 1) * P],
                                                        rw_sb[:, k, :], start=(k == 0), stop=(k == KD - 1))
                        last.then_inc(log_done, 1)

                def iteration(i):
                    first = isinstance(i, int) and i == 0
                    second = isinstance(i, int) and i == 1
                    for p in range(NP):
                        if first and p in (0, 2):
                            pe.wait_ge(early_lo, PRO + 2 * (p // 2))
                        up(i, p)
                        if p == 5 and not first:
                            gate("weights", i - 1)
                        if p >= LAG:
                            if first and p - LAG in (0, 2):
                                pe.wait_ge(early_lo, PRO + 3 + (p - LAG) // 2)
                            down(i, p - LAG)
                        elif not first:
                            down(i - 1, NP - LAG + p)
                        if not first:
                            if p in GATE_OF_LAST:
                                gate(GATE_OF_LAST[p], i - 1)
                            if p in GATE_BEFORE and not second:
                                gate(GATE_BEFORE[p], i - 2)
                GATE_OF_LAST = {2: "columns", 3: "hidden"}
                GATE_BEFORE = {1: "transpose", 3: "logits"}
                pe.wait_ge(warm_ready, 1)
                keep_warm(pe, pM, 14)
                iteration(0)
                pe.wait_ge(gate_in, 48)
                iteration(1)
                pe.wait_ge(early_lo, len(EARLY))
                with pe.Fori(2, NB) as i:
                    iteration(i)
                for p in range(LAG):
                    down(NB - 1, NP - LAG + p)
                gate("columns", NB - 1)
                gate("transpose", NB - 2)
                gate("hidden", NB - 1)
                gate("logits", NB - 2)
                gate("weights", NB - 1)
                keep_warm(pe, pG[1], 20)
                gate("transpose", NB - 1)
                gate("logits", NB - 1)
        NA = TOPK * NT
        ACH = 8
        onehot_slot = xt_area[:, :].bitcast(F32).rearrange("p (a m) -> p a m", a=NA)
        blk_vals = ffn_area[:, 12 * nw // 2:12 * nw // 2 + 2 * NA * 3 * NBLK].bitcast(F32).rearrange(
            "p (a v j) -> p a v j", a=NA, v=3)
        work = stage[:, :, :].rearrange("p a b -> p (a b)")
        NTE = NT * E

        def tile_of(n, dt=F32):
            v = work[:, n * NTE:(n + 1) * NTE]
            return v if dt == F32 else v.bitcast(dt)

        def te(ap):
            return ap.rearrange("p (t e) -> p t e", e=E)

        d_t, ex_t, p_t, eq_t, oh = te(tile_of(0)), te(tile_of(1)), te(tile_of(2)), te(tile_of(3)), [
            te(tile_of(4)), te(tile_of(5))]
        oh2 = work[:, 4 * NTE:6 * NTE].rearrange("p (r t e) -> p r t e", r=TOPK, e=E)
        at2 = work[:, 7 * NTE:9 * NTE].rearrange("p (r t e) -> p r t e", r=TOPK, e=E)
        M_h = tile_of(6).bitcast(BF16)[:, 0:NTE]
        pos_t = te(tile_of(9))
        before = tile_of(10)[:, 0:E * E].rearrange("p (a b) -> p a b", a=E)
        nb_before = tile_of(19)[:, 0:E * E].rearrange("p (a b) -> p a b", a=E)
        sm = tile_of(11)
        m16, s16, r16 = sm[:, 0:NT], sm[:, NT:2 * NT], sm[:, 2 * NT:3 * NT]
        gate2 = sm[:, 64:64 + NA].rearrange("p (r t) -> p r t", r=TOPK)
        k16 = sm[:, 3 * NT:4 * NT]
        sn = tile_of(12)
        nb_f, start_f = sn[:, 0:E], sn[:, 2 * E:3 * E]
        bend = sn[:, 3 * E:4 * E]
        nb_i = tile_of(13, I32)[:, 0:E]
        POS = tile_of(14)[:, 0:NA]
        pos_i, blk_i = (tile_of(15, I32)[:, n * NA:(n + 1) * NA] for n in range(2))
        blk_f, row_f, dest_f = (tile_of(16)[:, n * NA:(n + 1) * NA] for n in range(3))
        tab = work[:, 17 * NTE:17 * NTE + 3 * NBLK].rearrange("p (v j) -> p v j", v=3)
        un_t = tile_of(18)[:, 0:NBLK]
        pad_row = tile_of(18)[:, 64:64 + NBLK]
        be_cmp = work[0:1, 20 * NTE:20 * NTE + NBLK * E].rearrange("p (j e) -> p j e", e=E)
        be_f = work[0:1, 23 * NTE:23 * NTE + NBLK]
        dest_i = xb_sb[:, 0, 0:NBLK].bitcast(I32)
        tok_i = xb_sb[:, 0, 64:64 + NBLK].bitcast(I32)
        gate_silu = xb_sb[:, 0, 128:128 + NBLK]
        gate_up_s = xb_sb[:, 0, 192:192 + NBLK]
        be_i = xb_sb[0:1, 1, 0:NBLK].bitcast(I32)
        tok_col = xb_sb[:, 1, 64:64 + UNR].bitcast(I32)
        dest_col = xb_sb[:, 1, 80:80 + UNR].bitcast(I32)

        shift_done, exp_done, mask_done, prefix_done, slots_done, table_done, dest_ready = (
            sem(n) for n in ("shift_done", "exp_done", "mask_done", "prefix_done", "slots_done",
                             "table_done", "dest_ready"))
        route_link = sem("route_link")

        def over_e(ap):
            return ap.unsqueeze(2).to_broadcast([P, NT, E])

        def over_t(ap):
            return ap.unsqueeze(1).to_broadcast([P, NT, E])

        with nc.Block() as blk:
            @blk.gpsimd
            def _(pool):
                nc.gpsimd.iota(pad_row, pattern=[[P, NBLK]], base=TOPK * TOK, channel_multiplier=1,
                               allow_small_or_imprecise_dtypes=True).then_inc(dest_ready, 1)
                nc.gpsimd.iota(dest_f, pattern=[[TOK, TOPK], [P, NT]], base=0, channel_multiplier=1,
                               allow_small_or_imprecise_dtypes=True).then_inc(dest_ready, 1)

            @blk.scalar
            def _(act):
                act.wait_ge(shift_done, 1)
                nc.scalar.activation(ex_t, d_t, ACT.Exp).then_inc(exp_done, 1)
                nc.scalar.activation(tiny[:, 52:53], iota_p[:, :], ACT.Silu)

            @blk.vector
            def _(dve):
                lk = linker(dve, route_link)
                v = nc.vector
                lk(v.tensor_reduce(m16, LG[:, :, :], AX, ALU.max))
                v.tensor_tensor(d_t, LG[:, :, :], over_e(m16), ALU.subtract).then_inc(shift_done, 1)
                shape = [P, E, E]
                lk(v.tensor_tensor(before, rev_e[:, :].unsqueeze(1).to_broadcast(shape),
                                   rev_e[:, :].unsqueeze(2).to_broadcast(shape), ALU.is_gt))
                dve.wait_ge(exp_done, 1)
                lk(v.tensor_reduce(s16, ex_t, AX, ALU.add))
                lk(v.tensor_scalar(s16, s16, 1e-8, None, ALU.add))
                lk(v.reciprocal(r16, s16))
                lk(v.tensor_tensor(p_t, ex_t, over_e(r16), ALU.mult))
                lk(v.tensor_scalar(p_t, p_t, 1e-8, 1.0, ALU.max, ALU.min))
                for r in range(TOPK):
                    lk(v.tensor_reduce(gate2[:, r, :], p_t, AX, ALU.max))
                    lk(v.tensor_tensor(eq_t, p_t, over_e(gate2[:, r, :]), ALU.is_equal))
                    lk(v.tensor_tensor(eq_t, eq_t, over_t(rev_e[:, :]), ALU.mult))
                    lk(v.tensor_reduce(k16, eq_t, AX, ALU.max))
                    lk(v.tensor_tensor(oh[r], over_t(rev_e[:, :]), over_e(k16), ALU.is_equal))
                    if r == 0:
                        lk(v.scalar_tensor_tensor(p_t, oh[0], -4.0, p_t, ALU.mult, ALU.add))
                v.tensor_tensor(te(M_h), oh[0], oh[1], ALU.add).then_inc(mask_done, 1)
                dve.wait_ge(prefix_done, 1)
                lk(v.tensor_scalar(nb_i, pL[0][:, 0:E], float(P - 1), None, ALU.add))
                lk(v.tensor_scalar(nb_i, nb_i, 7, None, ALU.logical_shift_right))
                lk(v.tensor_copy(nb_f, nb_i))
                lk(v.tensor_tensor(nb_before, before, nb_f.unsqueeze(1).to_broadcast([P, E, E]), ALU.mult))
                lk(v.tensor_reduce(start_f, nb_before, AX, ALU.add))
                lk(v.scalar_tensor_tensor(pos_t, over_t(start_f), float(P), te(pG[0][:, 0:NTE]), ALU.mult, ALU.add))
                lk(v.tensor_tensor(at2, oh2, pos_t.unsqueeze(1).to_broadcast([P, TOPK, NT, E]), ALU.mult))
                lk(v.tensor_reduce(POS.rearrange("p (r t) -> p r t", r=TOPK), at2, AX, ALU.add))
                lk(v.tensor_copy(pos_i, POS))
                lk(v.tensor_scalar(blk_i, pos_i, 7, None, ALU.logical_shift_right))
                lk(v.tensor_copy(blk_f, blk_i))
                dve.wait_ge(dest_ready, 2)
                lk(v.scalar_tensor_tensor(row_f, blk_f, -float(P), POS, ALU.mult, ALU.add))
                for a in range(0, NA, ACH):
                    part = slice(a, a + ACH)
                    shape = [P, ACH, NBLK]
                    lk(v.tensor_tensor(blk_vals[:, part, 2, :], iota_row[:, 0:NBLK].unsqueeze(1).to_broadcast(shape),
                                       blk_f[:, part].unsqueeze(2).to_broadcast(shape), ALU.is_equal))
                    v.tensor_tensor(blk_vals[:, part, 0, :], blk_vals[:, part, 2, :],
                                    dest_f[:, part].unsqueeze(2).to_broadcast(shape), ALU.mult)
                    v.tensor_tensor(blk_vals[:, part, 1, :], blk_vals[:, part, 2, :],
                                    sm[:, 64:64 + NA][:, part].unsqueeze(2).to_broadcast(shape), ALU.mult)
                    shape = [P, ACH, P]
                    v.tensor_tensor(onehot_slot[:, part, :], iota_row[:, :].unsqueeze(1).to_broadcast(shape),
                                    row_f[:, part].unsqueeze(2).to_broadcast(shape),
                                    ALU.is_equal).then_inc(slots_done, 1)
                shape = [1, NBLK, E]
                lk(v.tensor_tensor(bend, start_f, nb_f, ALU.add))
                lk(v.tensor_tensor(be_cmp, bend[0:1, :].unsqueeze(1).to_broadcast(shape),
                                   iota_row[0:1, 0:NBLK].unsqueeze(2).to_broadcast(shape), ALU.is_le))
                lk(v.tensor_reduce(be_f, be_cmp, AX, ALU.add))
                lk(v.tensor_scalar(be_i, be_f, float(E - 1), None, ALU.min))
                dve.wait_ge(table_done, 1)
                lk(v.tensor_copy(tab, pR[:, 0:3 * NBLK].rearrange("p (v j) -> p v j", v=3)))
                lk(v.tensor_scalar(un_t, tab[:, 2, :], -1.0, 1.0, ALU.mult, ALU.add))
                lk(v.tensor_tensor(un_t, un_t, pad_row, ALU.mult))
                lk(v.tensor_tensor(dest_i, tab[:, 0, :], un_t, ALU.add))
                lk(v.tensor_scalar(tok_i, dest_i, TOK - 1, None, ALU.bitwise_and))
                lk(v.tensor_scalar(gate_silu, tab[:, 1, :], 1.0 / (SN * SE), None, ALU.mult))
                lk(v.tensor_scalar(gate_up_s, tab[:, 1, :], SHE / (SN * SE), None, ALU.mult))

            @blk.tensor
            def _(pe):
                keep_warm(pe, pG[1], 30)
                pe.wait_ge(mask_done, 1)
                nc.tensor.matmul(pG[0][:, 0:NTE], upper_h[:, :], M_h, start=True, stop=False, skip_group_check=True)
                for t in range(1, NT):
                    nc.tensor.matmul(pG[0][:, t * E:NTE], ones_h[:, :], M_h[:, 0:NTE - t * E], start=False,
                                     stop=(t == NT - 1), skip_group_check=True)
                for t in range(NT):
                    last = nc.tensor.matmul(pL[0][:, 0:E], ones_h[:, :], M_h[:, t * E:(t + 1) * E],
                                            start=(t == 0), stop=(t == NT - 1))
                last.then_inc(prefix_done, 1)
                keep_warm(pe, pM, 14)
                for a in range(NA):
                    if a % ACH == 0:
                        pe.wait_ge(slots_done, a // ACH + 1)
                    last = nc.tensor.matmul(pR[:, 0:3 * NBLK], onehot_slot[:, a, :],
                                            blk_vals[:, a].rearrange("p v j -> p (v j)"),
                                            start=(a == 0), stop=(a == NA - 1))
                last.then_inc(table_done, 1)
                keep_warm(pe, pM, 6)

        mix = ffn_area[:, 0:12 * nw // 2].bitcast(F32)
        xg = [mix[:, u * D:(u + 1) * D] for u in range(UNR)]
        orow = [mix[:, (UNR + u) * D:(UNR + u + 1) * D] for u in range(UNR)]
        sg = gelu_g[:, :, :].rearrange("p c s -> p (c s)")
        hm = hid[:, :, :].rearrange("p c s -> p (c s)")
        xgT = S_out[:, :, :].rearrange("p t d -> p (t d)").bitcast(F16).rearrange(
            "p (h k s) -> p h k s", h=4, k=KD)
        hT = hid_hl[:, 0].rearrange("p h c s -> p h (c s)").rearrange("p h (k s) -> p h k s", k=KE)
        pX, pH = pG[1], pL[1]
        xg_in, moe_stored = [sem(f"xg_in{u}") for u in range(UNR)], [sem(f"moe_stored{u}") for u in range(UNR)]
        xt_done, xh_done, xl_done, gu_done, silu_done, hm_done, ht_done, hth_done, htl_done, dnb_done, out_ready = (
            sem(n) for n in ("xt_done", "xh_done", "xl_done", "gu_done", "silu_done", "hm_done", "ht_done",
                             "hth_done", "htl_done", "dnb_done", "out_ready"))
        mix_link = sem("mix_link")
        NI = NBLK // UNR

        adapt = ffn_area[:, :].bitcast(F32)
        base = 2 * UNR * D
        per = KD * A + D + 2 * KD
        aRows = adapt[:, base:base + NB * per].rearrange("p (b v) -> p b v", b=NB)
        aW1 = aRows[:, :, 0:KD * A].rearrange("p b (k a) -> p b k a", k=KD)
        aW2 = aRows[0:A + 1, :, KD * A:KD * A + D]
        aGam = aRows[:, :, KD * A + D:KD * A + D + KD]
        aBet = aRows[:, :, KD * A + D + KD:per]
        base += NB * per
        aB1 = adapt[0:A, base:base + NB]
        base += NB
        RB = 4
        rr = adapt[:, base:base + RB * TOPK * TB * D].rearrange("p (q r t d) -> p q r t d", q=RB, r=TOPK, t=TB)
        base += RB * TOPK * TB * D
        x2T = adapt[:, base:base + KD * S].rearrange("p (k s) -> p k s", k=KD)
        base += KD * S
        aH = adapt[0:A + 1, base:base + S]
        assert base + S <= 12 * nw // 2, (base + S, 12 * nw // 2)
        X = stage[:, :, :].rearrange("p a b -> p (a b)").rearrange("p (n d) -> p n d", n=NT)
        w1_in = xt_area[:, 0:2 * KD * F].bitcast(F32).rearrange("p (k f) -> p k f", k=KD)
        w2_in = xt_area[:, 2 * KD * F:].bitcast(F32).rearrange("p (c d) -> p c d", c=FC)
        b1_sb = tiny[:, 44:44 + FC]
        b2_sb = gam[:, :]
        adapt_in, ffn1_in = sem("adapt_in"), sem("ffn1_in")
        FFN1_LOADS = 16 * (KD + 2 + 2 + NB)
        rows_in = [sem(f"rows_in{q}") for q in range(RB)]
        one_row = sem("one_row")
        rank_rows = moe_dram[0:TOPK * TOK, :].rearrange("(r b t p) d -> p b r t d", r=TOPK, t=TB, p=P)

        def load_rows(sp, b):
            for r in range(TOPK):
                sp.dma_start(rr[:, b % RB, r], rank_rows[:, b, r]).then_inc(rows_in[b % RB], 16)
        wq_link, wt_ready, wt_done, wd_ready, wd_done, w_scaled = (sem(n) for n in (
            "wq_link", "wt_ready", "wt_done", "wd_ready", "wd_done", "w_scaled"))
        stats = sb("stats", [P, 6 * NT])
        mv_all = sb("mv_all", [P, 2 * NT])
        mvv = mv_all[:, :].rearrange("p (n s) -> p n s", s=2)
        rstd_all = sb("rstd_all", [P, 2 * NT])
        nmr_all = rstd_all[:, NT:]
        amax = sb("amax", [P, 2 * NB + 2])
        spread = sb("spread", [P, 64])
        wmax, wtop, wdiag, wall = spread[:, 0:2], spread[0:2, 2:3], spread[0:2, 4:6], spread[:, 6:8]
        wstep, winv = spread[:, 8:10], spread[:, 10:12]
        xmax, xtop, xdiag, xall, xstep, xinv = (spread[:, 12 + n:13 + n] for n in range(6))
        hmax, htop, hdiag, hall, hstep, hinv = (spread[:, 18 + n:19 + n] for n in range(6))
        s1, s2, b1s = spread[:, 24:25], spread[:, 25:26], spread[:, 32:32 + FC]
        pW = pM
        w1q = g0_sb[:, :, :].rearrange("p c d -> p (c d)").bitcast(BF16).rearrange("p (k f) -> p k f", k=KD)
        w2q = [t[:, :, :].rearrange("p t d -> p (t d)").bitcast(BF16).rearrange("p (c d) -> p c d", d=D)
               for t in (E_out, XN)]

        def top_of(dve, link, bank, n, top, diag, t_done, d_ready):
            dve.wait_ge(t_done, 1)
            link(nc.vector.tensor_reduce(top, bank[0:n, 0:P], AX, ALU.max))
            nc.vector.tensor_scalar(diag, ident[0:n, 0:n], top, None, ALU.mult).then_inc(d_ready, 1)

        def step_of(dve, link, bank, n, full, step, inv, d_done):
            dve.wait_ge(d_done, 1)
            link(nc.vector.tensor_copy(full, bank[:, P:P + n]))
            link(nc.vector.tensor_scalar(step, full, 1e-6, 1.0 / 127.0, ALU.max, ALU.mult))
            link(nc.vector.reciprocal(inv, step))

        def turn_max(pe, part, bank, n, t_ready, t_done):
            pe.wait_ge(t_ready, 1)
            nc.tensor.transpose(bank[0:n, 0:P], part, ident[:, :]).then_inc(t_done, 1)

        def spread_max(pe, diag, bank, n, d_ready, d_done):
            pe.wait_ge(d_ready, 1)
            nc.tensor.matmul(bank[:, P:P + n], ones[0:n, :], diag, start=True, stop=True).then_inc(d_done, 1)


        with nc.Block() as blk:
            @blk.gpsimd
            def _(pool):
                held = pool.alloc_register("held_pool")
                def gather(i, u, links, wait=True):
                    j = i * UNR + u
                    if wait:
                        pool.wait_ge(xt_done, j - UNR + 1)
                    nc.gpsimd.tensor_copy(tok_col[:, u:u + 1], tok_i[:, bass.ds(j, 1)]).then_inc(mix_link, 1)
                    hold(pool, held, mix_link, links, (consts, 10))
                    nc.gpsimd.indirect_dma_start(xg[u], None, xn_dram, bass.IndirectOffsetOnAxis(
                        ap=tok_col[:, u:u + 1], axis=0)).then_inc(xg_in[u], 16)

                def scatter(i, u, links):
                    j = i * UNR + u
                    if not (isinstance(i, int) and i == 0):
                        pool.wait_ge(moe_stored[u], i * 16)
                    nc.gpsimd.tensor_copy(dest_col[:, u:u + 1], dest_i[:, bass.ds(j, 1)]).then_inc(mix_link, 1)
                    pool.wait_ge(mix_link, links)
                    hold(pool, held, out_ready, j + 1, (consts, 10))
                    nc.gpsimd.indirect_dma_start(moe_dram, bass.IndirectOffsetOnAxis(
                        ap=dest_col[:, u:u + 1], axis=0), orow[u], None).then_inc(moe_stored[u], 16)
                for u in range(UNR):
                    gather(0, u, u + 1, wait=False)
                for u in range(UNR):
                    gather(1, u, UNR + 2 * u + 1)
                    scatter(0, u, UNR + 2 * u + 2)
                with pool.Fori(1, NI - 1) as i:
                    for u in range(UNR):
                        gather(i + 1, u, UNR + i * 2 * UNR + 2 * u + 1)
                        scatter(i, u, UNR + i * 2 * UNR + 2 * u + 2)
                for u in range(UNR):
                    scatter(NI - 1, u, UNR + (NI - 1) * 2 * UNR + u + 1)
                nc.gpsimd.memset(aH[A:A + 1, :], 1.0).then_inc(one_row, 1)
                pool.wait_ge(one_row, 1)

            @blk.scalar
            def _(act):
                def split_x(j):
                    act.wait_ge(xt_done, j + 1)
                    nc.scalar.activation(xgT[:, 0], pX[:, 0:D].rearrange("p (k s) -> p k s", k=KD), ACT.Copy,
                                         scale=SN).then_inc(xh_done, 1)

                def block(j, last=False):
                    act.wait_ge(gu_done, 2 * j + 1)
                    nc.scalar.activation(sg, pG[0][:, :], ACT.Silu,
                                         scale=gate_silu[:, bass.ds(j, 1)]).then_inc(silu_done, 1)
                    if not last:
                        split_x(j + 1)
                    act.wait_ge(ht_done, j + 1)
                    nc.scalar.activation(hT[:, 0], pH[:, :].rearrange("p (k s) -> p k s", k=KE),
                                         ACT.Copy).then_inc(hth_done, 1)
                split_x(0)
                for u in range(UNR):
                    block(u)
                with act.Fori(1, NI - 1) as i:
                    for u in range(UNR):
                        block(i * UNR + u)
                for u in range(UNR):
                    block((NI - 1) * UNR + u, last=(u == UNR - 1))
                act.wait_ge(w_scaled, 1)
                nc.scalar.activation(w1q, w1_in, ACT.Copy, bias=-MAGIC)
                act.wait_ge(w_scaled, 2)
                for n, part in enumerate(w2q):
                    nc.scalar.activation(part, w2_in[:, n * 4:(n + 1) * 4, :], ACT.Copy, bias=-MAGIC)

            @blk.sync
            def _(sp):
                with sp.Fori(0, NB) as b:
                    n = sp.value_load(itC[0:1, bass.ds(b, 1)], min_val=0, max_val=NL - 1)
                    one = bass.ds(n, 1)
                    at = bass.ds(b, 1)
                    sp.dma_start(aW1[:, at], cW1[one, :, :].rearrange("l (k p) a -> p l k a", p=P)).then_inc(adapt_in, 16)
                    sp.dma_start(aW2[0:A, at, :], cW2[one, :, :].rearrange("l a d -> a l d")).then_inc(adapt_in, 16)
                    sp.dma_start(aW2[A:A + 1, at, :], cb2[one, :].unsqueeze(0)).then_inc(adapt_in, 16)
                    sp.dma_start(aB1[:, at], cb1T[one, :, :].rearrange("l a o -> (l a) o")).then_inc(adapt_in, 16)
                    sp.dma_start(aGam[:, at, :], cgammaT[one, :, :].rearrange("l p k -> p l k")).then_inc(adapt_in, 16)
                    sp.dma_start(aBet[:, at, :], cbetaT[one, :, :].rearrange("l p k -> p l k")).then_inc(adapt_in, 16)
                for k in range(KD):
                    sp.dma_start(w1_in[:, k, :], w1T.rearrange("(k p) f -> p k f", p=P)[:, k]).then_inc(ffn1_in, 16)
                for c in range(0, FC, FC // 2):
                    sp.dma_start(w2_in[:, c:c + FC // 2], w2T.rearrange("(c p) d -> p c d", p=P)[:, c:c + FC // 2]
                                 ).then_inc(ffn1_in, 16)
                sp.dma_start(b1_sb, b1T).then_inc(ffn1_in, 16)
                sp.dma_start(b2_sb, b2.partition_broadcast(P)).then_inc(ffn1_in, 16)
                for b in range(NB):
                    t = slice(b * TB, (b + 1) * TB)
                    sp.dma_start(X[:, t, :], res_dram.rearrange("(n p) d -> p n d", p=P)[:, t]).then_inc(ffn1_in, 16)
                sp.wait_ge(adapt_in, 6 * 16 * NB)
                sp.wait_ge(ffn1_in, FFN1_LOADS)
                for u in range(UNR):
                    sp.wait_ge(moe_stored[u], NI * 16)
                for b in range(RB):
                    load_rows(sp, b)

            @blk.vector
            def _(dve):
                def split_x(j):
                    dve.wait_ge(xh_done, j + 1)
                    nc.vector.scalar_tensor_tensor(xgT[:, 1], pX[:, 0:D].rearrange("p (k s) -> p k s", k=KD), SN,
                                                   xgT[:, 0], ALU.mult, ALU.subtract).then_inc(xl_done, 1)

                def emit(i, u):
                    dve.wait_ge(dnb_done, i * UNR + u + 1)
                    if not (isinstance(i, int) and i == 0):
                        dve.wait_ge(moe_stored[u], i * 16)
                    nc.vector.tensor_scalar(orow[u], pD[:, 0, 0:D], 1.0 / (SHE * SE), None,
                                            ALU.mult).then_inc(out_ready, 1)

                def block(i, u, first=False, last=False):
                    j = i * UNR + u
                    dve.wait_ge(silu_done, j + 1)
                    dve.wait_ge(gu_done, 2 * j + 2)
                    nc.vector.scalar_tensor_tensor(hm, pL[0][:, :], gate_up_s[:, bass.ds(j, 1)], sg,
                                                   ALU.mult, ALU.mult).then_inc(hm_done, 1)
                    if not last:
                        split_x(j + 1)
                    if not first:
                        emit(i if u else i - 1, (u - 1) % UNR)
                    dve.wait_ge(hth_done, j + 1)
                    nc.vector.tensor_tensor(hT[:, 1], pH[:, :].rearrange("p (k s) -> p k s", k=KE), hT[:, 0],
                                            ALU.subtract).then_inc(htl_done, 1)
                split_x(0)
                for u in range(UNR):
                    block(0, u, first=(u == 0))
                with dve.Fori(1, NI - 2) as i:
                    for u in range(UNR):
                        block(i, u)
                lk = linker(dve, wq_link)
                block(NI - 2, 0)
                dve.wait_ge(ffn1_in, FFN1_LOADS)
                lk(nc.vector.tensor_reduce(wmax[:, 0:1], w1_in.rearrange("p k f -> p (k f)"), AX, ALU.max,
                                           apply_absolute_value=True))
                block(NI - 2, 1)
                nc.vector.tensor_reduce(wmax[:, 1:2], w2_in.rearrange("p c d -> p (c d)"), AX, ALU.max,
                                        apply_absolute_value=True).then_inc(wt_ready, 1)
                block(NI - 2, 2)
                block(NI - 1, 0)
                top_of(dve, lk, pW, 2, wtop, wdiag, wt_done, wd_ready)
                block(NI - 1, 1)
                step_of(dve, lk, pW, 2, wall, wstep, winv, wd_done)
                block(NI - 1, 2, last=True)
                emit(NI - 1, UNR - 1)
                for j, w in enumerate((w1_in, w2_in)):
                    nc.vector.tensor_scalar(w, w, winv[:, j:j + 1], MAGIC, ALU.mult, ALU.add).then_inc(w_scaled, 1)

            @blk.tensor
            def _(pe):
                def transpose_x(i, u):
                    pe.wait_ge(xg_in[u], i * 16 + 16)
                    if not (isinstance(i, int) and i * UNR + u == 0):
                        pe.wait_ge(xl_done, i * UNR + u)
                    for k in range(KD):
                        last = nc.tensor.transpose(pX[:, k * P:(k + 1) * P], xg[u][:, k * P:(k + 1) * P], ident[:, :])
                    last.then_inc(xt_done, 1)

                def gate_up(i, u):
                    j = i * UNR + u
                    e = pe.snap(expert[u], min_val=0, max_val=E - 1)
                    pe.wait_ge(xl_done, j + 1)
                    if not (isinstance(j, int) and j == 0):
                        pe.wait_ge(hm_done, j)
                    for h, bank in enumerate((pG[0], pL[0])):
                        for k in range(KD):
                            wh = GUh[:, k, bass.ds(e, 1), h * FE:(h + 1) * FE].rearrange("p e f -> p (e f)")
                            wl = GUl[:, k, bass.ds(e, 1), h * FE:(h + 1) * FE].rearrange("p e f -> p (e f)")
                            nc.tensor.matmul(bank[:, :], xgT[:, 0, k, :], wh, start=(k == 0), stop=False)
                            nc.tensor.matmul(bank[:, :], xgT[:, 1, k, :], wh, start=False, stop=False)
                            last = nc.tensor.matmul(bank[:, :], xgT[:, 0, k, :], wl, start=False, stop=(k == KD - 1))
                        last.then_inc(gu_done, 1)

                def transpose_h(j):
                    pe.wait_ge(hm_done, j + 1)
                    if not (isinstance(j, int) and j == 0):
                        pe.wait_ge(htl_done, j)
                    for k in range(KE):
                        last = nc.tensor.transpose(pH[:, k * P:(k + 1) * P], hm[:, k * P:(k + 1) * P], ident[:, :])
                    last.then_inc(ht_done, 1)

                def down(i, u):
                    j = i * UNR + u
                    e = pe.snap(expert[u % UNR], min_val=0, max_val=E - 1)
                    pe.wait_ge(htl_done, j + 1)
                    if not (isinstance(j, int) and j == 0):
                        pe.wait_ge(out_ready, j)
                    for k in range(KE):
                        wh = DNh[:, k, bass.ds(e, 1), :].rearrange("p e d -> p (e d)")
                        wl = DNl[:, k, bass.ds(e, 1), :].rearrange("p e d -> p (e d)")
                        o = pD[:, 0, 0:D]
                        nc.tensor.matmul(o, hT[:, 0, k, :], wh, start=(k == 0), stop=False)
                        nc.tensor.matmul(o, hT[:, 1, k, :], wh, start=False, stop=False)
                        last = nc.tensor.matmul(o, hT[:, 0, k, :], wl, start=False, stop=(k == KE - 1))
                    last.then_inc(dnb_done, 1)

                def block(i, u, first=False, last=False):
                    j = i * UNR + u
                    gate_up(i, u)
                    if not last:
                        pe.reg_load(expert[(u + 1) % UNR], be_i[0:1, bass.ds(j + 1, 1)])
                        transpose_x(i + 1 if u == UNR - 1 else i, (u + 1) % UNR)
                    if not first:
                        down(i, u - 1)
                    transpose_h(j)
                expert = [pe.alloc_register(f"expert{u}") for u in range(UNR)]
                pe.reg_load(expert[0], be_i[0:1, 0:1])
                keep_warm(pe, pM, 14)
                transpose_x(0, 0)
                for u in range(UNR):
                    block(0, u, first=(u == 0))
                with pe.Fori(1, NI - 1) as i:
                    for u in range(UNR):
                        block(i, u)
                for u in range(UNR):
                    block(NI - 1, u, last=(u == UNR - 1))
                    if u == 0:
                        turn_max(pe, wmax, pW, 2, wt_ready, wt_done)
                    if u == 1:
                        spread_max(pe, wdiag, pW, 2, wd_ready, wd_done)
                down(NI - 1, UNR - 1)
                keep_warm(pe, pR, 22)
        big = moe_area[:, :].bitcast(F32)
        h_all = big[:, 0:FC * TOK].rearrange("p (f n) -> p f n", f=FC)
        o = FC * TOK
        X3 = big[:, o:o + NT * D].rearrange("p (n d) -> p n d", n=NT)
        o += NT * D
        x3q = big[:, o:o + KD * TOK // 2].bitcast(BF16).rearrange("p (k n) -> p k n", k=KD)
        x3T = xt_area[:, :].bitcast(F32).rearrange("p (k n) -> p k n", k=KD)
        hq = ffn_area[:, 0:FC * TOK].bitcast(BF16).rearrange("p (f n) -> p f n", f=FC)
        b2s = bet[:, :]

        rows_used, t2_done, t2c_done, m1_done, relu_done, m2_done, pre_done, pre_link = (sem(n) for n in (
            "rows_used", "t2_done", "t2c_done", "m1_done", "relu_done", "m2_done", "pre_done", "pre_link"))
        sum_done, bn2_done, rstd2_done, nmr_done, nrm2_done, t3_done, t3c_done, max_done, cp_link = (sem(n) for n in (
            "sum_done", "bn2_done", "rstd2_done", "nmr_done", "nrm2_done", "t3_done", "t3c_done", "max_done", "cp_link"))
        nrm2_dve, first_rank = sem("nrm2_dve"), sem("first_rank")

        pT2, pA, pT3 = pR, pG[1], [pG[0], pL[0]]

        with nc.Block() as blk:
            @blk.sync
            def _(sp):
                for b in range(RB, NB):
                    sp.wait_ge(rows_used, b - RB + 1)
                    load_rows(sp, b)

            @blk.gpsimd
            def _(pool):
                lk = linker(pool, cp_link)
                def add_rows(b):
                    q = b % RB
                    pool.wait_ge(rows_in[q], 32 * (b // RB + 1))
                    nc.gpsimd.tensor_tensor(rr[:, q, 0], rr[:, q, 0], rr[:, q, 1], ALU.add).then_inc(sum_done, 1)
                for b in range(1, 3):
                    add_rows(b)
                for b in range(NB):
                    if b + 3 < NB:
                        add_rows(b + 3)
                    t = slice(b * TB, (b + 1) * TB)
                    pool.wait_ge(bn2_done, b + 1)
                    lk(nc.gpsimd.tensor_tensor(rstd_all[:, t], mvv[:, t, 1], eps2, ALU.add))
                    nc.gpsimd.tensor_tensor(rstd_all[:, t], rstd_all[:, t], mhalf, ALU.pow).then_inc(rstd2_done, 1)

            @blk.scalar
            def _(act):
                for step in range(-1, NB + 3):
                    b = step
                    if 0 <= b < NB:
                        act.wait_ge(m1_done, b + 1)
                        if b:
                            act.wait_ge(m2_done, b)
                        nc.scalar.activation(aH[0:A, :], pA[0:A, 0:S], ACT.Relu, bias=aB1[:, b:b + 1]).then_inc(relu_done, 1)
                    b = step + 1
                    if b < NB:
                        act.wait_ge(t2_done, b + 1)
                        if b:
                            act.wait_ge(m1_done, b)
                        nc.scalar.activation(x2T, pT2.rearrange("p (k s) -> p k s", k=KD), ACT.Copy).then_inc(t2c_done, 1)
                    b = step - 2
                    if 0 <= b < NB - 2:
                        act.wait_ge(nmr_done, b + 1)
                        for n in range(b * TB, (b + 1) * TB):
                            last = nc.scalar.activation(X3[:, n, :], X3[:, n, :], ACT.Identity,
                                                        bias=nmr_all[:, n:n + 1], scale=rstd_all[:, n:n + 1])
                        last.then_inc(nrm2_done, 1)
                    b = step - 3
                    if 0 <= b < NB:
                        act.wait_ge(t3_done, b + 1)
                        for k in range(KD):
                            last = nc.scalar.activation(x3T[:, k, b * S:(b + 1) * S], pT3[b % 2][:, k * S:(k + 1) * S],
                                                        ACT.Identity, bias=aBet[:, b, k:k + 1], scale=aGam[:, b, k:k + 1])
                        last.then_inc(t3c_done, 1)

            @blk.vector
            def _(dve):
                v = nc.vector
                st = stats[:, :].rearrange("p (n s) -> p n s", s=6)
                for step in range(-1, NB + 4):
                    b = step + 1
                    t = slice(b * TB, (b + 1) * TB)
                    if b == 0:
                        dve.wait_ge(rows_in[0], 32)
                        v.tensor_tensor(X[:, t, :], X[:, t, :], rr[:, 0, 0], ALU.add).then_inc(first_rank, 1)
                        dve.wait_ge(first_rank, 1)
                        v.tensor_tensor(X[:, t, :], X[:, t, :], rr[:, 0, 1], ALU.add).then_inc(rows_used, 1)
                    elif b < NB:
                        dve.wait_ge(sum_done, b)
                        v.tensor_tensor(X[:, t, :], X[:, t, :], rr[:, b % RB, 0], ALU.add).then_inc(rows_used, 1)
                    b = step - 1
                    if 0 <= b < NB:
                        t = slice(b * TB, (b + 1) * TB)
                        dve.wait_ge(m2_done, b + 1)
                        dve.wait_ge(rows_used, b + 1)
                        v.tensor_tensor(X3[:, t, :], pD[:, :, 0:D], X[:, t, :], ALU.add).then_inc(pre_done, 1)
                        dve.wait_ge(pre_done, b + 1)
                        for n in range(b * TB, (b + 1) * TB):
                            v.bn_stats(st[:, n, :], X3[:, n, :]).then_inc(pre_link, 1)
                        for n in range(TB):
                            dve.wait_ge(pre_link, b * TB + n + 1)
                            last = v.bn_aggr(mvv[:, b * TB + n, :], st[:, b * TB + n, :])
                        last.then_inc(bn2_done, 1)
                    b = step - 2
                    if 0 <= b < NB:
                        t = slice(b * TB, (b + 1) * TB)
                        dve.wait_ge(rstd2_done, b + 1)
                        dve.wait_ge(bn2_done, b + 1)
                        if b < NB - 2:
                            v.scalar_tensor_tensor(nmr_all[:, t], mvv[:, t, 0], -1.0, rstd_all[:, t],
                                                   ALU.mult, ALU.mult).then_inc(nmr_done, 1)
                        else:
                            for n in range(b * TB, (b + 1) * TB):
                                last = v.tensor_scalar(X3[:, n, :], X3[:, n, :], mvv[:, n, 0:1], rstd_all[:, n:n + 1],
                                                       ALU.subtract, ALU.mult)
                            last.then_inc(nrm2_dve, 1)
                    b = step - 4
                    if 0 <= b < NB:
                        dve.wait_ge(t3c_done, b + 1)
                        v.tensor_reduce(amax[:, b:b + 1], x3T[:, :, b * S:(b + 1) * S], mybir.AxisListType.XY, ALU.max,
                                        apply_absolute_value=True).then_inc(max_done, 1)

            @blk.tensor
            def _(pe):
                pe.wait_ge(one_row, 1)
                keep_warm(pe, pM, 12)
                for step in range(-1, NB + 3):
                    b = step
                    if 0 <= b < NB:
                        pe.wait_ge(t2c_done, b + 1)
                        if b:
                            pe.wait_ge(relu_done, b)
                        for k in range(KD):
                            last = nc.tensor.matmul(pA[0:A, 0:S], aW1[:, b, k, :], x2T[:, k, :],
                                                    start=(k == 0), stop=(k == KD - 1))
                        last.then_inc(m1_done, 1)
                    b = step + 1
                    if b < NB:
                        pe.wait_ge(rows_used, b + 1)
                        if b:
                            pe.wait_ge(t2c_done, b)
                        for t in range(TB):
                            for k in range(KD):
                                last = nc.tensor.transpose(pT2[:, k * S + t * P:k * S + (t + 1) * P],
                                                           X[:, b * TB + t, k * P:(k + 1) * P], ident[:, :])
                        last.then_inc(t2_done, 1)
                    b = step - 3
                    if 0 <= b < NB:
                        if b < NB - 2:
                            pe.wait_ge(nrm2_done, b + 1)
                        else:
                            pe.wait_ge(nrm2_dve, b - NB + 3)
                        if b >= 2:
                            pe.wait_ge(t3c_done, b - 1)
                        for t in range(TB):
                            for k in range(KD):
                                last = nc.tensor.transpose(pT3[b % 2][:, k * S + t * P:k * S + (t + 1) * P],
                                                           X3[:, b * TB + t, k * P:(k + 1) * P], ident[:, :])
                        last.then_inc(t3_done, 1)
                    b = step
                    if 0 <= b < NB:
                        pe.wait_ge(relu_done, b + 1)
                        if b:
                            pe.wait_ge(pre_done, b)
                        for t in range(TB):
                            last = nc.tensor.matmul(pD[:, t, 0:D], aH[:, t * P:(t + 1) * P], aW2[:, b, :],
                                                    start=True, stop=True)
                        last.then_inc(m2_done, 1)

        NCH = 4
        CH = TOK // NCH
        d_link, xt_rdy, xt_dn, xd_rdy, xd_dn = (sem(n) for n in ("d_link", "xt_rdy", "xt_dn", "xd_rdy", "xd_dn"))
        s1_done, r1_done, q1_done, mm1_done, g_done = (sem(n) for n in (
            "s1_done", "r1_done", "q1_done", "mm1_done", "g_done"))
        ht_rdy, ht_dn, hd_rdy, hd_dn, b2_done, z_done, rh_done, qh_act, qh_dve, acc_done, o_done, out_stored = (
            sem(n) for n in ("ht_rdy", "ht_dn", "hd_rdy", "hd_dn", "b2_done", "z_done", "rh_done",
                             "qh_act", "qh_dve", "acc_done", "o_done", "out_stored"))
        act_chunks = [1, 3, 5, 6]
        acc = [halves[t // 8][:, (t % 8) // 2, (t % 2) * D:(t % 2 + 1) * D] for t in range(NT)]

        with nc.Block() as blk:
            @blk.sync
            def _(sp):
                o_rows = out.rearrange("b (t p) d -> p b t d", p=P)
                for b in range(NB):
                    sp.wait_ge(o_done, b + 1)
                    sp.dma_start(o_rows[:, b], X3[:, b * TB:(b + 1) * TB, :]).then_inc(out_stored, 16)
                sp.wait_ge(out_stored, 16 * NB)

            @blk.gpsimd
            def _(pool):
                pool.wait_ge(b2_done, 1)
                for b in range(NB):
                    xb = X[:, b * TB:(b + 1) * TB, :]
                    nc.gpsimd.tensor_tensor(xb, xb, b2s.unsqueeze(1).to_broadcast([P, TB, D]), ALU.add).then_inc(z_done, 1)

            @blk.scalar
            def _(act):
                nc.scalar.activation(tiny[:, 52:53], iota_p[:, :], ACT.Gelu)
                for c in range(NCH):
                    act.wait_ge(r1_done, c + 1)
                    nc.scalar.activation(x3q[:, :, c * CH:(c + 1) * CH], x3T[:, :, c * CH:(c + 1) * CH], ACT.Copy,
                                         bias=-MAGIC).then_inc(q1_done, 1)
                act.wait_ge(s1_done, 1)
                for f in range(FC):
                    for c in range(2):
                        act.wait_ge(mm1_done, 2 * f + c + 1)
                        if f not in (0, FC - 1):
                            if c == 0:
                                continue
                            nc.scalar.activation(h_all[:, f, :], halves[f % 2][:, :, :].rearrange("p b n -> p (b n)"),
                                                 ACT.Gelu, bias=b1s[:, f:f + 1], scale=s1).then_inc(g_done, 2)
                        else:
                            nc.scalar.activation(h_all[:, f, c * TOK // 2:(c + 1) * TOK // 2],
                                                 halves[f % 2][:, 2 * c:2 * c + 2, :].rearrange("p b n -> p (b n)"),
                                                 ACT.Gelu, bias=b1s[:, f:f + 1], scale=s1).then_inc(g_done, 1)
                for n, f in enumerate(act_chunks):
                    act.wait_ge(rh_done, f + 1)
                    nc.scalar.activation(hq[:, f, :], h_all[:, f, :], ACT.Copy, bias=-MAGIC).then_inc(qh_act, 1)

            @blk.vector
            def _(dve):
                v = nc.vector
                lk = linker(dve, d_link)
                v.tensor_reduce(xmax, amax[:, 0:NB], AX, ALU.max).then_inc(xt_rdy, 1)
                top_of(dve, lk, pR, 1, xtop[0:1], xdiag[0:1], xt_dn, xd_rdy)
                step_of(dve, lk, pR, 1, xall, xstep, xinv, xd_dn)
                for c in range(NCH):
                    xc = x3T[:, :, c * CH:(c + 1) * CH]
                    v.tensor_scalar(xc, xc, xinv, MAGIC, ALU.mult, ALU.add).then_inc(r1_done, 1)
                lk(v.tensor_tensor(s1, xstep, wstep[:, 0:1], ALU.mult))
                v.tensor_scalar(b1s, b1_sb, s1, None, ALU.mult).then_inc(s1_done, 1)
                parts = [(f, c, TOK // 2) for f in (0, FC - 1) for c in range(2)]
                parts[2:2] = [(f, 0, TOK) for f in range(1, FC - 1)]
                for n, (f, c, size) in enumerate(parts):
                    dve.wait_ge(g_done, 2 * f + c + 1 + (size == TOK))
                    last = v.tensor_reduce(amax[:, NB + n:NB + n + 1], h_all[:, f, c * size:(c + 1) * size], AX,
                                           ALU.max, apply_absolute_value=True)
                lk(last)
                v.tensor_reduce(hmax, amax[:, NB:NB + len(parts)], AX, ALU.max).then_inc(ht_rdy, 1)
                top_of(dve, lk, pR, 1, htop[0:1], hdiag[0:1], ht_dn, hd_rdy)
                step_of(dve, lk, pR, 1, hall, hstep, hinv, hd_dn)

                def to_grid(f):
                    v.tensor_scalar(h_all[:, f, :], h_all[:, f, :], hinv, MAGIC, ALU.mult, ALU.add).then_inc(rh_done, 1)
                for f in range(FC):
                    to_grid(f)
                    if f not in act_chunks:
                        dve.wait_ge(rh_done, f + 1)
                        v.tensor_scalar(hq[:, f, :], h_all[:, f, :], MAGIC, None, ALU.subtract).then_inc(qh_dve, 1)
                    if f == 1:
                        lk(v.tensor_tensor(s2, hstep, wstep[:, 1:2], ALU.mult))
                        v.tensor_scalar(b2s, b2_sb, s2, None, ALU.mult).then_inc(b2_done, 1)
                for b in range(NB):
                    dve.wait_ge(acc_done, b + 1)
                    dve.wait_ge(z_done, b + 1)
                    bank = halves[b // 4][:, b % 4, :].rearrange("p (t d) -> p t d", t=TB)
                    v.scalar_tensor_tensor(X3[:, b * TB:(b + 1) * TB, :], bank, s2, X[:, b * TB:(b + 1) * TB, :],
                                           ALU.mult, ALU.add).then_inc(o_done, 1)

            @blk.tensor
            def _(pe):
                turn_max(pe, xmax, pR, 1, xt_rdy, xt_dn)
                spread_max(pe, xdiag[0:1], pR, 1, xd_rdy, xd_dn)
                keep_warm(pe, pL[1], 12)
                for f in range(FC):
                    if f >= 2:
                        pe.wait_ge(g_done, 2 * (f - 1))
                    for c in range(NCH):
                        if f == 0:
                            pe.wait_ge(q1_done, c + 1)
                        if f == 1 and c == 0:
                            pe.wait_ge(d_link, 3)
                        for k in range(KD):
                            last = nc.tensor.matmul(halves[f % 2][:, c, :], w1q[:, k, f * P:(f + 1) * P],
                                                    x3q[:, k, c * CH:(c + 1) * CH], start=(k == 0), stop=(k == KD - 1))
                        if c % 2:
                            last.then_inc(mm1_done, 1)
                pe.wait_ge(g_done, 2 * FC)
                keep_warm(pe, pL[1], 8)
                turn_max(pe, hmax, pR, 1, ht_rdy, ht_dn)
                spread_max(pe, hdiag[0:1], pR, 1, hd_rdy, hd_dn)
                keep_warm(pe, pL[1], 10)
                def ready(f):
                    if f in act_chunks:
                        pe.wait_ge(qh_act, act_chunks.index(f) + 1)
                    else:
                        pe.wait_ge(qh_dve, f + 1 - sum(a < f for a in act_chunks))

                def second(t, f):
                    return nc.tensor.matmul(acc[t], hq[:, f, t * P:(t + 1) * P], w2q[f // 4][:, f % 4, :],
                                            start=(f == 0 and t % 2 == 0), stop=(f == FC - 1 and t % 2 == 1),
                                            skip_group_check=True)
                for f in range(FC - 2):
                    ready(f)
                    for t in range(NT):
                        second(t, f)
                for f in range(FC - 2, FC):
                    ready(f)
                for b in range(NB):
                    for f in range(FC - 2, FC):
                        for t in range(b * TB, (b + 1) * TB):
                            last = second(t, f)
                    last.then_inc(acc_done, 1)


def kernel(**inputs):
    import concourse.bacc as bacc
    from concourse.bass_utils import run_bass_kernel_spmd

    def host(name):
        return np.asarray(inputs[name])

    def swap(name):
        return np.ascontiguousarray(np.swapaxes(host(name), -1, -2))

    def columns(name):
        return np.ascontiguousarray(host(name).reshape(host(name).shape[0], -1, P).transpose(0, 2, 1))

    arrays = {
        "x": host("x"), "xT": swap("x"), "itokA": host("itok_B_0_2"), "itokC": host("itok_B_0_8"),
        "Wi0": host("L0_cond_Wi0"), "Wi1": host("L0_cond_Wi1"), "Wo": host("L0_cond_Wo"),
        "sWi0": host("L0_cond_sWi0"), "sWi1": host("L0_cond_sWi1"), "sWo": host("L0_cond_sWo"),
        "g0": host("L0_cond_g0"), "g1T": swap("L0_cond_g1"),
        "gamma0": host("L0_ffn_ln_gamma"), "beta0": host("L0_ffn_ln_beta"), "routerT": swap("L0_ffn_router_w"),
        "guT": swap("L0_ffn_gate_up_w"), "dnT": swap("L0_ffn_down_w"),
        "cW1": host("L1_cond_W1"), "cb1T": host("L1_cond_b1")[:, :, None],
        "cW2": host("L1_cond_W2"), "cb2": host("L1_cond_b2"),
        "cgammaT": columns("L1_cond_gamma"), "cbetaT": columns("L1_cond_beta"),
        "w1T": swap("L1_ffn_w1"), "b1T": np.ascontiguousarray(host("L1_ffn_b1").reshape(-1, P).T),
        "w2T": swap("L1_ffn_w2"), "b2": host("L1_ffn_b2"),
    }
    arrays = {"in_" + k: np.ascontiguousarray(v) for k, v in arrays.items()}
    nc = bacc.Bacc("TRN2", target_bir_lowering=False, num_devices=1)
    args = [nc.dram_tensor(k, v.shape, mybir.dt.from_np(v.dtype), kind="ExternalInput").ap()
            for k, v in arrays.items()]
    out = nc.dram_tensor("out_0", host("x").shape, F32, kind="ExternalOutput").ap()
    build(nc, *args, out)
    return run_bass_kernel_spmd(nc, [arrays], core_ids=[0]).results[0]["out_0"]
```
